# Optimizing a Trainium2 kernel written in Bass

```python
import numpy as np
import jax
import jax.numpy as jnp

def _softmax(x, axis=-1):
    return jax.nn.softmax(x, axis=axis)

def _gelu(x):
    return jax.nn.gelu(x, approximate=True)

def _silu(x):
    return jax.nn.silu(x)

def _sigmoid(x):
    return jax.nn.sigmoid(x)

def _layernorm(x, axis=-1, eps=1e-05):
    m = jnp.mean(x, axis=axis, keepdims=True)
    v = jnp.var(x, axis=axis, keepdims=True)
    return (x - m) / jnp.sqrt(v + eps)

def _scatter_add(tgt, idx, src, axis=0):
    return tgt.at[idx].add(src)

def _segment_sum(src, seg, n):
    return jax.ops.segment_sum(src, seg, n)
kernel_name = 'mk_adj_resnorm_d4_adj_r2_97c3d5'

def setup_inputs(seed: int=0):
    np.random.seed(seed)
    _w = jnp.asarray

    def _rec_inputs():
        import jax
        import jax.numpy as jnp
        _gk = jax.random.key(seed)
        x = 0.5001 + 0.2887 * jax.random.normal(jax.random.fold_in(_gk, 1), (2048, 64), jnp.float32)
        _a = jax.random.bernoulli(jax.random.fold_in(_gk, 2), 0.00390625, (2048, 2048))
        _a = jnp.logical_or(_a, jnp.eye(2048, dtype=bool))
        _af = _a.astype(jnp.float32)
        _af = _af * jax.random.uniform(jax.random.fold_in(_gk, 3), (2048, 2048), jnp.float32, 0.05, 1)
        adj = _af
        return (x, adj)
    x, adj = _rec_inputs()

    def _L0_gnn_setup():
        import jax, jax.numpy as jnp
        import numpy as np
        N = 5000
        DIM = 64
        F_CONST = 1.0
        B_CONST = 0.1
        R_CONST = 0.01
        key = jax.random.key(seed)
        k1, k2 = jax.random.split(key)
        t = jnp.zeros((1,), dtype=jnp.float32)
        x = jax.random.uniform(k1, (N, DIM), dtype=jnp.float32)
        A = jax.random.uniform(k2, (N, N), dtype=jnp.float32)
        return {'t': t, 'x': x, 'A': A}
    _L0_gnn_all = _L0_gnn_setup()
    _L0_gnn_in = {k: v for k, v in _L0_gnn_all.items() if k in ('t',)}
    del _L0_gnn_all

    def _L1_gnn_setup():
        import jax, jax.numpy as jnp
        import numpy as np

        def _laplacian(A):
            d = jnp.sum(A, axis=-1)
            dinv = 1.0 / jnp.sqrt(d)
            return A * dinv[:, None] * dinv[None, :]

        def _poly(A, theta):
            t = jax.nn.sigmoid(theta)
            N = A.shape[-1]
            P = jnp.eye(N, dtype=A.dtype)
            seg = P
            for i in range(theta.shape[0]):
                seg = seg @ A
                P = P + seg * t[i]
            return P
        key = jax.random.key(seed)
        k1, k2, k3, k4 = jax.random.split(key, 4)
        N, DIN, DOUT, K_CHEB = (2048, 64, 64, 2)
        return {'x': jax.random.normal(k1, (N, DIN), dtype=jnp.float32), 'A': jax.random.uniform(k2, (N, N), dtype=jnp.float32), 'theta': jax.random.normal(k3, (K_CHEB,), dtype=jnp.float32), 'W': jax.random.normal(k4, (DOUT, DIN), dtype=jnp.float32) / np.float32(np.sqrt(DIN)), 'b': jnp.zeros((DOUT,), dtype=jnp.float32), 'k': 4}
    _L1_gnn_all = _L1_gnn_setup()
    _L1_gnn_in = {k: v for k, v in _L1_gnn_all.items() if k in ('theta', 'W', 'b')}
    del _L1_gnn_all

    def _L2_gnn_setup():
        import jax, jax.numpy as jnp
        import numpy as np
        MIN_NORM = 1e-15
        EPS = 0.004

        def artanh(x):
            x = jnp.clip(x, -1 + 1e-07, 1 - 1e-07)
            return 0.5 * (jnp.log1p(x) - jnp.log1p(-x))

        def _norm(x):
            return jnp.sqrt(jnp.clip(jnp.sum(x * x, axis=-1, keepdims=True), MIN_NORM, None))

        def proj(x, c):
            norm = _norm(x)
            maxnorm = (1.0 - EPS) / jnp.sqrt(c)
            return jnp.where(norm > maxnorm, x / norm * maxnorm, x)

        def logmap0(p, c):
            sqrt_c = jnp.sqrt(c)
            p_norm = _norm(p)
            return p * artanh(sqrt_c * p_norm) / (sqrt_c * p_norm)

        def lambda_x(x, c):
            x2 = jnp.sum(x * x, axis=-1, keepdims=True)
            return 2.0 / jnp.clip(1.0 - c * x2, MIN_NORM, None)

        def mobius_add(x, y, c):
            x2 = jnp.sum(x * x, axis=-1, keepdims=True)
            y2 = jnp.sum(y * y, axis=-1, keepdims=True)
            xy = jnp.sum(x * y, axis=-1, keepdims=True)
            num = (1 + 2 * c * xy + c * y2) * x + (1 - c * x2) * y
            denom = 1 + 2 * c * xy + c * c * x2 * y2
            return num / jnp.clip(denom, MIN_NORM, None)

        def logmap(p1, p2, c):
            sub = mobius_add(-p1, p2, c)
            sub_norm = _norm(sub)
            lam = lambda_x(p1, c)
            sqrt_c = jnp.sqrt(c)
            return 2.0 / sqrt_c / lam * artanh(sqrt_c * sub_norm) * sub / sub_norm

        def expmap(p, u, c):
            sqrt_c = jnp.sqrt(c)
            u_norm = _norm(u)
            second = jnp.tanh(0.5 * sqrt_c * lambda_x(p, c) * u_norm) * u / (sqrt_c * u_norm)
            return mobius_add(p, second, c)
        key = jax.random.key(seed)
        k1, k2, k3 = jax.random.split(key, 3)
        N, D = (512, 64)
        x = 0.05 * jax.random.normal(k1, (N, D), jnp.float32)
        adj = (jax.random.uniform(k2, (N, N)) < 0.05).astype(jnp.float32)
        r = jnp.ones((1,), jnp.float32)
        w_att = 0.1 * jax.random.normal(k3, (2 * D, 1), jnp.float32)
        b_att = jnp.zeros((1,), jnp.float32)
        return {'x': x, 'adj': adj, 'r': r, 'w_att': w_att, 'b_att': b_att}
    _L2_gnn_all = _L2_gnn_setup()
    _L2_gnn_in = {k: v for k, v in _L2_gnn_all.items() if k in ('r', 'w_att', 'b_att')}
    del _L2_gnn_all

    def _L3_gnn_setup():
        import jax, jax.numpy as jnp
        import numpy as np
        N, D, H = (8192, 64, 128)
        GAIN = 0.2
        key = jax.random.key(seed)
        ks = jax.random.split(key, 6)
        X = jax.random.normal(ks[0], (N, D), dtype=jnp.float32)
        t = jax.random.uniform(ks[1], (1,), dtype=jnp.float32)
        Wt = jax.random.uniform(ks[2], (N, N), dtype=jnp.float32)
        B = GAIN * jnp.eye(D, dtype=jnp.float32) + 0.01 * jax.random.normal(ks[3], (D, D), dtype=jnp.float32)
        W1 = jax.random.normal(ks[4], (D + 1, H), dtype=jnp.float32) * (1.0 / np.sqrt(D + 1))
        b1 = jnp.zeros((H,), dtype=jnp.float32)
        W2 = jax.random.normal(ks[5], (H, D), dtype=jnp.float32) * (1.0 / np.sqrt(H))
        b2 = jnp.zeros((D,), dtype=jnp.float32)
        return {'X': X, 't': t, 'Wt': Wt, 'B': B, 'W1': W1, 'b1': b1, 'W2': W2, 'b2': b2}
    _L3_gnn_all = _L3_gnn_setup()
    _L3_gnn_in = {k: v for k, v in _L3_gnn_all.items() if k in ('t', 'B', 'W1', 'b1', 'W2', 'b2')}
    del _L3_gnn_all
    return {'x': x, 'adj': adj, 'L0_gnn_t': _L0_gnn_in['t'], 'L1_gnn_theta': _L1_gnn_in['theta'], 'L1_gnn_W': _L1_gnn_in['W'], 'L1_gnn_b': _L1_gnn_in['b'], 'L2_gnn_r': _L2_gnn_in['r'], 'L2_gnn_w_att': _L2_gnn_in['w_att'], 'L2_gnn_b_att': _L2_gnn_in['b_att'], 'L3_gnn_t': _L3_gnn_in['t'], 'L3_gnn_B': _L3_gnn_in['B'], 'L3_gnn_W1': _L3_gnn_in['W1'], 'L3_gnn_b1': _L3_gnn_in['b1'], 'L3_gnn_W2': _L3_gnn_in['W2'], 'L3_gnn_b2': _L3_gnn_in['b2']}

def reference(x, adj, L0_gnn_t, L1_gnn_theta, L1_gnn_W, L1_gnn_b, L2_gnn_r, L2_gnn_w_att, L2_gnn_b_att, L3_gnn_t, L3_gnn_B, L3_gnn_W1, L3_gnn_b1, L3_gnn_W2, L3_gnn_b2):
    import jax
    import jax.numpy as jnp

    def _L0_gnn_ref(t, x, A):
        import jax, jax.numpy as jnp
        import numpy as np
        N = 5000
        DIM = 64
        F_CONST = 1.0
        B_CONST = 0.1
        R_CONST = 0.01
        Ax = A @ x
        outer = R_CONST * jnp.sum(x * Ax, axis=1, keepdims=True)
        return F_CONST - B_CONST * x - outer

    def _L1_gnn_ref(x, A, theta, W, b, k):
        import jax, jax.numpy as jnp
        import numpy as np

        def _laplacian(A):
            d = jnp.sum(A, axis=-1)
            dinv = 1.0 / jnp.sqrt(d)
            return A * dinv[:, None] * dinv[None, :]

        def _poly(A, theta):
            t = jax.nn.sigmoid(theta)
            N = A.shape[-1]
            P = jnp.eye(N, dtype=A.dtype)
            seg = P
            for i in range(theta.shape[0]):
                seg = seg @ A
                P = P + seg * t[i]
            return P
        S = _laplacian(A)
        S = _poly(S, theta)
        S = _laplacian(S)
        rank = jnp.argsort(jnp.argsort(-S, axis=-1), axis=-1)
        mask = jnp.where(rank < k, jnp.float32(1.0), jnp.float32(0.0))
        S = S * mask
        x = S @ x
        return x @ W.T + b

    def _L2_gnn_ref(x, adj, r, w_att, b_att):
        import jax, jax.numpy as jnp
        import numpy as np
        MIN_NORM = 1e-15
        EPS = 0.004

        def artanh(x):
            x = jnp.clip(x, -1 + 1e-07, 1 - 1e-07)
            return 0.5 * (jnp.log1p(x) - jnp.log1p(-x))

        def _norm(x):
            return jnp.sqrt(jnp.clip(jnp.sum(x * x, axis=-1, keepdims=True), MIN_NORM, None))

        def proj(x, c):
            norm = _norm(x)
            maxnorm = (1.0 - EPS) / jnp.sqrt(c)
            return jnp.where(norm > maxnorm, x / norm * maxnorm, x)

        def logmap0(p, c):
            sqrt_c = jnp.sqrt(c)
            p_norm = _norm(p)
            return p * artanh(sqrt_c * p_norm) / (sqrt_c * p_norm)

        def lambda_x(x, c):
            x2 = jnp.sum(x * x, axis=-1, keepdims=True)
            return 2.0 / jnp.clip(1.0 - c * x2, MIN_NORM, None)

        def mobius_add(x, y, c):
            x2 = jnp.sum(x * x, axis=-1, keepdims=True)
            y2 = jnp.sum(y * y, axis=-1, keepdims=True)
            xy = jnp.sum(x * y, axis=-1, keepdims=True)
            num = (1 + 2 * c * xy + c * y2) * x + (1 - c * x2) * y
            denom = 1 + 2 * c * xy + c * c * x2 * y2
            return num / jnp.clip(denom, MIN_NORM, None)

        def logmap(p1, p2, c):
            sub = mobius_add(-p1, p2, c)
            sub_norm = _norm(sub)
            lam = lambda_x(p1, c)
            sqrt_c = jnp.sqrt(c)
            return 2.0 / sqrt_c / lam * artanh(sqrt_c * sub_norm) * sub / sub_norm

        def expmap(p, u, c):
            sqrt_c = jnp.sqrt(c)
            u_norm = _norm(u)
            second = jnp.tanh(0.5 * sqrt_c * lambda_x(p, c) * u_norm) * u / (sqrt_c * u_norm)
            return mobius_add(p, second, c)
        c = 1.0 / r[0] ** 2
        D = x.shape[1]
        x_t = logmap0(x, c)
        left = x_t @ w_att[:D, 0]
        right = x_t @ w_att[D:, 0]
        adj_att = jax.nn.sigmoid(left[:, None] + right[None, :] + b_att[0]) * adj
        x_local = logmap(x[:, None, :], x[None, :, :], c)
        support_t = jnp.einsum('ij,ijd->id', adj_att, x_local)
        return proj(expmap(x, support_t, c), c)

    def _L3_gnn_ref(X, t, Wt, B, W1, b1, W2, b2):
        import jax, jax.numpy as jnp
        import numpy as np
        N, D, H = (8192, 64, 128)
        GAIN = 0.2
        n = X.shape[0]
        tcol = jnp.broadcast_to(t.reshape(1, 1), (n, 1))
        h = jnp.tanh(jnp.concatenate([X, tcol], axis=1) @ W1 + b1)
        u_intra = h @ W2 + b2
        XB = X @ B.T
        u_comm = Wt @ XB - jnp.sum(Wt, axis=1, keepdims=True) * XB
        return u_intra + u_comm
    x = _layernorm(x + _L0_gnn_ref(L0_gnn_t, x, adj), axis=-1)
    x = _layernorm(x + _L1_gnn_ref(x, adj, L1_gnn_theta, L1_gnn_W, L1_gnn_b, 4), axis=-1)
    x = _layernorm(x + _L2_gnn_ref(x, adj, L2_gnn_r, L2_gnn_w_att, L2_gnn_b_att), axis=-1)
    x = _layernorm(x + _L3_gnn_ref(x, L3_gnn_t, adj, L3_gnn_B, L3_gnn_W1, L3_gnn_b1, L3_gnn_W2, L3_gnn_b2), axis=-1)
    return x

_drawn_inputs = setup_inputs


def setup_inputs(seed=0):
    import zlib

    import numpy as np

    out = dict(_drawn_inputs(seed))
    spreads = {'L1_gnn_b': (0.0, 0.1), 'L3_gnn_b1': (0.0, 0.1), 'L3_gnn_b2': (0.0, 0.1)}
    factors = {'L1_gnn_theta': 64.0, 'L2_gnn_w_att': 64.0}
    for name, (base, spread) in spreads.items():
        noise = np.random.default_rng([zlib.crc32(name.encode()), seed]).standard_normal(out[name].shape)
        drawn = base * np.exp(spread * noise) if base else spread * noise
        out[name] = jnp.asarray(drawn.astype(out[name].dtype))
    for name, factor in factors.items():
        out[name] = (out[name] * factor).astype(out[name].dtype)
    return out
```

```python
from contextlib import ExitStack

import concourse.bass as bass
from concourse import mybir

ALU = mybir.AluOpType
ACT = mybir.ActivationFunctionType
AX = mybir.AxisListType
F32 = mybir.dt.float32
F16 = mybir.dt.float16
U32 = mybir.dt.uint32

P = 128
EPS_LN = 1e-5
MIN_NORM = 1e-15
T_MAX = 1.0 - 1e-7
MAX_NORM = 1.0 - 0.004
R_SCALE = 4096.0
TINY = 2.0 ** -60


class Chain:

    def __init__(self, eng, sem):
        self.eng, self.sem, self.n = eng, sem, 0

    def link(self, ins):
        ins.then_inc(self.sem, 1)
        self.n += 1

    def settle(self):
        self.eng.wait_ge(self.sem, self.n)

    def step(self, ins):
        self.link(ins)
        self.settle()


def build(nc, x, adj, theta, w_l1, b_l1, r, w_att, b_att, t_l3, b_l3, w1, b1, w2, b2, out):
    N, D = x.shape
    NB = N // P
    CW = 512
    NC = N // CW
    BPC = CW // P
    H = w1.shape[1]
    TOP = 4
    KA = D + 3

    ctx = ExitStack()
    with ctx:
        def sb(name, shape, dt=F32):
            return ctx.enter_context(nc.sbuf_tensor(name, shape, dt))

        def sem(name):
            return ctx.enter_context(nc.semaphore(name))

        Rhi = sb("Rhi", [P, NB, N], F16)
        Rlo = sb("Rlo", [P, NB, N], F16)
        scratch = sb("scratch", [P, 12288])
        stage = scratch[:, 0:2 * N].rearrange("p (s n) -> p s n", s=2)
        vecB = scratch[:, 2 * N:3 * N]
        RT = scratch[:, 3 * N:5 * N].bitcast(F16).rearrange("p (s h k i) -> p s h k i", s=2, h=2, k=NB)
        xT = scratch[:, 5 * N:6 * N]
        AUG = scratch[:, 0:4 * N].rearrange("p (w n) -> p w n", w=4)
        WTs = scratch[:, 4 * N:5 * N]
        hT = scratch[:, N:2 * N]
        nat_t = scratch[:, 5 * N:5 * N + NB * D].rearrange("p (b d) -> p b d", b=NB)
        nat_u = scratch[:, 0:NB * (D + 1)].rearrange("p (b d) -> p b d", b=NB)
        small = scratch[:, 5 * N + NB * D:6 * N]
        gath = small[:, 0:2 * TOP * D].rearrange("p (s t d) -> p s t d", s=2, t=TOP)
        y_sb = small[:, 512:512 + 2 * D].rearrange("p (s d) -> p s d", s=2)
        yT = small[0:D, 640:640 + 2 * P].rearrange("p (s d) -> p s d", s=2)
        natL = [scratch[:, a:a + NB * KA].rearrange("p (b d) -> p b d", b=NB) for a in (4 * N, 5 * N)]
        x3T = scratch[:, 0:N]
        base = scratch[:, 2 * N:2 * N + NB * D].rearrange("p (b d) -> p b d", b=NB)
        xbs = scratch[:, 2 * N + NB * D:3 * N].bitcast(F16).rearrange("p (b h d) -> p b h d", b=NB, h=2)
        nat_x = sb("nat_x", [P, NB, D])
        nat_y = sb("nat_y", [P, NB, D])
        xaug = sb("xaug", [P, NB, D + 1])
        x2 = xaug[:, :, 0:D]
        work = sb("work", [P, 6, CW])
        w_pair = [work[:, i, :] for i in range(6)]
        identf = sb("identf", [P, P])
        ident = sb("ident", [P, P], F16)
        ones = sb("ones", [P, P])
        sm = sb("sm", [P, 40, NB])
        cols = sb("cols", [P, 24])
        outer4 = sb("outer4", [P, NB, NC])
        vals = sb("vals", [P, 2, 8])
        wts = sb("wts", [P, 2, TOP])
        idx = sb("idx", [P, 2, 8], U32)
        wl_nat = sb("wl_nat", [D, D])
        bl_nat = sb("bl_nat", [D, D])
        wlT = sb("wlT", [D, D])
        blT = sb("blT", [D, D])
        w1_sb = sb("w1_sb", [D, H])
        w2_sb = sb("w2_sb", [H, D])
        watt = sb("watt", [D, 2])
        b1B = sb("b1B", [P, D])
        b2B = sb("b2B", [P, D])
        x1_dram = nc.dram_tensor("x1_scratch", [N, D], F32, kind="Internal").ap()
        bank = [ctx.enter_context(nc.psum_tensor(f"bank{i}", [P, CW], F32)) for i in range(8)]
        bank16 = [b[:, :].bitcast(F16) for b in bank]

        names = ["d", "rd", "rs", "outer", "stat", "stat2", "rsq", "newt", "dinv", "sqd", "u1", "v2", "d2", "dinv2",
                 "cvec", "rowfac", "n2", "X", "om", "pn", "tcl", "lnp", "lnm", "q", "left", "right", "s", "inner",
                 "cf", "kf", "a1", "a2", "a3", "a4", "a5", "a6", "dsc", "omc"]
        V = {n: sm[:, i, :] for i, n in enumerate(names)}
        cn = ["th0", "th1", "t0s", "t1s", "r", "rr", "c", "batt", "tl3", "b1c", "w1t", "hb", "cmin", "lncmin", "sqc",
              "rsqc", "e0", "e1", "c2", "mxn", "nr"]
        C = {n: cols[:, i:i + 1] for i, n in enumerate(cn)}

        tiles = w_pair + [scratch[:, 5 * N + i * CW:5 * N + (i + 1) * CW] for i in range(4)]
        PT = {n: tiles[2 * i:2 * i + 2] for i, n in enumerate(["cd", "dn", "sg", "lz", "tt"])}

        def over_d(v):
            return v.unsqueeze(2).to_broadcast([P, NB, D])

        consts_ready = sem("consts_ready")
        x_loaded = sem("x_loaded")
        small_loaded = sem("small_loaded")
        adj_loaded = [sem(f"adj_loaded{i}") for i in range(2)]
        dve_chain, act_chain, pool_chain = sem("dve_chain"), sem("act_chain"), sem("pool_chain")
        tr_ready, tr_out = sem("tr_ready"), sem("tr_out")
        g_ready, g_used = sem("g_ready"), sem("g_used")
        rowsum_ready, scale_ready, hi_ready, lo_ready = sem("rowsum_ready"), sem("scale_ready"), sem("hi_ready"), sem("lo_ready")
        rsq_asked, rsq_given = sem("rsq_asked"), sem("rsq_given")
        theta_asked, theta_given = sem("theta_asked"), sem("theta_given")
        x1_ready, x1_stored = sem("x1_ready"), sem("x1_stored")
        vec_ready, diag_ready, bc_ready, bc_out = sem("vec_ready"), sem("diag_ready"), sem("bc_ready"), sem("bc_out")
        recon_ready, recon_used = sem("recon_ready"), sem("recon_used")
        rt_ready, rt_out, rt_out_lo = sem("rt_ready"), sem("rt_out"), sem("rt_out_lo")
        s_ready, s_used = sem("s_ready"), sem("s_used")
        rr_ready, top_ready = sem("rr_ready"), sem("top_ready")
        gathered = [sem(f"gathered{i}") for i in range(2)]
        y_ready, yT_ready, yT_out, yw_ready, z_ready = (sem(n) for n in ["y_ready", "yT_ready", "yT_out", "yw_ready", "z_ready"])
        wT_ready, wT_out = sem("wT_ready"), sem("wT_out")
        art_asked, art_given = sem("art_asked"), sem("art_given")
        nat_ready, aug_ready, aug_out = sem("nat_ready"), sem("aug_ready"), sem("aug_out")
        logit_ready = sem("logit_ready")
        dist_ready, dist_used, pl_ready, pl_used = sem("dist_ready"), sem("dist_used"), sem("pl_ready"), sem("pl_used")
        ln_ready, sig_ready, ratio_ready, t_ready = sem("ln_ready"), sem("sig_ready"), sem("ratio_ready"), sem("t_ready")
        weight_ready, clipped_ready, logw_ready = sem("weight_ready"), sem("clipped_ready"), sem("logw_ready")
        artanh_ready, wexp_ready, diff_ready = sem("artanh_ready"), sem("wexp_ready"), sem("diff_ready")
        at_ready, g3_ready, w_used, wsum_out = sem("at_ready"), sem("g3_ready"), sem("w_used"), sem("wsum_out")
        wnat_ready, wnat_out = sem("wnat_ready"), sem("wnat_out")
        tanh_asked, tanh_given = sem("tanh_asked"), sem("tanh_given")
        x3_ready, x3T_ready, x3T_out = sem("x3_ready"), sem("x3T_ready"), sem("x3T_out")
        h_ready, h_out, xb_ready, xb_hi, xb_split = sem("h_ready"), sem("h_out"), sem("xb_ready"), sem("xb_hi"), sem("xb_split")
        u_ready, u_used, ax_ready, ax_used = sem("u_ready"), sem("u_used"), sem("ax_ready"), sem("ax_used")
        r4_hi, r4_lo, r4_hi_out, r4_lo_out = sem("r4_hi"), sem("r4_lo"), sem("r4_hi_out"), sem("r4_lo_out")
        o_ready = sem("o_ready")
        out_stored = sem("out_stored")

        block = ctx.enter_context(nc.Block())
        NSMALL = 15
        NT = NC * NB

        @block.sync
        def _(sp):
            sp.dma_start(nat_x[:, :, :], x.rearrange("(b p) d -> p b d", p=P)).then_inc(x_loaded, 16)
            for b in range(NB):
                if b == 2:
                    sp.dma_start(C["th0"], theta[0:1].partition_broadcast(P)).then_inc(small_loaded, 16)
                    sp.dma_start(C["th1"], theta[1:2].partition_broadcast(P)).then_inc(small_loaded, 16)
                    sp.dma_start(C["r"], r.partition_broadcast(P)).then_inc(small_loaded, 16)
                    sp.dma_start(C["batt"], b_att.partition_broadcast(P)).then_inc(small_loaded, 16)
                    sp.dma_start(C["tl3"], t_l3.partition_broadcast(P)).then_inc(small_loaded, 16)
                    sp.dma_start(C["b1c"], b1.unsqueeze(1)).then_inc(small_loaded, 16)
                    sp.dma_start(C["w1t"], w1[D:D + 1, :].rearrange("a h -> h a")).then_inc(small_loaded, 16)
                    sp.dma_start(wl_nat[:, :], w_l1).then_inc(small_loaded, 16)
                    sp.dma_start(bl_nat[:, :], b_l3).then_inc(small_loaded, 16)
                    sp.dma_start(w1_sb[:, :], w1[0:D, :]).then_inc(small_loaded, 16)
                    sp.dma_start(w2_sb[:, :], w2).then_inc(small_loaded, 16)
                    sp.dma_start(watt[:, 0:1], w_att[0:D, :]).then_inc(small_loaded, 16)
                    sp.dma_start(watt[:, 1:2], w_att[D:2 * D, :]).then_inc(small_loaded, 16)
                    sp.dma_start(b1B[:, :], b_l1.partition_broadcast(P)).then_inc(small_loaded, 16)
                    sp.dma_start(b2B[:, :], b2.partition_broadcast(P)).then_inc(small_loaded, 16)
                if b >= 2:
                    sp.wait_ge(lo_ready, b - 1)
                sp.dma_start(stage[:, b % 2, :], adj[b * P:(b + 1) * P, :]).then_inc(adj_loaded[b % 2], 16)
            sp.wait_ge(x1_ready, 1)
            sp.dma_start(x1_dram.rearrange("(b p) d -> p b d", p=P), nat_y[:, :, :]).then_inc(x1_stored, 16)
            sp.wait_ge(o_ready, 1)
            sp.dma_start(out.rearrange("(b p) d -> p b d", p=P), nat_y[:, :, :]).then_inc(out_stored, 16)
            sp.wait_ge(out_stored, 16)
            sp.wait_ge(x1_stored, 16)

        @block.gpsimd
        def _(pool):
            ch = Chain(pool, pool_chain)
            ch.link(nc.gpsimd.memset(identf[:, :], 0.0))
            ch.link(nc.gpsimd.memset(ident[:, :], 0.0))
            nc.gpsimd.memset(ones[:, :], 1.0).then_inc(consts_ready, 1)
            ch.settle()
            for m in (identf, ident):
                nc.gpsimd.affine_select(out=m[:, :], in_=m[:, :], compare_op=ALU.not_equal, fill=1.0, base=0,
                                        pattern=[[-1, P]], channel_multiplier=1).then_inc(consts_ready, 1)

            def diag(k, vec):
                pool.wait_ge(vec_ready, k + 1)
                for q in range(NC):
                    n = NC * k + q
                    if n >= 2:
                        pool.wait_ge(bc_ready, n - 1)
                    for j in range(BPC):
                        b = BPC * q + j
                        ins = nc.gpsimd.tensor_scalar(w_pair[n % 2][:, j * P:(j + 1) * P], identf[:, :], vec[:, b:b + 1],
                                                      None, ALU.mult)
                        ins.then_inc(diag_ready, 1)

            pool.wait_ge(consts_ready, 3)
            for k, name in enumerate(["dinv", "u1"]):
                diag(k, V[name])
                for b in range(NB):
                    n = NB * k + b
                    if n >= 2:
                        pool.wait_ge(recon_used, n - 1)
                    nc.gpsimd.tensor_tensor(stage[:, n % 2, :], Rhi[:, b, :], Rlo[:, b, :], ALU.add).then_inc(recon_ready, 1)
            diag(2, V["cvec"])

            def start_v(m):
                v = stage[:, m % 2, :]
                if m < 2:
                    pool.wait_ge(recon_used, 2 * NB)
                else:
                    pool.wait_ge(top_ready, m - 1)
                ch.step(nc.gpsimd.tensor_tensor(v, Rhi[:, m, :], Rlo[:, m, :], ALU.add))
                ch.step(nc.gpsimd.tensor_scalar(v, v, C["t0s"], None, ALU.mult))
                d = v[:, m * P:(m + 1) * P]
                nc.gpsimd.tensor_tensor(d, d, identf[:, :], ALU.add).then_inc(rr_ready, 1)

            start_v(0)
            start_v(1)
            pool.wait_ge(x1_stored, 16)
            for m in range(NB):
                pool.wait_ge(top_ready, m + 1)
                if m >= 2:
                    pool.wait_ge(y_ready, m - 1)
                for t in range(TOP):
                    nc.gpsimd.indirect_dma_start(gath[:, m % 2, t, :], None, x1_dram,
                                                 bass.IndirectOffsetOnAxis(idx[:, m % 2, t:t + 1], 0)).then_inc(gathered[m % 2], 16)
                if m + 2 < NB:
                    start_v(m + 2)


            for n in range(NT):
                s = n % 2
                pool.wait_ge(weight_ready, n + 1)
                pool.wait_ge(sig_ready, n + 1)
                nc.gpsimd.tensor_tensor(PT["dn"][s], PT["dn"][s], PT["sg"][s], ALU.subtract).then_inc(logw_ready, 1)
                pool.wait_ge(artanh_ready, n + 1)
                nc.gpsimd.tensor_tensor(PT["cd"][s], PT["cd"][s], PT["lz"][s], ALU.subtract).then_inc(diff_ready, 1)

        @block.scalar
        def _(act):
            ch = Chain(act, act_chain)
            nc.scalar.preload_act_table_set("natural_log_exp_and_others")

            def rsqrt(k, v, e):
                act.wait_ge(rsq_asked, k + 1)
                ch.step(nc.scalar.activation(e, v, ACT.Ln))
                nc.scalar.activation(e, e, ACT.Exp, scale=-0.5).then_inc(rsq_given, 1)

            def spread_out(k):
                for n in range(NC * k, NC * k + NC):
                    act.wait_ge(bc_ready, n + 1)
                    q = n % NC
                    nc.scalar.copy(vecB[:, q * CW:(q + 1) * CW], bank[6 + n % 2][:, :]).then_inc(bc_out, 1)

            def turned_out(m):
                for g in range(4 * m, 4 * m + 4):
                    h, half = (g % 4) // 2, g % 2
                    act.wait_ge(rt_ready, g + 1)
                    nc.scalar.copy(RT[:, m % 2, h, half * 8:half * 8 + 8, :].rearrange("p k i -> p (k i)"),
                                   bank16[4 + g % 2]).then_inc(rt_out, 1)

            for q in range(NC):
                act.wait_ge(tr_ready, q + 1)
                nc.scalar.copy(xT[0:D, q * CW:(q + 1) * CW], bank[q % 2][0:D, :]).then_inc(tr_out, 1)
            for b in range(NB):
                act.wait_ge(adj_loaded[b % 2], 16 * (b // 2 + 1))
                nc.scalar.activation(Rhi[:, b, :], stage[:, b % 2, :], ACT.Copy,
                                     accum_out=V["d"][:, b:b + 1]).then_inc(rowsum_ready, 1)
                act.wait_ge(scale_ready, b + 1)
                nc.scalar.activation(Rhi[:, b, :], stage[:, b % 2, :], ACT.Copy,
                                     scale=V["rs"][:, b:b + 1]).then_inc(hi_ready, 1)
            rsqrt(0, V["d"], V["rsq"])
            spread_out(0)
            act.wait_ge(wT_ready, 1)
            nc.scalar.copy(wlT[:, :], bank[0][0:D, 0:D]).then_inc(wT_out, 1)
            nc.scalar.copy(blT[:, :], bank[0][0:D, D:2 * D]).then_inc(wT_out, 1)
            turned_out(0)
            act.wait_ge(theta_asked, 1)
            nc.scalar.activation(cols[:, 16:18], cols[:, 0:2], ACT.Exp, scale=-1.0).then_inc(theta_given, 1)
            rsqrt(1, V["stat2"], V["rsq"])
            spread_out(1)
            turned_out(1)
            rsqrt(2, V["d2"], V["rsq"])
            spread_out(2)

            def turn_y(m):
                act.wait_ge(yT_ready, m + 1)
                nc.scalar.copy(yT[:, m % 2, :], bank[6][0:D, 0:P]).then_inc(yT_out, 1)

            for m in range(1, NB):
                if m >= 2:
                    turn_y(m - 2)
                if m + 1 < NB:
                    turned_out(m + 1)
            turn_y(NB - 2)
            turn_y(NB - 1)
            rsqrt(3, V["stat2"], V["rsq"])
            rsqrt(4, V["pn"], V["rsq"])
            act.wait_ge(art_asked, 1)
            nc.scalar.activation(V["lnp"], V["tcl"], ACT.Ln, bias=1.0)
            nc.scalar.activation(V["lnm"], V["tcl"], ACT.Ln, bias=1.0, scale=-1.0)
            nc.scalar.activation(C["lncmin"], C["cmin"], ACT.Ln).then_inc(art_given, 1)
            for n in range(4 * NC):
                kind, q = n // NC, n % NC
                act.wait_ge(aug_ready, n + 1)
                nc.scalar.copy(AUG[0:KA, kind, q * CW:(q + 1) * CW], bank[n % 2][0:KA, :]).then_inc(aug_out, 1)

            def sigmoid_part(n):
                s = n % 2
                act.wait_ge(pl_ready, n + 1)
                if n >= 2:
                    act.wait_ge(logw_ready, n - 1)
                sg = PT["sg"][s]
                ch.step(nc.scalar.activation(sg, bank[4 + s][:, :], ACT.Abs))
                ch.step(nc.scalar.activation(sg, sg, ACT.Exp, scale=-1.0))
                nc.scalar.activation(sg, sg, ACT.Ln, bias=1.0).then_inc(sig_ready, 1)

            def logs(n):
                s = n % 2
                act.wait_ge(dist_used, n + 1)
                nc.scalar.activation(PT["cd"][s], PT["cd"][s], ACT.Ln)
                nc.scalar.activation(PT["dn"][s], PT["dn"][s], ACT.Ln).then_inc(ln_ready, 1)

            def sum_out(c):
                act.wait_ge(w_used, NB * (c + 1))
                nc.scalar.copy(WTs[0:D + 1, c * CW:(c + 1) * CW], bank[7][0:D + 1, :]).then_inc(wsum_out, 1)

            sigmoid_part(0)
            logs(0)
            for n in range(NT):
                s = n % 2
                act.wait_ge(ratio_ready, n + 1)
                nc.scalar.activation(PT["tt"][s], PT["lz"][s], ACT.Exp, scale=0.5).then_inc(t_ready, 1)
                if n + 1 < NT:
                    sigmoid_part(n + 1)
                act.wait_ge(clipped_ready, n + 1)
                nc.scalar.activation(PT["cd"][s], PT["tt"][s], ACT.Ln, bias=1.0)
                nc.scalar.activation(PT["lz"][s], PT["tt"][s], ACT.Ln, bias=1.0, scale=-1.0).then_inc(artanh_ready, 1)
                act.wait_ge(logw_ready, n + 1)
                nc.scalar.activation(PT["dn"][s], PT["dn"][s], ACT.Exp).then_inc(wexp_ready, 1)
                if n + 1 < NT:
                    logs(n + 1)
                if n and n % NB == 0:
                    sum_out(n // NB - 1)
            sum_out(NC - 1)
            rsqrt(5, V["a1"], V["rsq"])
            act.wait_ge(tanh_asked, 1)
            nc.scalar.activation(V["a3"], V["a2"], ACT.Tanh).then_inc(tanh_given, 1)
            nc.scalar.preload_act_table_set("natural_log_exp_and_others")
            rsqrt(6, V["a1"], V["rsq"])
            rsqrt(7, V["stat2"], V["rsq"])

            for q in range(NC):
                act.wait_ge(x3T_ready, q + 1)
                nc.scalar.copy(x3T[0:D, q * CW:(q + 1) * CW], bank[q % 2][0:D, :]).then_inc(x3T_out, 1)
            for q in range(NC):
                act.wait_ge(h_ready, q + 1)
                nc.scalar.activation(hT[:, q * CW:(q + 1) * CW], bank[2 + q % 2][:, :], ACT.Tanh,
                                     bias=C["hb"]).then_inc(h_out, 1)
            for q in range(2):
                act.wait_ge(xb_ready, q + 1)
                nc.scalar.copy(xbs[:, 8 * q:8 * q + 8, 0, :], bank[q][:, :].rearrange("p (b d) -> p b d", b=8)).then_inc(xb_hi, 1)
            nc.scalar.preload_act_table_set("natural_log_exp_and_others")
            for i in range(NB):
                for half in range(2):
                    act.wait_ge(r4_hi, 2 * i + half + 1)
                    nc.scalar.copy(RT[:, i % 2, 0, half * 8:half * 8 + 8, :].rearrange("p k i -> p (k i)"),
                                   bank16[4 + half]).then_inc(r4_hi_out, 1)
            rsqrt(8, V["stat2"], V["rsq"])

        @block.vector
        def _(dve):
            ch = Chain(dve, dve_chain)
            v = nc.vector
            asked = [0]

            def rsqrt(val, to):
                ch.settle()
                v.engine_nop().then_inc(rsq_asked, 1)
                asked[0] += 1
                dve.wait_ge(rsq_given, asked[0])
                e = V["rsq"]
                ch.step(v.tensor_tensor(V["newt"], e, e, ALU.mult))
                ch.step(v.tensor_tensor(V["newt"], V["newt"], val, ALU.mult))
                ch.step(v.tensor_scalar(V["newt"], V["newt"], -0.5, 1.5, ALU.mult, ALU.add))
                ch.step(v.tensor_tensor(to, e, V["newt"], ALU.mult))

            def rows_sum(to, src3):
                ch.step(v.tensor_reduce(to, src3, AX.X, ALU.add))

            def layer_norm(t, dst):
                rows_sum(V["stat"], t)
                ch.step(v.tensor_scalar(V["stat"], V["stat"], 1.0 / D, None, ALU.mult))
                ch.step(v.tensor_tensor(dst, t, over_d(V["stat"]), ALU.subtract))
                ch.step(v.tensor_tensor(nat_t, dst, dst, ALU.mult))
                rows_sum(V["stat2"], nat_t)
                ch.step(v.tensor_scalar(V["stat2"], V["stat2"], 1.0 / D, EPS_LN, ALU.mult, ALU.add))
                rsqrt(V["stat2"], V["stat"])
                return v.tensor_tensor(dst, dst, over_d(V["stat"]), ALU.mult)

            for b in range(NB):
                dve.wait_ge(rowsum_ready, b + 1)
                ch.step(v.reciprocal(V["rd"][:, b:b + 1], V["d"][:, b:b + 1]))
                v.tensor_scalar(V["rs"][:, b:b + 1], V["rd"][:, b:b + 1], R_SCALE, None, ALU.mult).then_inc(scale_ready, 1)
                dve.wait_ge(adj_loaded[b % 2], 16 * (b // 2 + 1))
                for c in range(NC):
                    g = NC * b + c
                    dve.wait_ge(g_ready, g + 1)
                    v.tensor_tensor_reduce(w_pair[2 + g % 4], stage[:, b % 2, c * CW:(c + 1) * CW], bank[2 + g % 4][:, :],
                                           1.0, 0.0, ALU.mult, ALU.add, outer4[:, b, c:c + 1]).then_inc(g_used, 1)
                dve.wait_ge(scale_ready, b + 1)
                dve.wait_ge(hi_ready, b + 1)
                v.scalar_tensor_tensor(Rlo[:, b, :], stage[:, b % 2, :], V["rs"][:, b:b + 1], Rhi[:, b, :],
                                       ALU.mult, ALU.subtract).then_inc(lo_ready, 1)
            rsqrt(V["d"], V["dinv"])
            v.tensor_tensor(V["sqd"], V["d"], V["dinv"], ALU.mult).then_inc(vec_ready, 1)
            dve.wait_ge(small_loaded, 16 * NSMALL)
            v.engine_nop().then_inc(theta_asked, 1)
            dve.wait_ge(g_used, NC * NB)
            rows_sum(V["outer"], outer4[:, :, :])
            ch.step(v.tensor_scalar(V["outer"], V["outer"], -0.01, None, ALU.mult))
            dve.wait_ge(x_loaded, 16)
            ch.step(v.tensor_scalar(nat_y[:, :, :], nat_x[:, :, :], -0.1, 1.0, ALU.mult, ALU.add))
            ch.step(v.tensor_tensor(nat_y[:, :, :], nat_y[:, :, :], over_d(V["outer"]), ALU.add))
            ch.step(v.tensor_tensor(nat_y[:, :, :], nat_y[:, :, :], nat_x[:, :, :], ALU.add))
            dve.wait_ge(theta_given, 1)
            ch.step(v.tensor_scalar(cols[:, 16:18], cols[:, 16:18], 1.0, None, ALU.add))
            ch.step(v.reciprocal(cols[:, 16:18], cols[:, 16:18]))
            layer_norm(nat_y[:, :, :], nat_y[:, :, :]).then_inc(x1_ready, 1)

            def times_r(k, to):
                dve.wait_ge(bc_out, NC * (k + 1))
                for b in range(NB):
                    n = NB * k + b
                    dve.wait_ge(recon_ready, n + 1)
                    s = stage[:, n % 2, :]
                    v.tensor_tensor_reduce(s, s, vecB, 1.0 / R_SCALE, 0.0, ALU.mult, ALU.add,
                                           to[:, b:b + 1]).then_inc(recon_used, 1)
                dve.wait_ge(recon_used, NB * (k + 1))

            times_r(0, V["u1"])
            v.engine_nop().then_inc(vec_ready, 1)
            times_r(1, V["v2"])
            ch.step(v.tensor_scalar(V["a1"], V["u1"], C["e0"], None, ALU.mult))
            ch.step(v.scalar_tensor_tensor(V["a1"], V["v2"], C["e1"], V["a1"], ALU.mult, ALU.add))
            ch.step(v.tensor_tensor(V["a1"], V["a1"], V["sqd"], ALU.mult))
            ch.step(v.tensor_scalar(V["d2"], V["a1"], 1.0, None, ALU.add))
            rsqrt(V["d2"], V["dinv2"])
            ch.link(v.tensor_tensor(V["rowfac"], V["sqd"], V["dinv2"], ALU.mult))
            ch.link(v.tensor_scalar(C["t1s"], C["e1"], 1.0 / (R_SCALE * R_SCALE), None, ALU.mult))
            ch.link(v.tensor_scalar(C["t0s"], C["e0"], 1.0 / R_SCALE, None, ALU.mult))
            v.tensor_tensor(V["cvec"], V["dinv"], V["dinv2"], ALU.mult).then_inc(vec_ready, 1)

            def weighted(m):
                s = m % 2
                dve.wait_ge(gathered[s], 16 * TOP * (m // 2 + 1))
                if m >= 2:
                    dve.wait_ge(yT_ready, m - 1)
                ch.step(v.tensor_scalar(y_sb[:, s, :], gath[:, s, 0, :], wts[:, s, 0:1], None, ALU.mult))
                for t in range(1, TOP):
                    ins = v.scalar_tensor_tensor(y_sb[:, s, :], gath[:, s, t, :], wts[:, s, t:t + 1], y_sb[:, s, :],
                                                 ALU.mult, ALU.add)
                    if t < TOP - 1:
                        ch.step(ins)
                    else:
                        ins.then_inc(y_ready, 1)

            def residual(m):
                dve.wait_ge(yw_ready, m + 1)
                ch.step(v.tensor_tensor(nat_x[:, m, :], bank[7][:, 0:D], b1B[:, :], ALU.add))
                v.tensor_tensor(nat_x[:, m, :], nat_x[:, m, :], nat_y[:, m, :], ALU.add).then_inc(z_ready, 1)

            ch.settle()
            dve.wait_ge(bc_out, 3 * NC)
            for m in range(NB):
                dve.wait_ge(rr_ready, m + 1)
                for c in range(NC):
                    vc = stage[:, m % 2, c * CW:(c + 1) * CW]
                    dve.wait_ge(s_ready, NC * m + c + 1)
                    v.scalar_tensor_tensor(vc, bank[c][:, :], C["t1s"], vc, ALU.mult, ALU.add).then_inc(s_used, 1)
                    dve.wait_ge(s_used, NC * m + c + 1)
                    ch.link(v.tensor_tensor(vc, vc, vecB[:, c * CW:(c + 1) * CW], ALU.mult))
                if m >= 2:
                    residual(m - 2)
                ch.settle()
                s = m % 2
                ch.step(v.max(vals[:, s, :], stage[:, s, :]))
                if m >= 2:
                    dve.wait_ge(gathered[s], 16 * TOP * (m // 2))
                v.max_index(idx[:, s, :], vals[:, s, :], stage[:, s, :]).then_inc(top_ready, 1)
                if m >= 1:
                    weighted(m - 1)
                ch.step(v.tensor_scalar(wts[:, s, :], vals[:, s, 0:TOP], V["rowfac"][:, m:m + 1], None, ALU.mult))
            weighted(NB - 1)
            residual(NB - 2)
            residual(NB - 1)
            dve.wait_ge(z_ready, NB)
            ch.step(layer_norm(nat_x[:, :, :], x2))

            ch.link(v.tensor_tensor(nat_t, x2, x2, ALU.mult))
            ch.step(v.reciprocal(C["rr"], C["r"]))
            rows_sum(V["n2"], nat_t)
            ch.link(v.tensor_tensor(C["c"], C["rr"], C["rr"], ALU.mult))
            ch.step(v.tensor_scalar(C["nr"], C["rr"], -1.0, None, ALU.mult))
            ch.step(v.tensor_tensor(C["sqc"], C["rr"], C["nr"], ALU.max))
            ch.link(v.reciprocal(C["rsqc"], C["sqc"]))
            ch.link(v.tensor_scalar(C["c2"], C["c"], 2.0, None, ALU.mult))
            ch.link(v.tensor_scalar(C["cmin"], C["c"], MIN_NORM, None, ALU.mult))
            ch.link(v.tensor_scalar(V["X"], V["n2"], C["c"], None, ALU.mult))
            ch.step(v.tensor_scalar(V["pn"], V["n2"], MIN_NORM, None, ALU.max))
            ch.link(v.tensor_scalar(C["mxn"], C["rsqc"], MAX_NORM, None, ALU.mult))
            ch.link(v.tensor_scalar(V["om"], V["X"], -1.0, 1.0, ALU.mult, ALU.add))
            ch.link(v.tensor_scalar(xaug[:, :, D], V["X"], 1.0, None, ALU.add))
            rsqrt(V["pn"], V["a1"])
            ch.step(v.tensor_tensor(V["a1"], V["a1"], V["pn"], ALU.mult))
            ch.step(v.tensor_scalar(V["a1"], V["a1"], C["sqc"], None, ALU.mult))
            v.tensor_scalar(V["tcl"], V["a1"], T_MAX, None, ALU.min).then_inc(art_asked, 1)
            ch.step(v.reciprocal(V["a2"], V["a1"]))

            ch.link(v.tensor_copy(natL[0][:, :, 0:D], x2))
            ch.link(v.memset(natL[0][:, :, D], 1.0))
            ch.link(v.tensor_copy(natL[0][:, :, D + 1], V["X"]))
            ch.link(v.memset(natL[0][:, :, D + 2], 0.0))
            ch.settle()
            v.engine_nop().then_inc(nat_ready, 1)
            ch.link(v.tensor_copy(natL[1][:, :, 0:D], x2))
            ch.link(v.tensor_copy(natL[1][:, :, D], V["X"]))
            ch.link(v.memset(natL[1][:, :, D + 1], 1.0))
            ch.link(v.memset(natL[1][:, :, D + 2], 0.0))
            ch.settle()
            v.engine_nop().then_inc(nat_ready, 1)
            dve.wait_ge(art_given, 1)
            ch.step(v.tensor_tensor(V["q"], V["lnp"], V["lnm"], ALU.subtract))
            ch.step(v.tensor_tensor(V["q"], V["q"], V["a2"], ALU.mult))
            ch.step(v.tensor_scalar(V["q"], V["q"], 0.5, None, ALU.mult))
            dve.wait_ge(logit_ready, 1)
            lg = bank[2][:, 0:2 * NB].rearrange("p (b k) -> p b k", k=2)
            ch.link(v.tensor_tensor(V["left"], lg[:, :, 0], V["q"], ALU.mult))
            ch.step(v.tensor_tensor(V["right"], lg[:, :, 1], V["q"], ALU.mult))
            dve.wait_ge(aug_ready, NC)
            ch.link(v.tensor_scalar(natL[0][:, :, 0:D], x2, C["c2"], -1.0, ALU.mult, ALU.mult))
            ch.link(v.tensor_copy(natL[0][:, :, D], V["X"]))
            ch.link(v.memset(natL[0][:, :, D + 1], 1.0))
            ch.link(v.tensor_scalar(natL[0][:, :, D + 2], V["right"], C["batt"], None, ALU.add))
            ch.settle()
            v.engine_nop().then_inc(nat_ready, 1)
            dve.wait_ge(aug_ready, 2 * NC)
            ch.link(v.memset(natL[1][:, :, D], 0.0))
            ch.link(v.tensor_copy(natL[1][:, :, D + 1], V["left"]))
            ch.link(v.memset(natL[1][:, :, D + 2], 1.0))
            ch.settle()
            v.engine_nop().then_inc(nat_ready, 1)

            def distances(n):
                s = n % 2
                dve.wait_ge(dist_ready, n + 1)
                if n >= 2:
                    dve.wait_ge(w_used, n - 1)
                if n < 2:
                    dve.wait_ge(aug_ready, 4 * NC)
                ch.link(v.tensor_scalar(PT["cd"][s], bank[s][:, :], TINY, None, ALU.max))
                v.tensor_scalar(PT["dn"][s], bank[2 + s][:, :], MIN_NORM, None, ALU.max).then_inc(dist_used, 1)

            def weights(n):
                s = n % 2
                dve.wait_ge(wexp_ready, n + 1)
                dve.wait_ge(diff_ready, n + 1)
                ch.step(v.tensor_tensor(PT["dn"][s], PT["dn"][s], PT["cd"][s], ALU.mult))
                dve.wait_ge(at_ready, n + 1)
                v.tensor_tensor(PT["dn"][s], PT["dn"][s], bank[6][:, :], ALU.mult).then_inc(g3_ready, 1)

            dve.wait_ge(art_given, 1)
            distances(0)
            for n in range(NT):
                s = n % 2
                cd, dn, lz, tt = (PT[k][s] for k in ("cd", "dn", "lz", "tt"))
                dve.wait_ge(ln_ready, n + 1)
                ch.step(v.tensor_tensor(lz, cd, dn, ALU.subtract))
                v.tensor_scalar(lz, lz, C["lncmin"], None, ALU.max).then_inc(ratio_ready, 1)
                if n:
                    weights(n - 1)
                dve.wait_ge(ratio_ready, n + 1)
                ch.step(v.scalar_tensor_tensor(dn, lz, 0.5, dn, ALU.mult, ALU.add))
                dve.wait_ge(pl_ready, n + 1)
                v.scalar_tensor_tensor(dn, bank[4 + s][:, :], 0.0, dn, ALU.min, ALU.subtract).then_inc(weight_ready, 1)
                dve.wait_ge(t_ready, n + 1)
                v.tensor_scalar(tt, tt, T_MAX, None, ALU.min).then_inc(clipped_ready, 1)
                if n + 1 < NT:
                    distances(n + 1)
            weights(NT - 1)

            for q in range(NC):
                dve.wait_ge(wnat_ready, q + 1)
                v.tensor_copy(nat_u[:, BPC * q:BPC * q + BPC, :],
                              bank[q][:, :].rearrange("p (b d) -> p b d", b=BPC)[:, :, 0:D + 1]).then_inc(wnat_out, 1)
            dve.wait_ge(wnat_out, NC)
            wv, sv = nat_u[:, :, 0:D], nat_u[:, :, D]
            A, B = nat_x[:, :, :], nat_y[:, :, :]
            ch.step(v.tensor_tensor(nat_t, x2, wv, ALU.mult))
            rows_sum(V["inner"], nat_t)
            ch.link(v.scalar_tensor_tensor(V["cf"], V["inner"], C["c2"], sv, ALU.mult, ALU.subtract))
            ch.step(v.tensor_scalar(V["omc"], V["om"], MIN_NORM, None, ALU.max))
            ch.step(v.tensor_tensor(V["kf"], V["omc"], V["d"], ALU.mult))
            ch.link(v.tensor_scalar(V["kf"], V["kf"], 0.5 / R_SCALE, None, ALU.mult))
            ch.link(v.tensor_tensor(A, x2, over_d(V["cf"]), ALU.mult))
            ch.step(v.tensor_tensor(B, wv, over_d(V["om"]), ALU.mult))
            ch.step(v.tensor_tensor(A, A, B, ALU.add))
            ch.step(v.tensor_tensor(A, A, over_d(V["kf"]), ALU.mult))
            ch.step(v.tensor_tensor(nat_t, A, A, ALU.mult))
            rows_sum(V["a1"], nat_t)
            ch.step(v.tensor_scalar(V["a1"], V["a1"], MIN_NORM, None, ALU.max))
            rsqrt(V["a1"], V["a4"])
            ch.link(v.reciprocal(V["a5"], V["omc"]))
            ch.step(v.tensor_tensor(V["a2"], V["a1"], V["a4"], ALU.mult))
            ch.step(v.tensor_tensor(V["a2"], V["a2"], V["a5"], ALU.mult))
            v.tensor_scalar(V["a2"], V["a2"], C["sqc"], None, ALU.mult).then_inc(tanh_asked, 1)
            dve.wait_ge(tanh_given, 1)
            ch.step(v.tensor_tensor(V["a3"], V["a3"], V["a4"], ALU.mult))
            ch.step(v.tensor_scalar(V["a3"], V["a3"], C["rsqc"], None, ALU.mult))
            ch.step(v.tensor_tensor(B, A, over_d(V["a3"]), ALU.mult))
            ch.step(v.tensor_tensor(nat_t, B, B, ALU.mult))
            rows_sum(V["a1"], nat_t)
            ch.step(v.tensor_tensor(nat_t, B, x2, ALU.mult))
            rows_sum(V["a2"], nat_t)
            ch.link(v.tensor_scalar(V["a3"], V["a1"], C["c"], None, ALU.mult))
            ch.step(v.tensor_scalar(V["a2"], V["a2"], C["c2"], 1.0, ALU.mult, ALU.add))
            ch.link(v.tensor_tensor(V["a4"], V["a2"], V["a3"], ALU.add))
            ch.step(v.tensor_tensor(V["a5"], V["X"], V["a3"], ALU.mult))
            ch.step(v.tensor_tensor(V["a5"], V["a5"], V["a2"], ALU.add))
            ch.step(v.tensor_scalar(V["a5"], V["a5"], MIN_NORM, None, ALU.max))
            ch.step(v.reciprocal(V["a6"], V["a5"]))
            ch.link(v.tensor_tensor(V["a4"], V["a4"], V["a6"], ALU.mult))
            ch.step(v.tensor_tensor(V["a5"], V["om"], V["a6"], ALU.mult))
            ch.link(v.tensor_tensor(A, x2, over_d(V["a4"]), ALU.mult))
            ch.step(v.tensor_tensor(B, B, over_d(V["a5"]), ALU.mult))
            ch.step(v.tensor_tensor(A, A, B, ALU.add))
            ch.step(v.tensor_tensor(nat_t, A, A, ALU.mult))
            rows_sum(V["a1"], nat_t)
            ch.step(v.tensor_scalar(V["a1"], V["a1"], MIN_NORM, None, ALU.max))
            rsqrt(V["a1"], V["a2"])
            ch.step(v.tensor_scalar(V["a2"], V["a2"], C["mxn"], 1.0, ALU.mult, ALU.min))
            ch.step(v.tensor_tensor(A, A, over_d(V["a2"]), ALU.mult))
            ch.step(v.tensor_tensor(A, A, x2, ALU.add))
            layer_norm(A, nat_y[:, :, :]).then_inc(x3_ready, 1)

            ch.step(v.tensor_tensor(C["hb"], C["w1t"], C["tl3"], ALU.mult))
            ch.link(v.tensor_tensor(C["hb"], C["hb"], C["b1c"], ALU.add))
            ch.step(v.tensor_scalar(V["dsc"], V["d"], 1.0 / R_SCALE, None, ALU.mult))
            v.engine_nop().then_inc(x3_ready, 1)
            for q in range(2):
                bl = slice(8 * q, 8 * q + 8)
                dve.wait_ge(xb_hi, q + 1)
                ch.step(v.tensor_copy(nat_x[:, bl, :], bank[q][:, :].rearrange("p (b d) -> p b d", b=8)))
                v.tensor_tensor(xbs[:, bl, 1, :], nat_x[:, bl, :], xbs[:, bl, 0, :], ALU.subtract).then_inc(xb_split, 1)
            ch.settle()
            ch.link(v.tensor_tensor(nat_t, nat_x[:, :, :], over_d(V["d"]), ALU.mult))
            for q in range(2):
                bl = slice(8 * q, 8 * q + 8)
                dve.wait_ge(u_ready, q + 1)
                ch.link(v.tensor_tensor(base[:, bl, :], bank[2 + q][:, :].rearrange("p (b d) -> p b d", b=8),
                                        b2B[:, :].unsqueeze(1).to_broadcast([P, 8, D]), ALU.add))
            ch.settle()
            ch.step(v.tensor_tensor(base, base, nat_t, ALU.subtract))

            def low_out(i):
                for half in range(2):
                    dve.wait_ge(r4_lo, 2 * i + half + 1)
                    v.tensor_copy(RT[:, i % 2, 1, half * 8:half * 8 + 8, :].rearrange("p k i -> p (k i)"),
                                  bank16[half]).then_inc(r4_lo_out, 1)

            low_out(0)
            for i in range(NB):
                if i + 1 < NB:
                    low_out(i + 1)
                dve.wait_ge(ax_ready, i + 1)
                o = bank[6 + i % 2]
                ch.step(v.scalar_tensor_tensor(base[:, i, :], o[:, D:2 * D], V["dsc"][:, i:i + 1], base[:, i, :],
                                               ALU.mult, ALU.add))
                v.scalar_tensor_tensor(base[:, i, :], o[:, 0:D], V["dsc"][:, i:i + 1], base[:, i, :],
                                       ALU.mult, ALU.add).then_inc(ax_used, 1)
            dve.wait_ge(ax_used, NB)
            ch.step(v.tensor_tensor(base, base, nat_y[:, :, :], ALU.add))
            layer_norm(base, nat_y[:, :, :]).then_inc(o_ready, 1)

        @block.tensor
        def _(pe):
            mm = nc.tensor.matmul

            def spread(k):
                for n in range(NC * k, NC * k + NC):
                    pe.wait_ge(diag_ready, BPC * (n + 1))
                    if n >= 2:
                        pe.wait_ge(bc_out, n - 1)
                    mm(bank[6 + n % 2][:, :], ones[:, :], w_pair[n % 2], start=True, stop=True).then_inc(bc_ready, 1)

            def turn(m):
                for g in range(4 * m, 4 * m + 4):
                    part, half = (Rhi, Rlo)[(g % 4) // 2], g % 2
                    if g >= 2:
                        pe.wait_ge(rt_out, g - 1)
                    for k in range(8):
                        ins = nc.tensor.transpose(bank16[4 + g % 2][:, k * P:(k + 1) * P],
                                                  part[:, m, (8 * half + k) * P:(8 * half + k + 1) * P], ident[:, :])
                    ins.then_inc(rt_ready, 1)

            def square(m, c):
                if c == 0:
                    pe.wait_ge(rt_out, 4 * (m + 1))
                if m:
                    pe.wait_ge(s_used, NC * (m - 1) + c + 1)
                cs = slice(c * CW, (c + 1) * CW)
                for k in range(NB):
                    hi, lo = RT[:, m % 2, 0, k, :], RT[:, m % 2, 1, k, :]
                    mm(bank[c][:, :], hi, Rhi[:, k, cs], start=(k == 0), stop=False)
                    mm(bank[c][:, :], hi, Rlo[:, k, cs], start=False, stop=False)
                    ins = mm(bank[c][:, :], lo, Rhi[:, k, cs], start=False, stop=(k == NB - 1))
                ins.then_inc(s_ready, 1)

            def turn_y(m):
                pe.wait_ge(y_ready, m + 1)
                if m >= 1:
                    pe.wait_ge(yT_out, m)
                nc.tensor.transpose(bank[6][0:D, 0:P], y_sb[:, m % 2, :], identf[:, :]).then_inc(yT_ready, 1)

            def y_w(m):
                pe.wait_ge(yT_out, m + 1)
                if m >= 1:
                    pe.wait_ge(z_ready, m)
                mm(bank[7][:, 0:D], yT[:, m % 2, :], wlT[:, :], start=True, stop=True).then_inc(yw_ready, 1)

            pe.wait_ge(consts_ready, 3)
            pe.wait_ge(x_loaded, 16)
            for q in range(NC):
                if q >= 2:
                    pe.wait_ge(tr_out, q - 1)
                for j in range(BPC):
                    ins = nc.tensor.transpose(bank[q % 2][0:D, j * P:(j + 1) * P], nat_x[:, BPC * q + j, :], identf[:, :])
                ins.then_inc(tr_ready, 1)
            pe.wait_ge(tr_out, NC)
            for g in range(NC * NB):
                b, c = g // NC, g % NC
                if g >= 4:
                    pe.wait_ge(g_used, g - 3)
                mm(bank[2 + g % 4][:, :], xT[0:D, b * P:(b + 1) * P], xT[0:D, c * CW:(c + 1) * CW],
                   start=True, stop=True).then_inc(g_ready, 1)
            spread(0)
            pe.wait_ge(small_loaded, 16 * NSMALL)
            nc.tensor.transpose(bank[0][0:D, 0:D], wl_nat[:, :], identf[0:D, 0:D])
            nc.tensor.transpose(bank[0][0:D, D:2 * D], bl_nat[:, :], identf[0:D, 0:D]).then_inc(wT_ready, 1)
            pe.wait_ge(lo_ready, NB)
            pe.wait_ge(g_used, NC * NB)
            turn(0)
            pe.wait_ge(wT_out, 2)
            for c in range(NC):
                square(0, c)
            spread(1)
            turn(1)
            spread(2)
            for m in range(1, NB):
                square(m, 0)
                square(m, 1)
                if m >= 2:
                    turn_y(m - 2)
                square(m, 2)
                if m >= 2:
                    y_w(m - 2)
                if m + 1 < NB:
                    turn(m + 1)
                square(m, 3)
            for m in (NB - 2, NB - 1):
                turn_y(m)
                y_w(m)

            def aug(kind):
                pe.wait_ge(nat_ready, kind + 1)
                for q in range(NC):
                    n = NC * kind + q
                    if n >= 2:
                        pe.wait_ge(aug_out, n - 1)
                    for j in range(BPC):
                        ins = nc.tensor.transpose(bank[n % 2][0:KA, j * P:(j + 1) * P], natL[kind % 2][:, BPC * q + j, :],
                                                  identf[:, :])
                    ins.then_inc(aug_ready, 1)

            aug(0)
            aug(1)
            for b in range(NB):
                ins = mm(bank[2][:, 2 * b:2 * b + 2], AUG[0:D, 0, b * P:(b + 1) * P], watt[:, :], start=True, stop=True)
            ins.then_inc(logit_ready, 1)
            aug(2)
            aug(3)
            pe.wait_ge(aug_out, 4 * NC)

            def pair_products(n):
                c, j, s = n // NB, n % NB, n % 2
                js, cs = slice(j * P, (j + 1) * P), slice(c * CW, (c + 1) * CW)
                if n >= 2:
                    pe.wait_ge(dist_used, n - 1)
                mm(bank[s][:, :], AUG[0:KA, 2, js], AUG[0:KA, 0, cs], start=True, stop=True)
                mm(bank[2 + s][:, :], AUG[0:KA, 2, js], AUG[0:KA, 1, cs], start=True, stop=True).then_inc(dist_ready, 1)
                if n >= 2:
                    pe.wait_ge(weight_ready, n - 1)
                    pe.wait_ge(sig_ready, n - 1)
                mm(bank[4 + s][:, :], AUG[D:KA, 2, js], AUG[D:KA, 3, cs], start=True, stop=True).then_inc(pl_ready, 1)

            def adjacency(n):
                c, j = n // NB, n % NB
                if n >= 1:
                    pe.wait_ge(g3_ready, n)
                for k in range(BPC):
                    i = BPC * c + k
                    o = bank[6][:, k * P:(k + 1) * P]
                    mm(o, Rhi[:, i, j * P:(j + 1) * P], ident[:, :], start=True, stop=False)
                    ins = mm(o, Rlo[:, i, j * P:(j + 1) * P], ident[:, :], start=False, stop=True)
                ins.then_inc(at_ready, 1)

            pair_products(0)
            adjacency(0)
            for n in range(NT):
                if n + 1 < NT:
                    pair_products(n + 1)
                c, j = n // NB, n % NB
                pe.wait_ge(g3_ready, n + 1)
                if j == 0 and c:
                    pe.wait_ge(wsum_out, c)
                mm(bank[7][0:D + 1, :], xaug[:, j, :], PT["dn"][n % 2], start=(j == 0), stop=(j == NB - 1)).then_inc(w_used, 1)
                if n + 1 < NT:
                    adjacency(n + 1)
            pe.wait_ge(wsum_out, NC)
            for q in range(NC):
                for j in range(BPC):
                    b = BPC * q + j
                    ins = nc.tensor.transpose(bank[q][:, j * P:j * P + D + 1], WTs[0:D + 1, b * P:(b + 1) * P],
                                              identf[0:D + 1, 0:D + 1])
                ins.then_inc(wnat_ready, 1)

            pe.wait_ge(x3_ready, 2)
            for q in range(NC):
                if q >= 2:
                    pe.wait_ge(x3T_out, q - 1)
                for j in range(BPC):
                    ins = nc.tensor.transpose(bank[q % 2][0:D, j * P:(j + 1) * P], nat_y[:, BPC * q + j, :], identf[:, :])
                ins.then_inc(x3T_ready, 1)
            pe.wait_ge(x3T_out, NC)
            for q in range(NC):
                if q >= 2:
                    pe.wait_ge(h_out, q - 1)
                mm(bank[2 + q % 2][:, :], w1_sb[:, :], x3T[0:D, q * CW:(q + 1) * CW], start=True, stop=True).then_inc(h_ready, 1)
            for q in range(2):
                for b in range(8):
                    i = 8 * q + b
                    ins = mm(bank[q][:, b * D:(b + 1) * D], x3T[0:D, i * P:(i + 1) * P], blT[:, :], start=True, stop=True)
                ins.then_inc(xb_ready, 1)
            pe.wait_ge(h_out, NC)
            for q in range(2):
                for b in range(8):
                    i = 8 * q + b
                    ins = mm(bank[2 + q][:, b * D:(b + 1) * D], hT[:, i * P:(i + 1) * P], w2_sb[:, :], start=True, stop=True)
                ins.then_inc(u_ready, 1)
            pe.wait_ge(xb_split, 2)

            def turn4(i):
                for half in range(2):
                    for part, bk, made, out_ in ((Rhi, 4, r4_hi, r4_hi_out), (Rlo, 0, r4_lo, r4_lo_out)):
                        if i:
                            pe.wait_ge(out_, 2 * (i - 1) + half + 1)
                        for k in range(8):
                            ins = nc.tensor.transpose(bank16[bk + half][:, k * P:(k + 1) * P],
                                                      part[:, i, (8 * half + k) * P:(8 * half + k + 1) * P], ident[:, :])
                        ins.then_inc(made, 1)

            turn4(0)
            for i in range(NB):
                if i + 1 < NB:
                    turn4(i + 1)
                pe.wait_ge(r4_hi_out, 2 * i + 2)
                pe.wait_ge(r4_lo_out, 2 * i + 2)
                if i >= 2:
                    pe.wait_ge(ax_used, i - 1)
                o = bank[6 + i % 2]
                for k in range(NB):
                    mm(o[:, 0:2 * D], RT[:, i % 2, 0, k, :], xbs[:, k, :, :].rearrange("p h d -> p (h d)"),
                       start=(k == 0), stop=False, skip_group_check=True)
                    ins = mm(o[:, 0:D], RT[:, i % 2, 1, k, :], xbs[:, k, 0, :], start=False, stop=(k == NB - 1),
                             skip_group_check=True)
                ins.then_inc(ax_ready, 1)


_INS = ["x", "adj", "L1_gnn_theta", "L1_gnn_W", "L1_gnn_b", "L2_gnn_r", "L2_gnn_w_att", "L2_gnn_b_att",
        "L3_gnn_t", "L3_gnn_B", "L3_gnn_W1", "L3_gnn_b1", "L3_gnn_W2", "L3_gnn_b2"]


def kernel(**inputs):
    import numpy as _np
    import concourse.bacc as _bacc
    from concourse import mybir as _mybir
    from concourse.bass_utils import run_bass_kernel_spmd as _run

    nc = _bacc.Bacc("TRN2", target_bir_lowering=False, num_devices=1)
    arrays, args = {}, []
    for name in _INS:
        a = _np.ascontiguousarray(inputs[name])
        arrays[f"in_{name}_dram"] = a
        args.append(nc.dram_tensor(f"in_{name}_dram", a.shape, _mybir.dt.from_np(a.dtype), kind="ExternalInput").ap())
    out = nc.dram_tensor("out_dram", (2048, 64), _mybir.dt.float32, kind="ExternalOutput").ap()
    build(nc, *args, out)
    res = _run(nc, [arrays], core_ids=[0])
    return res.results[0]["out_dram"]
```

```python
from contextlib import ExitStack

import concourse.bass as bass
from concourse import mybir

ALU = mybir.AluOpType
ACT = mybir.ActivationFunctionType
AX = mybir.AxisListType
F32 = mybir.dt.float32
F16 = mybir.dt.float16
BF16 = mybir.dt.bfloat16
U32 = mybir.dt.uint32

P = 128
EPS_LN = 1e-5
MIN_NORM = 1e-15
T_MAX = 1.0 - 1e-7
MAX_NORM = 1.0 - 0.004
R_SCALE = 4096.0
TINY = 2.0 ** -60


class Chain:

    def __init__(self, eng, sem):
        self.eng, self.sem, self.n = eng, sem, 0

    def link(self, ins):
        ins.then_inc(self.sem, 1)
        self.n += 1

    def settle(self):
        self.eng.wait_ge(self.sem, self.n)

    def step(self, ins):
        self.link(ins)
        self.settle()


def build(nc, x, adj, theta, w_l1, b_l1, r, w_att, b_att, t_l3, b_l3, w1, b1, w2, b2, out):
    N, D = x.shape
    NB = N // P
    CW = 512
    NC = N // CW
    BPC = CW // P
    H = w1.shape[1]
    TOP = 4
    E0, E1 = D, D + 6
    LROW = 32

    ctx = ExitStack()
    with ctx:
        def sb(name, shape, dt=F32):
            return ctx.enter_context(nc.sbuf_tensor(name, shape, dt))

        def sem(name):
            return ctx.enter_context(nc.semaphore(name))

        Rhi = sb("Rhi", [P, NB, N], F16)
        Rlo = sb("Rlo", [P, NB, N], F16)
        scratch = sb("scratch", [P, 12288])
        stage = scratch[:, 0:2 * N].rearrange("p (s n) -> p s n", s=2)
        NS = 3
        load = scratch[:, 0:NS * N].rearrange("p (s n) -> p s n", s=NS)
        vecB = scratch[:, 2 * N:3 * N]
        RT = scratch[:, 3 * N:5 * N].bitcast(F16).rearrange("p (s h k i) -> p s h k i", s=2, h=2, k=NB)
        xT = scratch[:, 5 * N:6 * N].bitcast(F16).rearrange("p (w n) -> p w n", w=2)
        AUG = scratch[:, 0:2 * N].bitcast(F16).rearrange("p (w n) -> p w n", w=4)
        WTs = scratch[:, 4 * N:5 * N]
        hT = scratch[:, N:2 * N]
        nat_t = scratch[:, 5 * N:5 * N + NB * D].rearrange("p (b d) -> p b d", b=NB)
        nat_u = scratch[:, 0:NB * (D + 1)].rearrange("p (b d) -> p b d", b=NB)
        small = scratch[:, 5 * N + NB * D:6 * N]
        gath = small[:, 0:2 * TOP * D].rearrange("p (s t d) -> p s t d", s=2, t=TOP)
        y_sb = small[:, 512:512 + 2 * D].rearrange("p (s d) -> p s d", s=2)
        yT = small[0:D, 640:640 + 2 * P].rearrange("p (s d) -> p s d", s=2)
        natL = [scratch[:, a:a + NB * D].bitcast(F16).rearrange("p (b d) -> p b d", b=NB) for a in (3 * N, 3 * N + NB * D)]
        natW = [t.bitcast(BF16) for t in natL]
        x3T = scratch[:, 0:N]
        base = scratch[:, 2 * N:2 * N + NB * D].rearrange("p (b d) -> p b d", b=NB)
        xbs = scratch[:, 2 * N + NB * D:3 * N].bitcast(F16).rearrange("p (b h d) -> p b h d", b=NB, h=2)
        nat_x = sb("nat_x", [P, NB, D])
        nat_y = sb("nat_y", [P, NB, D])
        xaug = sb("xaug", [P, NB, D + 1])
        x2 = xaug[:, :, 0:D]
        xT_low = xaug[0:D, :, :].rearrange("p b d -> p (b d)")[:, 0:N // 2].bitcast(F16)
        work = sb("work", [P, 6, CW])
        w_pair = [work[:, i, :] for i in range(6)]
        identf = sb("identf", [P, P])
        ident = sb("ident", [P, P], F16)
        ones = sb("ones", [P, P])
        sm = sb("sm", [P, 40, NB])
        cols = sb("cols", [P, 24])
        outer4 = sb("outer4", [P, NB, NC])
        vals = sb("vals", [P, 2, 8])
        wts = sb("wts", [P, 2, TOP])
        idx = sb("idx", [P, 2, 8], U32)
        wl_nat = sb("wl_nat", [D, D])
        bl_nat = sb("bl_nat", [D, D])
        wlT = sb("wlT", [D, D])
        blT = sb("blT", [D, D])
        w1_sb = sb("w1_sb", [D, H])
        w2_sb = sb("w2_sb", [H, D])
        wattB = sb("wattB", [P, 2, D])
        b1B = sb("b1B", [P, D])
        b2B = sb("b2B", [P, D])
        x1_dram = nc.dram_tensor("x1_scratch", [N, D], F32, kind="Internal").ap()
        bank = [ctx.enter_context(nc.psum_tensor(f"bank{i}", [P, CW], F32)) for i in range(8)]
        bank16 = [b[:, :].bitcast(F16) for b in bank]

        names = ["d", "rd", "rs", "part", "rest", "outer", "stat", "stat2", "rsq", "newt", "dinv", "sqd", "u1", "v2", "d2", "dinv2",
                 "cvec", "rowfac", "n2", "X", "om", "pn", "tcl", "lnp", "lnm", "q", "left", "right", "s", "inner",
                 "cf", "kf", "a1", "a2", "a3", "a4", "a5", "a6", "dsc", "omc"]
        V = {n: sm[:, i, :] for i, n in enumerate(names)}
        cn = ["th0", "th1", "t0s", "t1s", "r", "rr", "c", "nc2", "batt", "tl3", "b1c", "w1t", "hb", "cmin", "lncmin", "sqc",
              "rsqc", "e0", "e1", "c2", "mxn", "nr"]
        C = {n: cols[:, i:i + 1] for i, n in enumerate(cn)}

        free = [nat_x[:, 0:8, :].rearrange("p b d -> p (b d)"), nat_x[:, 8:16, :].rearrange("p b d -> p (b d)"),
                nat_y[:, 0:8, :].rearrange("p b d -> p (b d)"), nat_y[:, 8:16, :].rearrange("p b d -> p (b d)")]
        free = free + w_pair + [scratch[:, 5 * N + i * CW:5 * N + (i + 1) * CW] for i in range(4)]
        depth = {"cd": 4, "dn": 4, "sg": 2, "lz": 2, "tt": 2}
        PT = {}
        for name, k in depth.items():
            PT[name], free = free[0:k], free[k:]

        def pt(name, n):
            return PT[name][n % depth[name]]

        i01 = cn.index("e0")
        C01 = cols[:, i01:i01 + 2]

        x_hl = work[:, 0:2, :].rearrange("p w n -> p (w n)").bitcast(F16).rearrange("p (b d) -> p b d", b=NB)
        x_hh = work[:, 2:4, :].rearrange("p w n -> p (w n)").bitcast(F16).rearrange("p (b d) -> p b d", b=NB)

        def over_d(v):
            return v.unsqueeze(2).to_broadcast([P, NB, D])

        consts_ready = sem("consts_ready")
        x_split = sem("x_split")
        x_loaded = sem("x_loaded")
        small_loaded = sem("small_loaded")
        adj_loaded = [sem(f"adj_loaded{i}") for i in range(NS)]
        dve_chain, act_chain, pool_chain = sem("dve_chain"), sem("act_chain"), sem("pool_chain")
        tr_ready, tr_out = sem("tr_ready"), sem("tr_out")
        g_ready, g_used = sem("g_ready"), sem("g_used")
        rowsum_ready, scale_ready, hi_ready, lo_ready = sem("rowsum_ready"), sem("scale_ready"), sem("hi_ready"), sem("lo_ready")
        rsq_asked, rsq_given = sem("rsq_asked"), sem("rsq_given")
        theta_loaded, theta_given, theta_ready = sem("theta_loaded"), sem("theta_given"), sem("theta_ready")
        x1_ready, x1_stored = sem("x1_ready"), sem("x1_stored")
        vec_ready, diag_ready, bc_ready, bc_out = sem("vec_ready"), sem("diag_ready"), sem("bc_ready"), sem("bc_out")
        mv_ready, mv_used = sem("mv_ready"), sem("mv_used")
        rt_ready, rt_out, rt_out_lo = sem("rt_ready"), sem("rt_out"), sem("rt_out_lo")
        s_ready, s_used = sem("s_ready"), sem("s_used")
        rr_ready, top_ready = sem("rr_ready"), sem("top_ready")
        gathered = [sem(f"gathered{i}") for i in range(2)]
        y_ready, yT_ready, yT_out, yw_ready, z_ready = (sem(n) for n in ["y_ready", "yT_ready", "yT_out", "yw_ready", "z_ready"])
        wT_ready, wT_out = sem("wT_ready"), sem("wT_out")
        abs_ready = sem("abs_ready")
        art_asked, art_given = sem("art_asked"), sem("art_given")
        nat_ready, aug_ready, aug_out = sem("nat_ready"), sem("aug_ready"), sem("aug_out")
        logit_ready = sem("logit_ready")
        dist_ready, dist_used, pl_ready, pl_used = sem("dist_ready"), sem("dist_used"), sem("pl_ready"), sem("pl_used")
        ln_ready, sig_ready, ratio_ready, t_ready = sem("ln_ready"), sem("sig_ready"), sem("ratio_ready"), sem("t_ready")
        weight_ready, clipped_ready, logw_ready = sem("weight_ready"), sem("clipped_ready"), sem("logw_ready")
        artanh_ready, wexp_ready, diff_ready = sem("artanh_ready"), sem("wexp_ready"), sem("diff_ready")
        at_ready, g3_ready, w_used, wsum_out = sem("at_ready"), sem("g3_ready"), sem("w_used"), sem("wsum_out")
        wnat_ready, wnat_out = sem("wnat_ready"), sem("wnat_out")
        tanh_asked, tanh_given = sem("tanh_asked"), sem("tanh_given")
        x3_ready, x3T_ready, x3T_out = sem("x3_ready"), sem("x3T_ready"), sem("x3T_out")
        h_ready, h_out, xb_ready, xb_hi, xb_split = sem("h_ready"), sem("h_out"), sem("xb_ready"), sem("xb_hi"), sem("xb_split")
        u_ready, u_used, ax_ready, ax_used = sem("u_ready"), sem("u_used"), sem("ax_ready"), sem("ax_used")
        r4_hi, r4_lo, r4_hi_out, r4_lo_out = sem("r4_hi"), sem("r4_lo"), sem("r4_hi_out"), sem("r4_lo_out")
        o_ready = sem("o_ready")
        out_stored = sem("out_stored")

        block = ctx.enter_context(nc.Block())
        NSMALL = 12
        NT = NC * NB

        @block.sync
        def _(sp):
            sp.dma_start(nat_x[:, :, :], x.rearrange("(b p) d -> p b d", p=P)).then_inc(x_loaded, 16)
            sp.dma_start(C["th0"], theta[0:1].partition_broadcast(P)).then_inc(theta_loaded, 16)
            sp.dma_start(C["th1"], theta[1:2].partition_broadcast(P)).then_inc(theta_loaded, 16)
            for b in range(NB):
                if b == 3:
                    sp.dma_start(C["r"], r.partition_broadcast(P)).then_inc(small_loaded, 16)
                    sp.dma_start(C["batt"], b_att.partition_broadcast(P)).then_inc(small_loaded, 16)
                    sp.dma_start(C["tl3"], t_l3.partition_broadcast(P)).then_inc(small_loaded, 16)
                    sp.dma_start(C["b1c"], b1.unsqueeze(1)).then_inc(small_loaded, 16)
                    sp.dma_start(C["w1t"], w1[D:D + 1, :].rearrange("a h -> h a")).then_inc(small_loaded, 16)
                    sp.dma_start(wl_nat[:, :], w_l1).then_inc(small_loaded, 16)
                    sp.dma_start(bl_nat[:, :], b_l3).then_inc(small_loaded, 16)
                    sp.dma_start(w1_sb[:, :], w1[0:D, :]).then_inc(small_loaded, 16)
                    sp.dma_start(w2_sb[:, :], w2).then_inc(small_loaded, 16)
                    sp.dma_start(wattB[:, :, :].rearrange("p k d -> p (k d)"),
                                 w_att.rearrange("(d a) o -> d (a o)", a=1).rearrange("d a -> a d").squeeze(0).partition_broadcast(P)
                                 ).then_inc(small_loaded, 16)
                    sp.dma_start(b1B[:, :], b_l1.partition_broadcast(P)).then_inc(small_loaded, 16)
                    sp.dma_start(b2B[:, :], b2.partition_broadcast(P)).then_inc(small_loaded, 16)
                if b >= NS:
                    sp.wait_ge(lo_ready, b - NS + 1)
                sp.dma_start(load[:, b % NS, :], adj[b * P:(b + 1) * P, :]).then_inc(adj_loaded[b % NS], 16)
            sp.wait_ge(x1_ready, 1)
            sp.dma_start(x1_dram.rearrange("(b p) d -> p b d", p=P), nat_y[:, :, :]).then_inc(x1_stored, 16)
            sp.wait_ge(o_ready, 1)
            sp.dma_start(out.rearrange("(b p) d -> p b d", p=P), nat_y[:, :, :]).then_inc(out_stored, 16)
            sp.wait_ge(out_stored, 16)
            sp.wait_ge(x1_stored, 16)

        @block.gpsimd
        def _(pool):
            ch = Chain(pool, pool_chain)
            ch.link(nc.gpsimd.memset(identf[:, :], 0.0))
            ch.link(nc.gpsimd.memset(ident[:, :], 0.0))
            nc.gpsimd.memset(ones[:, :], 1.0).then_inc(consts_ready, 1)
            ch.settle()
            for m in (identf, ident):
                nc.gpsimd.affine_select(out=m[:, :], in_=m[:, :], compare_op=ALU.not_equal, fill=1.0, base=0,
                                        pattern=[[-1, P]], channel_multiplier=1).then_inc(consts_ready, 1)

            def diag(k, vec):
                pool.wait_ge(vec_ready, k + 1)
                for q in range(NC):
                    n = NC * k + q
                    if n >= 2:
                        pool.wait_ge(bc_ready, n - 1)
                    for j in range(BPC):
                        b = BPC * q + j
                        ins = nc.gpsimd.tensor_scalar(w_pair[n % 2][:, j * P:(j + 1) * P], identf[:, :], vec[:, b:b + 1],
                                                      None, ALU.mult)
                        ins.then_inc(diag_ready, 1)

            pool.wait_ge(consts_ready, 3)
            def start_v(m):
                v = stage[:, 1 - m % 2, :]
                if m < 2:
                    pool.wait_ge(lo_ready, NB - 2 * (1 - m))
                else:
                    pool.wait_ge(top_ready, m - 1)
                ch.step(nc.gpsimd.tensor_tensor(v, Rhi[:, m, :], Rlo[:, m, :], ALU.add))
                ch.step(nc.gpsimd.tensor_scalar(v, v, C["t0s"], None, ALU.mult))
                d = v[:, m * P:(m + 1) * P]
                nc.gpsimd.tensor_tensor(d, d, identf[:, :], ALU.add).then_inc(rr_ready, 1)

            pool.wait_ge(theta_ready, 1)
            start_v(0)
            diag(0, V["dinv"])
            start_v(1)
            diag(1, V["u1"])
            diag(2, V["cvec"])
            pool.wait_ge(x1_stored, 16)
            for m in range(NB):
                pool.wait_ge(top_ready, m + 1)
                if m >= 2:
                    pool.wait_ge(y_ready, m - 1)
                for t in range(TOP):
                    nc.gpsimd.indirect_dma_start(gath[:, m % 2, t, :], None, x1_dram,
                                                 bass.IndirectOffsetOnAxis(idx[:, m % 2, t:t + 1], 0)).then_inc(gathered[m % 2], 16)
                if m + 2 < NB:
                    start_v(m + 2)


            for n in range(NT):
                dn, cd, tt = pt("dn", n), pt("cd", n), pt("tt", n)
                pool.wait_ge(weight_ready, n + 1)
                pool.wait_ge(sig_ready, n + 1)
                nc.gpsimd.tensor_tensor(dn, dn, pt("sg", n), ALU.subtract).then_inc(logw_ready, 1)
                pool.wait_ge(artanh_ready, n + 1)
                ch.step(nc.gpsimd.tensor_tensor(cd, cd, tt, ALU.subtract))
                pool.wait_ge(wexp_ready, n + 1)
                nc.gpsimd.tensor_tensor(dn, dn, cd, ALU.mult).then_inc(diff_ready, 1)

        @block.scalar
        def _(act):
            ch = Chain(act, act_chain)
            nc.scalar.preload_act_table_set("natural_log_exp_and_others")

            def rsqrt(k, v, e):
                act.wait_ge(rsq_asked, k + 1)
                ch.step(nc.scalar.activation(e, v, ACT.Ln))
                nc.scalar.activation(e, e, ACT.Exp, scale=-0.5).then_inc(rsq_given, 1)

            def spread_out(k):
                for n in range(NC * k, NC * k + NC):
                    act.wait_ge(bc_ready, n + 1)
                    q = n % NC
                    nc.scalar.copy(vecB[:, q * CW:(q + 1) * CW], bank[6 + n % 2][:, :]).then_inc(bc_out, 1)

            def turned_out(m):
                for g in range(4 * m, 4 * m + 4):
                    h, half = (g % 4) // 2, g % 2
                    act.wait_ge(rt_ready, g + 1)
                    nc.scalar.copy(RT[:, m % 2, h, half * 8:half * 8 + 8, :].rearrange("p k i -> p (k i)"),
                                   bank16[4 + g % 2]).then_inc(rt_out, 1)

            act.wait_ge(theta_loaded, 32)
            nc.scalar.activation(C01, cols[:, 0:2], ACT.Exp, scale=-1.0).then_inc(theta_given, 1)
            for n in range(6):
                kind, half = n // 2, n % 2
                to = (xT[:, 0, :], xT[:, 1, :], xT_low)[kind]
                act.wait_ge(tr_ready, n + 1)
                nc.scalar.copy(to[:, half * N // 2:(half + 1) * N // 2],
                               bank16[n % 2][0:to.shape[0], :]).then_inc(tr_out, 1)
            def rowsum(b):
                act.wait_ge(adj_loaded[b % NS], 16 * (b // NS + 1))
                nc.scalar.activation(Rhi[:, b, :], load[:, b % NS, :], ACT.Copy,
                                     accum_out=V["d"][:, b:b + 1]).then_inc(rowsum_ready, 1)

            rowsum(0)
            for b in range(NB):
                if b + 1 < NB:
                    rowsum(b + 1)
                act.wait_ge(scale_ready, b + 1)
                nc.scalar.activation(Rhi[:, b, :], load[:, b % NS, :], ACT.Copy,
                                     scale=V["rs"][:, b:b + 1]).then_inc(hi_ready, 1)
                if b == 2:
                    turned_out(0)
            rsqrt(0, V["d"], V["rsq"])
            spread_out(0)
            act.wait_ge(wT_ready, 1)
            nc.scalar.copy(wlT[:, :], bank[6][0:D, 0:D]).then_inc(wT_out, 1)
            nc.scalar.copy(blT[:, :], bank[6][0:D, D:2 * D]).then_inc(wT_out, 1)
            turned_out(1)
            spread_out(1)
            turned_out(2)
            rsqrt(1, V["d2"], V["rsq"])
            spread_out(2)
            turned_out(3)
            rsqrt(2, V["stat2"], V["rsq"])

            def turn_y(m):
                act.wait_ge(yT_ready, m + 1)
                nc.scalar.copy(yT[:, m % 2, :], bank[6][0:D, 0:P]).then_inc(yT_out, 1)

            turn_y(0)
            for m in range(3, NB):
                turn_y(m - 2)
                if m + 1 < NB:
                    turned_out(m + 1)
            turn_y(NB - 2)
            turn_y(NB - 1)
            rsqrt(3, V["stat2"], V["rsq"])
            rsqrt(4, V["pn"], V["rsq"])
            act.wait_ge(art_asked, 1)
            nc.scalar.activation(V["lnp"], V["tcl"], ACT.Ln, bias=1.0)
            nc.scalar.activation(V["lnm"], V["tcl"], ACT.Ln, bias=1.0, scale=-1.0)
            nc.scalar.activation(C["lncmin"], C["cmin"], ACT.Ln).then_inc(art_given, 1)
            for n in range(8):
                kind, half = n // 2, n % 2
                rows = P if kind < 2 else D
                act.wait_ge(aug_ready, n + 1)
                nc.scalar.copy(AUG[0:rows, kind, half * N // 2:(half + 1) * N // 2],
                               bank16[n % 2][0:rows, :]).then_inc(aug_out, 1)

            def exp_logit(n):
                sg = pt("sg", n)
                act.wait_ge(pl_ready, n + 1)
                if n >= 2:
                    act.wait_ge(weight_ready, n - 1)
                    act.wait_ge(logw_ready, n - 1)
                nc.scalar.activation(sg, bank[4 + n % 2][:, :], ACT.Abs).then_inc(abs_ready, 1)
                act.wait_ge(abs_ready, n + 1)
                ch.step(nc.scalar.activation(sg, sg, ACT.Exp, scale=-1.0))

            def log_logit(n):
                nc.scalar.activation(pt("sg", n), pt("sg", n), ACT.Ln, bias=1.0).then_inc(sig_ready, 1)

            def logs(n):
                act.wait_ge(dist_used, n + 1)
                nc.scalar.activation(pt("cd", n), pt("cd", n), ACT.Ln)
                nc.scalar.activation(pt("dn", n), pt("dn", n), ACT.Ln).then_inc(ln_ready, 1)

            def sum_out(c):
                act.wait_ge(w_used, NB * (c + 1))
                nc.scalar.copy(WTs[0:D + 1, c * CW:(c + 1) * CW], bank[7][0:D + 1, :]).then_inc(wsum_out, 1)

            logs(0)
            exp_logit(0)
            log_logit(0)
            for n in range(NT):
                act.wait_ge(ratio_ready, n + 1)
                if n >= 2:
                    act.wait_ge(diff_ready, n - 1)
                nc.scalar.activation(pt("tt", n), pt("lz", n), ACT.Exp, scale=0.5).then_inc(t_ready, 1)
                if n + 1 < NT:
                    logs(n + 1)
                act.wait_ge(clipped_ready, n + 1)
                ch.step(nc.scalar.activation(pt("cd", n), pt("tt", n), ACT.Ln, bias=1.0))
                nc.scalar.activation(pt("tt", n), pt("tt", n), ACT.Ln, bias=1.0, scale=-1.0).then_inc(artanh_ready, 1)
                if n + 1 < NT:
                    exp_logit(n + 1)
                act.wait_ge(logw_ready, n + 1)
                nc.scalar.activation(pt("dn", n), pt("dn", n), ACT.Exp).then_inc(wexp_ready, 1)
                if n + 1 < NT:
                    log_logit(n + 1)
                if n > NB and n % NB == 1:
                    sum_out(n // NB - 1)
            sum_out(NC - 1)
            rsqrt(5, V["a1"], V["rsq"])
            act.wait_ge(tanh_asked, 1)
            nc.scalar.activation(V["a3"], V["a2"], ACT.Tanh).then_inc(tanh_given, 1)
            nc.scalar.preload_act_table_set("natural_log_exp_and_others")
            rsqrt(6, V["a1"], V["rsq"])
            rsqrt(7, V["stat2"], V["rsq"])

            for q in range(NC):
                act.wait_ge(x3T_ready, q + 1)
                nc.scalar.copy(x3T[0:D, q * CW:(q + 1) * CW], bank[q % 2][0:D, :]).then_inc(x3T_out, 1)
            for q in range(NC):
                act.wait_ge(h_ready, q + 1)
                nc.scalar.activation(hT[:, q * CW:(q + 1) * CW], bank[2 + q % 2][:, :], ACT.Tanh,
                                     bias=C["hb"]).then_inc(h_out, 1)
            for q in range(2):
                act.wait_ge(xb_ready, q + 1)
                nc.scalar.copy(xbs[:, 8 * q:8 * q + 8, 0, :], bank[q][:, :].rearrange("p (b d) -> p b d", b=8)).then_inc(xb_hi, 1)
            nc.scalar.preload_act_table_set("natural_log_exp_and_others")
            for i in range(NB):
                for half in range(2):
                    act.wait_ge(r4_hi, 2 * i + half + 1)
                    nc.scalar.copy(RT[:, i % 2, 0, half * 8:half * 8 + 8, :].rearrange("p k i -> p (k i)"),
                                   bank16[4 + half]).then_inc(r4_hi_out, 1)
            rsqrt(8, V["stat2"], V["rsq"])

        @block.vector
        def _(dve):
            ch = Chain(dve, dve_chain)
            v = nc.vector
            asked = [0]

            def rsqrt(val, to):
                ch.settle()
                v.engine_nop().then_inc(rsq_asked, 1)
                asked[0] += 1
                dve.wait_ge(rsq_given, asked[0])
                e = V["rsq"]
                ch.step(v.tensor_tensor(V["newt"], e, e, ALU.mult))
                ch.step(v.tensor_tensor(V["newt"], V["newt"], val, ALU.mult))
                ch.step(v.tensor_scalar(V["newt"], V["newt"], -0.5, 1.5, ALU.mult, ALU.add))
                ch.step(v.tensor_tensor(to, e, V["newt"], ALU.mult))

            def rows_sum(to, src3):
                ch.step(v.tensor_reduce(to, src3, AX.X, ALU.add))

            def layer_norm(t, dst):
                rows_sum(V["stat"], t)
                ch.step(v.tensor_scalar(V["stat"], V["stat"], 1.0 / D, None, ALU.mult))
                ch.step(v.tensor_tensor(dst, t, over_d(V["stat"]), ALU.subtract))
                ch.step(v.tensor_tensor(nat_t, dst, dst, ALU.mult))
                rows_sum(V["stat2"], nat_t)
                ch.step(v.tensor_scalar(V["stat2"], V["stat2"], 1.0 / D, EPS_LN, ALU.mult, ALU.add))
                rsqrt(V["stat2"], V["stat"])
                return v.tensor_tensor(dst, dst, over_d(V["stat"]), ALU.mult)

            dve.wait_ge(theta_given, 1)
            ch.step(v.tensor_scalar(C01, C01, 1.0, None, ALU.add))
            ch.step(v.reciprocal(C01, C01))
            ch.link(v.tensor_scalar(C["t1s"], C["e1"], 1.0 / (R_SCALE * R_SCALE), None, ALU.mult))
            v.tensor_scalar(C["t0s"], C["e0"], 1.0 / R_SCALE, None, ALU.mult).then_inc(theta_ready, 1)
            dve.wait_ge(x_loaded, 16)
            ch.link(v.tensor_copy(x_hl[:, :, 0:D], nat_x[:, :, :]))
            ch.settle()
            ch.link(v.tensor_tensor(x_hl[:, :, D:2 * D], nat_x[:, :, :], x_hl[:, :, 0:D], ALU.subtract))
            ch.link(v.tensor_copy(x_hh[:, :, 0:D], x_hl[:, :, 0:D]))
            ch.link(v.tensor_copy(x_hh[:, :, D:2 * D], x_hl[:, :, 0:D]))
            ch.settle()
            v.engine_nop().then_inc(x_split, 1)
            dve.wait_ge(tr_ready, 6)
            def low(b):
                dve.wait_ge(scale_ready, b + 1)
                dve.wait_ge(hi_ready, b + 1)
                v.scalar_tensor_tensor(Rlo[:, b, :], load[:, b % NS, :], V["rs"][:, b:b + 1], Rhi[:, b, :],
                                       ALU.mult, ALU.subtract).then_inc(lo_ready, 1)

            for b in range(NB):
                dve.wait_ge(rowsum_ready, b + 1)
                ch.step(v.reciprocal(V["rd"][:, b:b + 1], V["d"][:, b:b + 1]))
                v.tensor_scalar(V["rs"][:, b:b + 1], V["rd"][:, b:b + 1], R_SCALE, None, ALU.mult).then_inc(scale_ready, 1)
                if b:
                    low(b - 1)
                dve.wait_ge(adj_loaded[b % NS], 16 * (b // NS + 1))
                for c in range(NC):
                    g = NC * b + c
                    dve.wait_ge(g_ready, g + 1)
                    v.tensor_tensor_reduce(w_pair[2 + g % 4], load[:, b % NS, c * CW:(c + 1) * CW], bank[4 + g % 4][:, :],
                                           1.0, 0.0, ALU.mult, ALU.add, outer4[:, b, c:c + 1]).then_inc(g_used, 1)
            low(NB - 1)
            rsqrt(V["d"], V["dinv"])
            v.tensor_tensor(V["sqd"], V["d"], V["dinv"], ALU.mult).then_inc(vec_ready, 1)
            dve.wait_ge(g_used, NC * NB)
            rows_sum(V["outer"], outer4[:, :, :])

            def fold(m, c):
                vc = stage[:, 1 - m % 2, c * CW:(c + 1) * CW]
                dve.wait_ge(rr_ready, m + 1)
                dve.wait_ge(s_ready, NC * m + c + 1)
                v.scalar_tensor_tensor(vc, bank[c][:, :], C["t1s"], vc, ALU.mult, ALU.add).then_inc(s_used, 1)

            def scale(m, c):
                vc = stage[:, 1 - m % 2, c * CW:(c + 1) * CW]
                dve.wait_ge(s_used, NC * m + c + 1)
                ch.link(v.tensor_tensor(vc, vc, vecB[:, c * CW:(c + 1) * CW], ALU.mult))

            def times_r(k, to):
                dve.wait_ge(bc_out, NC * (k + 1))
                for g in range(NC * NB * k, NC * NB * (k + 1)):
                    b, c = g // NC % NB, g % NC
                    dve.wait_ge(mv_ready, g + 1)
                    v.tensor_tensor_reduce(w_pair[2 + g % 4], bank[4 + g % 2][:, :], vecB[:, c * CW:(c + 1) * CW],
                                           1.0 / R_SCALE, 0.0, ALU.mult, ALU.add, outer4[:, b, c:c + 1]).then_inc(mv_used, 1)
                dve.wait_ge(mv_used, NC * NB * (k + 1))
                rows_sum(to, outer4[:, :, :])

            for c in range(NC):
                fold(0, c)
            times_r(0, V["u1"])
            v.engine_nop().then_inc(vec_ready, 1)
            for c in range(NC):
                fold(1, c)
            times_r(1, V["v2"])
            ch.step(v.tensor_scalar(V["a1"], V["u1"], C["e0"], None, ALU.mult))
            ch.step(v.scalar_tensor_tensor(V["a1"], V["v2"], C["e1"], V["a1"], ALU.mult, ALU.add))
            ch.step(v.tensor_tensor(V["a1"], V["a1"], V["sqd"], ALU.mult))
            ch.step(v.tensor_scalar(V["d2"], V["a1"], 1.0, None, ALU.add))
            rsqrt(V["d2"], V["dinv2"])
            v.tensor_tensor(V["cvec"], V["dinv"], V["dinv2"], ALU.mult).then_inc(vec_ready, 1)
            ch.link(v.tensor_tensor(V["rowfac"], V["sqd"], V["dinv2"], ALU.mult))

            ch.step(v.tensor_scalar(V["outer"], V["outer"], -0.01, None, ALU.mult))
            ch.step(v.tensor_scalar(nat_y[:, :, :], nat_x[:, :, :], -0.1, 1.0, ALU.mult, ALU.add))
            ch.step(v.tensor_tensor(nat_y[:, :, :], nat_y[:, :, :], over_d(V["outer"]), ALU.add))
            ch.step(v.tensor_tensor(nat_y[:, :, :], nat_y[:, :, :], nat_x[:, :, :], ALU.add))
            layer_norm(nat_y[:, :, :], nat_y[:, :, :]).then_inc(x1_ready, 1)

            def weighted(m):
                s = m % 2
                dve.wait_ge(gathered[s], 16 * TOP * (m // 2 + 1))
                if m >= 2:
                    dve.wait_ge(yT_ready, m - 1)
                ch.step(v.tensor_scalar(y_sb[:, s, :], gath[:, s, 0, :], wts[:, s, 0:1], None, ALU.mult))
                for t in range(1, TOP):
                    ins = v.scalar_tensor_tensor(y_sb[:, s, :], gath[:, s, t, :], wts[:, s, t:t + 1], y_sb[:, s, :],
                                                 ALU.mult, ALU.add)
                    if t < TOP - 1:
                        ch.step(ins)
                    else:
                        ins.then_inc(y_ready, 1)

            def residual(m):
                dve.wait_ge(yw_ready, m + 1)
                ch.step(v.tensor_tensor(nat_x[:, m, :], bank[7][:, 0:D], b1B[:, :], ALU.add))
                v.tensor_tensor(nat_x[:, m, :], nat_x[:, m, :], nat_y[:, m, :], ALU.add).then_inc(z_ready, 1)

            ch.settle()
            dve.wait_ge(x1_ready, 1)
            dve.wait_ge(bc_out, 3 * NC)
            dve.wait_ge(small_loaded, 16 * NSMALL)
            for m in range(NB):
                for c in range(NC):
                    if m >= 2:
                        fold(m, c)
                    scale(m, c)
                if m >= 2:
                    residual(m - 2)
                ch.settle()
                s = m % 2
                ch.step(v.max(vals[:, s, :], stage[:, 1 - s, :]))
                if m >= 2:
                    dve.wait_ge(gathered[s], 16 * TOP * (m // 2))
                v.max_index(idx[:, s, :], vals[:, s, :], stage[:, 1 - s, :]).then_inc(top_ready, 1)
                if m >= 1:
                    weighted(m - 1)
                ch.step(v.tensor_scalar(wts[:, s, :], vals[:, s, 0:TOP], V["rowfac"][:, m:m + 1], None, ALU.mult))
            weighted(NB - 1)
            residual(NB - 2)
            residual(NB - 1)
            dve.wait_ge(z_ready, NB)
            ch.step(layer_norm(nat_x[:, :, :], x2))

            ch.link(v.tensor_tensor(nat_t, x2, x2, ALU.mult))
            ch.step(v.reciprocal(C["rr"], C["r"]))
            rows_sum(V["n2"], nat_t)
            ch.link(v.tensor_tensor(C["c"], C["rr"], C["rr"], ALU.mult))
            ch.step(v.tensor_scalar(C["nr"], C["rr"], -1.0, None, ALU.mult))
            ch.step(v.tensor_tensor(C["sqc"], C["rr"], C["nr"], ALU.max))
            ch.link(v.reciprocal(C["rsqc"], C["sqc"]))
            ch.link(v.tensor_scalar(C["c2"], C["c"], 2.0, None, ALU.mult))
            ch.link(v.tensor_scalar(C["nc2"], C["c"], -2.0, None, ALU.mult))
            ch.link(v.tensor_scalar(C["cmin"], C["c"], MIN_NORM, None, ALU.mult))
            ch.link(v.tensor_scalar(V["X"], V["n2"], C["c"], None, ALU.mult))
            ch.step(v.tensor_scalar(V["pn"], V["n2"], MIN_NORM, None, ALU.max))
            ch.link(v.tensor_scalar(C["mxn"], C["rsqc"], MAX_NORM, None, ALU.mult))
            ch.link(v.tensor_scalar(V["om"], V["X"], -1.0, 1.0, ALU.mult, ALU.add))
            ch.link(v.tensor_scalar(xaug[:, :, D], V["X"], 1.0, None, ALU.add))
            rsqrt(V["pn"], V["a1"])
            ch.step(v.tensor_tensor(V["a1"], V["a1"], V["pn"], ALU.mult))
            ch.step(v.tensor_scalar(V["a1"], V["a1"], C["sqc"], None, ALU.mult))
            v.tensor_scalar(V["tcl"], V["a1"], T_MAX, None, ALU.min).then_inc(art_asked, 1)
            ch.step(v.reciprocal(V["a2"], V["a1"]))

            dve.wait_ge(art_given, 1)
            ch.step(v.tensor_tensor(V["q"], V["lnp"], V["lnm"], ALU.subtract))
            ch.step(v.tensor_tensor(V["q"], V["q"], V["a2"], ALU.mult))
            ch.step(v.tensor_scalar(V["q"], V["q"], 0.5, None, ALU.mult))
            for k, side in enumerate(["left", "right"]):
                ch.step(v.tensor_tensor(nat_t, x2, wattB[:, k, :].unsqueeze(1).to_broadcast([P, NB, D]), ALU.mult))
                rows_sum(V[side], nat_t)
                ch.step(v.tensor_tensor(V[side], V[side], V["q"], ALU.mult))
            ch.step(v.tensor_scalar(V["right"], V["right"], C["batt"], None, ALU.add))

            def parts(t, vec, at):
                ch.settle()
                rest = vec
                for cols_of in at:
                    for col in cols_of:
                        ch.link(v.tensor_copy(t[:, :, col], rest))
                    if cols_of is not at[-1]:
                        ch.settle()
                        ch.step(v.tensor_tensor(V["rest"], rest, t[:, :, cols_of[0]], ALU.subtract))
                        rest = V["rest"]

            def ones_in(t, lo, hi):
                ch.link(v.memset(t[:, :, lo:hi], 1.0))

            def given():
                ch.settle()
                v.engine_nop().then_inc(nat_ready, 1)

            ch.step(v.tensor_scalar(V["cf"], V["n2"], -0.5, None, ALU.mult))
            h, low_ = natL
            ch.link(v.tensor_copy(h[:, :, 0:D], x2))
            ch.link(v.memset(h[:, :, E1:P], 0.0))
            parts(h, V["cf"], [[E0], [E0 + 1], [E0 + 2]])
            ones_in(h, E0 + 3, E1)
            given()
            ch.link(v.tensor_tensor(low_[:, :, 0:D], x2, h[:, :, 0:D], ALU.subtract))
            ch.link(v.memset(low_[:, :, E1:P], 0.0))
            parts(low_, V["cf"], [[E0 + 3], [E0 + 4], [E0 + 5]])
            ones_in(low_, E0, E0 + 3)
            given()
            w = natW[0]
            dve.wait_ge(aug_ready, 2)
            ch.step(v.memset(w[:, :, 0:D], 0.0))
            parts(w, V["om"], [[0, 1, 3], [2, 5], [4]])
            parts(w, V["right"], [[LROW], [LROW + 1], [LROW + 2]])
            ones_in(w, LROW + 3, LROW + 6)
            given()
            w = natW[1]
            dve.wait_ge(aug_ready, 4)
            ch.step(v.memset(w[:, :, 0:D], 0.0))
            parts(w, V["om"], [[0, 2, 4], [1, 5], [3]])
            parts(w, V["left"], [[LROW + 3], [LROW + 4], [LROW + 5]])
            ones_in(w, LROW, LROW + 3)
            given()

            def distance(n):
                dve.wait_ge(dist_ready, n + 1)
                ch.link(v.tensor_scalar(pt("cd", n), bank[n % 2][:, :], C["nc2"], TINY, ALU.mult, ALU.max))

            def den(n):
                if n >= 4:
                    dve.wait_ge(w_used, n - 3)
                ch.link(v.tensor_tensor(pt("dn", n), pt("cd", n), bank[2 + n % 2][:, :], ALU.add))

            def den_guard(n):
                v.tensor_scalar(pt("dn", n), pt("dn", n), MIN_NORM, None, ALU.max).then_inc(dist_used, 1)

            def weights(n):
                dve.wait_ge(diff_ready, n + 1)
                dve.wait_ge(at_ready, n + 1)
                v.tensor_tensor(pt("dn", n), pt("dn", n), bank[6][:, :], ALU.mult).then_inc(g3_ready, 1)

            dve.wait_ge(art_given, 1)
            dve.wait_ge(aug_ready, 8)
            for n in range(2):
                distance(n)
                ch.settle()
                den(n)
                ch.settle()
                den_guard(n)
            for n in range(NT):
                cd, dn, lz, tt = (pt(k, n) for k in ("cd", "dn", "lz", "tt"))
                dve.wait_ge(ln_ready, n + 1)
                ch.step(v.tensor_tensor(lz, cd, dn, ALU.subtract))
                v.tensor_scalar(lz, lz, C["lncmin"], None, ALU.max).then_inc(ratio_ready, 1)
                if n + 2 < NT:
                    distance(n + 2)
                dve.wait_ge(ratio_ready, n + 1)
                ch.link(v.scalar_tensor_tensor(dn, lz, 0.5, dn, ALU.mult, ALU.add))
                dve.wait_ge(t_ready, n + 1)
                v.tensor_scalar(tt, tt, T_MAX, None, ALU.min).then_inc(clipped_ready, 1)
                ch.settle()
                dve.wait_ge(abs_ready, n + 1)
                v.scalar_tensor_tensor(dn, bank[4 + n % 2][:, :], 0.0, dn, ALU.min, ALU.subtract).then_inc(weight_ready, 1)
                if n + 2 < NT:
                    den(n + 2)
                if n:
                    weights(n - 1)
                if n + 2 < NT:
                    ch.settle()
                    den_guard(n + 2)
            weights(NT - 1)

            for q in range(NC):
                dve.wait_ge(wnat_ready, q + 1)
                v.tensor_copy(nat_u[:, BPC * q:BPC * q + BPC, :],
                              bank[q][:, :].rearrange("p (b d) -> p b d", b=BPC)[:, :, 0:D + 1]).then_inc(wnat_out, 1)
            dve.wait_ge(wnat_out, NC)
            wv, sv = nat_u[:, :, 0:D], nat_u[:, :, D]
            A, B = nat_x[:, :, :], nat_y[:, :, :]
            ch.step(v.tensor_tensor(nat_t, x2, wv, ALU.mult))
            rows_sum(V["inner"], nat_t)
            ch.link(v.scalar_tensor_tensor(V["cf"], V["inner"], C["c2"], sv, ALU.mult, ALU.subtract))
            ch.step(v.tensor_scalar(V["omc"], V["om"], MIN_NORM, None, ALU.max))
            ch.step(v.tensor_tensor(V["kf"], V["omc"], V["d"], ALU.mult))
            ch.link(v.tensor_scalar(V["kf"], V["kf"], 0.5 / R_SCALE, None, ALU.mult))
            ch.link(v.tensor_tensor(A, x2, over_d(V["cf"]), ALU.mult))
            ch.step(v.tensor_tensor(B, wv, over_d(V["om"]), ALU.mult))
            ch.step(v.tensor_tensor(A, A, B, ALU.add))
            ch.step(v.tensor_tensor(A, A, over_d(V["kf"]), ALU.mult))
            ch.step(v.tensor_tensor(nat_t, A, A, ALU.mult))
            rows_sum(V["a1"], nat_t)
            ch.step(v.tensor_scalar(V["a1"], V["a1"], MIN_NORM, None, ALU.max))
            rsqrt(V["a1"], V["a4"])
            ch.link(v.reciprocal(V["a5"], V["omc"]))
            ch.step(v.tensor_tensor(V["a2"], V["a1"], V["a4"], ALU.mult))
            ch.step(v.tensor_tensor(V["a2"], V["a2"], V["a5"], ALU.mult))
            v.tensor_scalar(V["a2"], V["a2"], C["sqc"], None, ALU.mult).then_inc(tanh_asked, 1)
            dve.wait_ge(tanh_given, 1)
            ch.step(v.tensor_tensor(V["a3"], V["a3"], V["a4"], ALU.mult))
            ch.step(v.tensor_scalar(V["a3"], V["a3"], C["rsqc"], None, ALU.mult))
            ch.step(v.tensor_tensor(B, A, over_d(V["a3"]), ALU.mult))
            ch.step(v.tensor_tensor(nat_t, B, B, ALU.mult))
            rows_sum(V["a1"], nat_t)
            ch.step(v.tensor_tensor(nat_t, B, x2, ALU.mult))
            rows_sum(V["a2"], nat_t)
            ch.link(v.tensor_scalar(V["a3"], V["a1"], C["c"], None, ALU.mult))
            ch.step(v.tensor_scalar(V["a2"], V["a2"], C["c2"], 1.0, ALU.mult, ALU.add))
            ch.link(v.tensor_tensor(V["a4"], V["a2"], V["a3"], ALU.add))
            ch.step(v.tensor_tensor(V["a5"], V["X"], V["a3"], ALU.mult))
            ch.step(v.tensor_tensor(V["a5"], V["a5"], V["a2"], ALU.add))
            ch.step(v.tensor_scalar(V["a5"], V["a5"], MIN_NORM, None, ALU.max))
            ch.step(v.reciprocal(V["a6"], V["a5"]))
            ch.link(v.tensor_tensor(V["a4"], V["a4"], V["a6"], ALU.mult))
            ch.step(v.tensor_tensor(V["a5"], V["om"], V["a6"], ALU.mult))
            ch.link(v.tensor_tensor(A, x2, over_d(V["a4"]), ALU.mult))
            ch.step(v.tensor_tensor(B, B, over_d(V["a5"]), ALU.mult))
            ch.step(v.tensor_tensor(A, A, B, ALU.add))
            ch.step(v.tensor_tensor(nat_t, A, A, ALU.mult))
            rows_sum(V["a1"], nat_t)
            ch.step(v.tensor_scalar(V["a1"], V["a1"], MIN_NORM, None, ALU.max))
            rsqrt(V["a1"], V["a2"])
            ch.step(v.tensor_scalar(V["a2"], V["a2"], C["mxn"], 1.0, ALU.mult, ALU.min))
            ch.step(v.tensor_tensor(A, A, over_d(V["a2"]), ALU.mult))
            ch.step(v.tensor_tensor(A, A, x2, ALU.add))
            layer_norm(A, nat_y[:, :, :]).then_inc(x3_ready, 1)

            ch.step(v.tensor_tensor(C["hb"], C["w1t"], C["tl3"], ALU.mult))
            ch.link(v.tensor_tensor(C["hb"], C["hb"], C["b1c"], ALU.add))
            ch.step(v.tensor_scalar(V["dsc"], V["d"], 1.0 / R_SCALE, None, ALU.mult))
            v.engine_nop().then_inc(x3_ready, 1)
            for q in range(2):
                bl = slice(8 * q, 8 * q + 8)
                dve.wait_ge(xb_hi, q + 1)
                ch.step(v.tensor_copy(nat_x[:, bl, :], bank[q][:, :].rearrange("p (b d) -> p b d", b=8)))
                v.tensor_tensor(xbs[:, bl, 1, :], nat_x[:, bl, :], xbs[:, bl, 0, :], ALU.subtract).then_inc(xb_split, 1)
            ch.settle()
            ch.link(v.tensor_tensor(nat_t, nat_x[:, :, :], over_d(V["d"]), ALU.mult))
            for q in range(2):
                bl = slice(8 * q, 8 * q + 8)
                dve.wait_ge(u_ready, q + 1)
                ch.link(v.tensor_tensor(base[:, bl, :], bank[2 + q][:, :].rearrange("p (b d) -> p b d", b=8),
                                        b2B[:, :].unsqueeze(1).to_broadcast([P, 8, D]), ALU.add))
            ch.settle()
            ch.step(v.tensor_tensor(base, base, nat_t, ALU.subtract))

            def low_out(i):
                for half in range(2):
                    dve.wait_ge(r4_lo, 2 * i + half + 1)
                    v.tensor_copy(RT[:, i % 2, 1, half * 8:half * 8 + 8, :].rearrange("p k i -> p (k i)"),
                                  bank16[half]).then_inc(r4_lo_out, 1)

            low_out(0)
            for i in range(NB):
                if i + 1 < NB:
                    low_out(i + 1)
                dve.wait_ge(ax_ready, i + 1)
                o = bank[6 + i % 2]
                ch.step(v.scalar_tensor_tensor(base[:, i, :], o[:, D:2 * D], V["dsc"][:, i:i + 1], base[:, i, :],
                                               ALU.mult, ALU.add))
                v.scalar_tensor_tensor(base[:, i, :], o[:, 0:D], V["dsc"][:, i:i + 1], base[:, i, :],
                                       ALU.mult, ALU.add).then_inc(ax_used, 1)
            dve.wait_ge(ax_used, NB)
            ch.step(v.tensor_tensor(base, base, nat_y[:, :, :], ALU.add))
            layer_norm(base, nat_y[:, :, :]).then_inc(o_ready, 1)

        @block.tensor
        def _(pe):
            mm = nc.tensor.matmul

            def spread(k):
                for n in range(NC * k, NC * k + NC):
                    pe.wait_ge(diag_ready, BPC * (n + 1))
                    if n >= 2:
                        pe.wait_ge(bc_out, n - 1)
                    mm(bank[6 + n % 2][:, :], ones[:, :], w_pair[n % 2], start=True, stop=True).then_inc(bc_ready, 1)

            def turn(m):
                if m == 2 or m == 3:
                    pe.wait_ge(mv_used, NC * NB * (m - 1))
                for g in range(4 * m, 4 * m + 4):
                    part, half = (Rhi, Rlo)[(g % 4) // 2], g % 2
                    if g >= 2:
                        pe.wait_ge(rt_out, g - 1)
                    for k in range(8):
                        ins = nc.tensor.transpose(bank16[4 + g % 2][:, k * P:(k + 1) * P],
                                                  part[:, m, (8 * half + k) * P:(8 * half + k + 1) * P], ident[:, :])
                    ins.then_inc(rt_ready, 1)

            def square(m, c):
                if c == 0:
                    pe.wait_ge(rt_out, 4 * (m + 1))
                if m:
                    pe.wait_ge(s_used, NC * (m - 1) + c + 1)
                cs = slice(c * CW, (c + 1) * CW)
                for k in range(NB):
                    hi, lo = RT[:, m % 2, 0, k, :], RT[:, m % 2, 1, k, :]
                    mm(bank[c][:, :], hi, Rhi[:, k, cs], start=(k == 0), stop=False)
                    mm(bank[c][:, :], hi, Rlo[:, k, cs], start=False, stop=False)
                    ins = mm(bank[c][:, :], lo, Rhi[:, k, cs], start=False, stop=(k == NB - 1))
                ins.then_inc(s_ready, 1)

            def turn_y(m):
                pe.wait_ge(y_ready, m + 1)
                if m >= 1:
                    pe.wait_ge(yT_out, m)
                nc.tensor.transpose(bank[6][0:D, 0:P], y_sb[:, m % 2, :], identf[:, :]).then_inc(yT_ready, 1)

            def y_w(m):
                pe.wait_ge(yT_out, m + 1)
                if m >= 1:
                    pe.wait_ge(z_ready, m)
                mm(bank[7][:, 0:D], yT[:, m % 2, :], wlT[:, :], start=True, stop=True).then_inc(yw_ready, 1)

            pe.wait_ge(consts_ready, 3)
            pe.wait_ge(x_loaded, 16)
            pe.wait_ge(x_split, 1)
            for n in range(6):
                kind, half = n // 2, n % 2
                src = (x_hl[:, :, :], x_hh[:, :, :], x_hl[:, :, D:2 * D])[kind]
                if n >= 2:
                    pe.wait_ge(tr_out, n - 1)
                for k in range(8):
                    ins = nc.tensor.transpose(bank16[n % 2][0:src.shape[2], k * P:(k + 1) * P], src[:, 8 * half + k, :],
                                              ident[:, :])
                ins.then_inc(tr_ready, 1)
            pe.wait_ge(tr_out, 6)
            def square_step(m, k, chunks):
                pe.wait_ge(rt_out, 4 * (m + 1))
                for c in chunks:
                    if k == 0 and m:
                        pe.wait_ge(s_used, NC * (m - 1) + c + 1)
                    hi, lo = RT[:, m % 2, 0, k, :], RT[:, m % 2, 1, k, :]
                    cs = slice(c * CW, (c + 1) * CW)
                    mm(bank[c][:, :], hi, Rhi[:, k, cs], start=(k == 0), stop=False)
                    mm(bank[c][:, :], hi, Rlo[:, k, cs], start=False, stop=False)
                    ins = mm(bank[c][:, :], lo, Rhi[:, k, cs], start=False, stop=(k == NB - 1))
                    if k == NB - 1:
                        ins.then_inc(s_ready, 1)

            for g in range(NC * NB):
                b, c = g // NC, g % NC
                if g >= 4:
                    pe.wait_ge(g_used, g - 3)
                if g == 2 * NC:
                    pe.wait_ge(g_used, 2 * NC)
                    pe.wait_ge(lo_ready, 1)
                    turn(0)
                    pe.wait_ge(rt_out, 4)
                bs, cs = slice(b * P, (b + 1) * P), slice(c * CW, (c + 1) * CW)
                mm(bank[4 + g % 4][:, :], xT[:, 0, bs], xT[:, 1, cs], start=True, stop=False)
                mm(bank[4 + g % 4][:, :], xT[0:D, 0, bs], xT_low[:, cs], start=False, stop=True).then_inc(g_ready, 1)
                if c == NC - 1 and b >= 2:
                    pe.wait_ge(lo_ready, b - 1)
                    square_step(0, b - 2, range(NC))
            for k in (NB - 2, NB - 1):
                pe.wait_ge(lo_ready, k + 1)
                square_step(0, k, range(NC))
            pe.wait_ge(g_used, NC * NB)
            spread(0)
            pe.wait_ge(small_loaded, 16 * NSMALL)
            pe.wait_ge(bc_out, NC)
            nc.tensor.transpose(bank[6][0:D, 0:D], wl_nat[:, :], identf[0:D, 0:D])
            nc.tensor.transpose(bank[6][0:D, D:2 * D], bl_nat[:, :], identf[0:D, 0:D]).then_inc(wT_ready, 1)
            pe.wait_ge(wT_out, 2)
            turn(1)
            for k in range(2):
                for g in range(NC * NB * k, NC * NB * (k + 1)):
                    b, c = g // NC % NB, g % NC
                    if g >= 2:
                        pe.wait_ge(mv_used, g - 1)
                    if g < 2:
                        pe.wait_ge(rt_out, 8)
                    cs = slice(c * CW, (c + 1) * CW)
                    mm(bank[4 + g % 2][:, :], ident[:, :], Rhi[:, b, cs], start=True, stop=False)
                    mm(bank[4 + g % 2][:, :], ident[:, :], Rlo[:, b, cs], start=False, stop=True).then_inc(mv_ready, 1)
                    square_step(k + 1, b, [c])
                if k == 0:
                    spread(1)
                    turn(2)
                    pe.wait_ge(rt_out, 12)
                else:
                    spread(2)
                    turn(3)
            for m in range(3, NB):
                square(m, 0)
                if m == 3:
                    turn_y(0)
                    y_w(0)
                square(m, 1)
                turn_y(m - 2)
                square(m, 2)
                y_w(m - 2)
                if m + 1 < NB:
                    turn(m + 1)
                square(m, 3)
            for m in (NB - 2, NB - 1):
                turn_y(m)
                y_w(m)

            def aug(kind):
                rows = P if kind < 2 else D
                pe.wait_ge(nat_ready, kind + 1)
                for half in range(2):
                    n = 2 * kind + half
                    if n >= 2:
                        pe.wait_ge(aug_out, n - 1)
                    for k in range(8):
                        ins = nc.tensor.transpose(bank16[n % 2][0:rows, k * P:(k + 1) * P],
                                                  natL[kind % 2][:, 8 * half + k, 0:rows], ident[:, :])
                    ins.then_inc(aug_ready, 1)

            for kind in range(4):
                aug(kind)
            pe.wait_ge(aug_out, 8)
            xh, xl = AUG[:, 0, :], AUG[:, 1, :]
            node_l, node_r = AUG[:, 2, :].bitcast(BF16), AUG[:, 3, :].bitcast(BF16)

            def pair_distance(n):
                c, j, s = n // NB, n % NB, n % 2
                js, cs = slice(j * P, (j + 1) * P), slice(c * CW, (c + 1) * CW)
                if n >= 2:
                    pe.wait_ge(dist_used, n - 1)
                mm(bank[s][:, :], xh[0:D, js], xh[0:D, cs], start=True, stop=False)
                mm(bank[s][:, :], xl[0:D, js], xh[0:D, cs], start=False, stop=False)
                mm(bank[s][:, :], xh[0:E1, js], xl[0:E1, cs], start=False, stop=True)
                mm(bank[2 + s][:, :], node_l[0:6, js], node_r[0:6, cs], start=True, stop=True).then_inc(dist_ready, 1)

            def pair_logit(n):
                c, j, s = n // NB, n % NB, n % 2
                js, cs = slice(j * P, (j + 1) * P), slice(c * CW, (c + 1) * CW)
                if n >= 2:
                    pe.wait_ge(weight_ready, n - 1)
                ls = slice(LROW, LROW + 6)
                mm(bank[4 + s][:, :], node_l[ls, js], node_r[ls, cs], start=True, stop=True).then_inc(pl_ready, 1)

            def adjacency(n):
                c, j = n // NB, n % NB
                if n >= 1:
                    pe.wait_ge(g3_ready, n)
                for k in range(BPC):
                    i = BPC * c + k
                    o = bank[6][:, k * P:(k + 1) * P]
                    mm(o, Rhi[:, i, j * P:(j + 1) * P], ident[:, :], start=True, stop=False)
                    ins = mm(o, Rlo[:, i, j * P:(j + 1) * P], ident[:, :], start=False, stop=True)
                ins.then_inc(at_ready, 1)

            def weighted_sum(n):
                c, j = n // NB, n % NB
                pe.wait_ge(g3_ready, n + 1)
                if j == 0 and c:
                    pe.wait_ge(wsum_out, c)
                mm(bank[7][0:D + 1, :], xaug[:, j, :], pt("dn", n), start=(j == 0), stop=(j == NB - 1)).then_inc(w_used, 1)

            pair_distance(0)
            pair_logit(0)
            pair_distance(1)
            for n in range(NT):
                if n + 2 < NT:
                    pair_distance(n + 2)
                if n + 1 < NT:
                    pair_logit(n + 1)
                if n >= 2:
                    weighted_sum(n - 2)
                if n:
                    adjacency(n - 1)
            weighted_sum(NT - 2)
            adjacency(NT - 1)
            weighted_sum(NT - 1)
            pe.wait_ge(wsum_out, NC)
            for q in range(NC):
                for j in range(BPC):
                    b = BPC * q + j
                    ins = nc.tensor.transpose(bank[q][:, j * P:j * P + D + 1], WTs[0:D + 1, b * P:(b + 1) * P],
                                              identf[0:D + 1, 0:D + 1])
                ins.then_inc(wnat_ready, 1)

            pe.wait_ge(x3_ready, 2)
            for q in range(NC):
                if q >= 2:
                    pe.wait_ge(x3T_out, q - 1)
                for j in range(BPC):
                    ins = nc.tensor.transpose(bank[q % 2][0:D, j * P:(j + 1) * P], nat_y[:, BPC * q + j, :], identf[:, :])
                ins.then_inc(x3T_ready, 1)
            pe.wait_ge(x3T_out, NC)
            for q in range(NC):
                if q >= 2:
                    pe.wait_ge(h_out, q - 1)
                mm(bank[2 + q % 2][:, :], w1_sb[:, :], x3T[0:D, q * CW:(q + 1) * CW], start=True, stop=True).then_inc(h_ready, 1)
            for q in range(2):
                for b in range(8):
                    i = 8 * q + b
                    ins = mm(bank[q][:, b * D:(b + 1) * D], x3T[0:D, i * P:(i + 1) * P], blT[:, :], start=True, stop=True)
                ins.then_inc(xb_ready, 1)
            pe.wait_ge(h_out, NC)
            for q in range(2):
                for b in range(8):
                    i = 8 * q + b
                    ins = mm(bank[2 + q][:, b * D:(b + 1) * D], hT[:, i * P:(i + 1) * P], w2_sb[:, :], start=True, stop=True)
                ins.then_inc(u_ready, 1)
            pe.wait_ge(xb_split, 2)

            def turn4(i):
                for half in range(2):
                    for part, bk, made, out_ in ((Rhi, 4, r4_hi, r4_hi_out), (Rlo, 0, r4_lo, r4_lo_out)):
                        if i:
                            pe.wait_ge(out_, 2 * (i - 1) + half + 1)
                        for k in range(8):
                            ins = nc.tensor.transpose(bank16[bk + half][:, k * P:(k + 1) * P],
                                                      part[:, i, (8 * half + k) * P:(8 * half + k + 1) * P], ident[:, :])
                        ins.then_inc(made, 1)

            turn4(0)
            for i in range(NB):
                if i + 1 < NB:
                    turn4(i + 1)
                pe.wait_ge(r4_hi_out, 2 * i + 2)
                pe.wait_ge(r4_lo_out, 2 * i + 2)
                if i >= 2:
                    pe.wait_ge(ax_used, i - 1)
                o = bank[6 + i % 2]
                for k in range(NB):
                    mm(o[:, 0:2 * D], RT[:, i % 2, 0, k, :], xbs[:, k, :, :].rearrange("p h d -> p (h d)"),
                       start=(k == 0), stop=False, skip_group_check=True)
                    ins = mm(o[:, 0:D], RT[:, i % 2, 1, k, :], xbs[:, k, 0, :], start=False, stop=(k == NB - 1),
                             skip_group_check=True)
                ins.then_inc(ax_ready, 1)


_INS = ["x", "adj", "L1_gnn_theta", "L1_gnn_W", "L1_gnn_b", "L2_gnn_r", "L2_gnn_w_att", "L2_gnn_b_att",
        "L3_gnn_t", "L3_gnn_B", "L3_gnn_W1", "L3_gnn_b1", "L3_gnn_W2", "L3_gnn_b2"]


def kernel(**inputs):
    import numpy as _np
    import concourse.bacc as _bacc
    from concourse import mybir as _mybir
    from concourse.bass_utils import run_bass_kernel_spmd as _run

    nc = _bacc.Bacc("TRN2", target_bir_lowering=False, num_devices=1)
    arrays, args = {}, []
    for name in _INS:
        a = _np.ascontiguousarray(inputs[name])
        arrays[f"in_{name}_dram"] = a
        args.append(nc.dram_tensor(f"in_{name}_dram", a.shape, _mybir.dt.from_np(a.dtype), kind="ExternalInput").ap())
    out = nc.dram_tensor("out_dram", (2048, 64), _mybir.dt.float32, kind="ExternalOutput").ap()
    build(nc, *args, out)
    res = _run(nc, [arrays], core_ids=[0])
    return res.results[0]["out_dram"]
```

```python
from contextlib import ExitStack

import concourse.bass as bass
from concourse import mybir

ALU = mybir.AluOpType
ACT = mybir.ActivationFunctionType
AX = mybir.AxisListType
F32 = mybir.dt.float32
F16 = mybir.dt.float16
BF16 = mybir.dt.bfloat16
U32 = mybir.dt.uint32

P = 128
EPS_LN = 1e-5
MIN_NORM = 1e-15
T_MAX = 1.0 - 1e-7
MAX_NORM = 1.0 - 0.004
R_SCALE = 4096.0
TINY = 2.0 ** -60


class Chain:

    def __init__(self, eng, sem):
        self.eng, self.sem, self.n = eng, sem, 0

    def link(self, ins):
        ins.then_inc(self.sem, 1)
        self.n += 1

    def settle(self, upto=None):
        self.eng.wait_ge(self.sem, self.n if upto is None else upto)

    def step(self, ins):
        self.link(ins)
        self.settle()


def build(nc, x, adj, theta, w_l1, b_l1, r, w_att, b_att, t_l3, b_l3, w1, b1, w2, b2, out):
    N, D = x.shape
    NB = N // P
    CW = 512
    NC = N // CW
    BPC = CW // P
    H = w1.shape[1]
    TOP = 4
    E0, E1 = D, D + 6
    LROW = 32

    ctx = ExitStack()
    with ctx:
        def sb(name, shape, dt=F32):
            return ctx.enter_context(nc.sbuf_tensor(name, shape, dt))

        def sem(name):
            return ctx.enter_context(nc.semaphore(name))

        Rhi = sb("Rhi", [P, NB, N], F16)
        Rlo = sb("Rlo", [P, NB, N], F16)
        scratch = sb("scratch", [P, 12288])
        stage = scratch[:, 0:2 * N].rearrange("p (s n) -> p s n", s=2)
        NS = 4
        load = [scratch[:, a:a + N] for a in (0, N, 2 * N, 4 * N)]
        vecB = scratch[:, 2 * N:3 * N]
        RT = scratch[:, 3 * N:5 * N].bitcast(F16).rearrange("p (s h k i) -> p s h k i", s=2, h=2, k=NB)
        xT = scratch[:, 5 * N:6 * N].bitcast(F16).rearrange("p (w n) -> p w n", w=2)
        pair_x = scratch[:, 3 * N:4 * N].bitcast(F16).rearrange("p (w n) -> p w n", w=2)
        pair_nodes = scratch[:, N:2 * N].bitcast(F16).rearrange("p (w n) -> p w n", w=2)
        WTs = scratch[:, 4 * N:5 * N]
        hT = scratch[:, N:2 * N]
        nat_t = scratch[:, 5 * N:5 * N + NB * D].rearrange("p (b d) -> p b d", b=NB)
        small = scratch[:, 5 * N + NB * D:6 * N]
        gath = small[:, 0:2 * TOP * D].rearrange("p (s t d) -> p s t d", s=2, t=TOP)
        y_sb = small[:, 512:512 + 2 * D].rearrange("p (s d) -> p s d", s=2)
        yT = small[0:D, 640:640 + 2 * P].rearrange("p (s d) -> p s d", s=2)
        x3T = scratch[:, 0:N]
        base = scratch[:, 2 * N:2 * N + NB * D].rearrange("p (b d) -> p b d", b=NB)
        xbs = scratch[:, 2 * N + NB * D:3 * N].bitcast(F16).rearrange("p (b h d) -> p b h d", b=NB, h=2)
        nat_x = sb("nat_x", [P, NB, D])
        nat_y = sb("nat_y", [P, NB, D])
        xaug = sb("xaug", [P, NB, D + 1])
        x2 = xaug[:, :, 0:D]
        xT_low = xaug[0:D, :, :].rearrange("p b d -> p (b d)")[:, 0:N // 2].bitcast(F16)
        work = sb("work", [P, 6, CW])
        w_pair = [work[:, i, :] for i in range(6)]
        aside = [w_pair[2:6], [scratch[:, 5 * N + i * CW:5 * N + (i + 1) * CW] for i in range(2)]
                 + [xaug[:, :, :].rearrange("p b d -> p (b d)")[:, i * CW:(i + 1) * CW] for i in range(2)]]
        products = [scratch[:, 5 * N + i * N // 2:5 * N + (i + 1) * N // 2] for i in range(2)]
        unread = xaug[:, :, :].rearrange("p b d -> p (b d)")[:, 0:N // 2].bitcast(BF16)
        nat_hi, nat_lo = (work[:, 2 * i:2 * i + 2, :].rearrange("p w n -> p (w n)").bitcast(F16)
                          .rearrange("p (b d) -> p b d", b=NB) for i in range(2))
        nat_left_bits, nat_right_bits = (work[:, 4 + i, :].bitcast(F16).rearrange("p (b d) -> p b d", b=NB) for i in range(2))
        nat_left, nat_right = (work[:, 4 + i, :].bitcast(BF16).rearrange("p (b d) -> p b d", b=NB) for i in range(2))
        identf = sb("identf", [P, P])
        ident = sb("ident", [P, P], F16)
        ones = sb("ones", [P, P])
        sm = sb("sm", [P, 46, NB])
        cols = sb("cols", [P, 24])
        outer4 = sb("outer4", [P, NB, NC])
        vals = sb("vals", [P, 2, 8])
        wts = sb("wts", [P, 2, TOP])
        idx = sb("idx", [P, 2, 8], U32)
        wl_nat = sb("wl_nat", [D, D])
        bl_nat = sb("bl_nat", [D, D])
        wlT = sb("wlT", [D, D])
        blT = sb("blT", [D, D])
        w1_sb = sb("w1_sb", [D, H])
        w2_sb = sb("w2_sb", [H, D])
        wattB = sb("wattB", [P, 2, D])
        b1B = sb("b1B", [P, D])
        b2B = sb("b2B", [P, D])
        parts = sb("parts", [P, 3, 4, NB], BF16)
        x1_dram = nc.dram_tensor("x1_scratch", [N, D], F32, kind="Internal").ap()
        psum = ctx.enter_context(nc.psum_tensor("psum", [P, 8 * CW], F32))
        rt_dram = nc.dram_tensor("rt_scratch", [NB, P, 2, N], F16, kind="Internal").ap()
        bank = [psum[:, i * CW:(i + 1) * CW] for i in range(8)]
        bank16 = [b[:, :].bitcast(F16) for b in bank]

        four = ["cf", "om", "right", "left"]
        names = four + [n + "_rest" for n in four] + [
            "d", "rd", "rs", "outer", "stat", "stat2", "rsq", "newt", "dinv", "sqd", "u1", "v2", "dinv2",
            "cvec", "rowfac", "n2", "X", "pn", "tcl", "lnp", "lnm", "q", "inner",
            "kf", "a1", "a2", "a3", "a4", "a5", "a6", "dsc", "omc", "reach", "okf", "uu",
            "ux", "f"]
        V = {n: sm[:, i, :] for i, n in enumerate(names)}
        cn = ["th0", "th1", "t0s", "t1s", "r", "rr", "c", "nc2", "batt", "tl3", "b1c", "w1t", "hb", "cmin", "lncmin", "sqc",
              "rsqc", "e0", "e1", "c2", "mxn", "nr"]
        C = {n: cols[:, i:i + 1] for i, n in enumerate(cn)}

        WIDE = 2 * CW
        wide = {a: scratch[:, a:a + WIDE] for a in (0, WIDE, 2 * N, 2 * N + WIDE, 5 * N, 5 * N + WIDE)}
        work_wide = [work[:, 2 * i:2 * i + 2, :].rearrange("p w n -> p (w n)") for i in range(3)]
        PT = {"cd": [wide[0], nat_x[:, :, :].rearrange("p b d -> p (b d)"), nat_y[:, :, :].rearrange("p b d -> p (b d)")],
              "dn": [wide[WIDE]] + work_wide,
              "sg": [wide[2 * N], wide[5 * N]], "lz": [wide[2 * N + WIDE]], "tt": [wide[5 * N + WIDE]]}

        def pt(name, n):
            return PT[name][n % len(PT[name])]

        dist_bank, om_bank, logit_bank = psum[:, 0:WIDE], psum[:, WIDE:2 * WIDE], psum[:, 2 * WIDE:3 * WIDE]

        i01 = cn.index("e0")
        C01 = cols[:, i01:i01 + 2]

        x_hl = work[:, 0:2, :].rearrange("p w n -> p (w n)").bitcast(F16).rearrange("p (b d) -> p b d", b=NB)
        x_hh = work[:, 2:4, :].rearrange("p w n -> p (w n)").bitcast(F16).rearrange("p (b d) -> p b d", b=NB)

        def over_d(v):
            return v.unsqueeze(2).to_broadcast([P, v.shape[1], D])

        consts_ready = sem("consts_ready")
        x_split = sem("x_split")
        x_loaded = sem("x_loaded")
        small_loaded = sem("small_loaded")
        adj_loaded = [sem(f"adj_loaded{i}") for i in range(NS)]
        dve_chain, act_chain, pool_chain = sem("dve_chain"), sem("act_chain"), sem("pool_chain")
        x_turned, xT_out = sem("x_turned"), sem("xT_out")
        gram_ready, gram_used = sem("gram_ready"), sem("gram_used")
        rowsum_ready, scale_ready, hi_ready, lo_ready = sem("rowsum_ready"), sem("scale_ready"), sem("hi_ready"), sem("lo_ready")
        pool_lo_ready = sem("pool_lo_ready")
        rsq_asked, rsq_given = sem("rsq_asked"), sem("rsq_given")
        theta_loaded, theta_given, theta_ready = sem("theta_loaded"), sem("theta_given"), sem("theta_ready")
        x1_ready, x1_stored = sem("x1_ready"), sem("x1_stored")
        diag_ready, spread_ready, vector_out = sem("diag_ready"), sem("spread_ready"), sem("vector_out")
        product_ready, dot_ready = sem("product_ready"), sem("dot_ready")
        r_turned, turned_copied = sem("r_turned"), sem("turned_copied")
        turned_stored = [sem(f"turned_stored{i}") for i in range(2)]
        turned_loaded = [sem(f"turned_loaded{i}") for i in range(NC)]
        square_ready, square_folded, set_aside = sem("square_ready"), sem("square_folded"), sem("set_aside")
        v_ready, top_ready = sem("v_ready"), sem("top_ready")
        gathered = [sem(f"gathered{i}") for i in range(2)]
        y_ready, yT_ready, yT_out, yw_ready, z_ready = (sem(n) for n in ["y_ready", "yT_ready", "yT_out", "yw_ready", "z_ready"])
        wT_ready, wT_out = sem("wT_ready"), sem("wT_out")
        abs_ready = sem("abs_ready")
        artanh_asked, artanh_given = sem("artanh_asked"), sem("artanh_given")
        node_terms_ready, operand_ready, operand_out = sem("node_terms_ready"), sem("operand_ready"), sem("operand_out")
        dist_ready, dist_read, den_ready, logits_ready = sem("dist_ready"), sem("dist_read"), sem("den_ready"), sem("logits_ready")
        logs_ready, siglog_ready, ratio_ready, root_ready = sem("logs_ready"), sem("siglog_ready"), sem("ratio_ready"), sem("root_ready")
        weight_ready, clipped_ready, logw_ready = sem("weight_ready"), sem("clipped_ready"), sem("logw_ready")
        artanh_ready, wexp_ready, artanh_sub, diff_ready = (sem(n) for n in ["artanh_ready", "wexp_ready", "artanh_sub", "diff_ready"])
        adjacency_ready, weight_done, sum_done, sum_copied = sem("adjacency_ready"), sem("weight_done"), sem("sum_done"), sem("sum_copied")
        sums_turned = sem("sums_turned")
        tanh_asked, tanh_given = sem("tanh_asked"), sem("tanh_given")
        x3_ready, x3T_ready, x3T_out = sem("x3_ready"), sem("x3T_ready"), sem("x3T_out")
        h_ready, h_out, xb_ready, xb_hi, xb_split = sem("h_ready"), sem("h_out"), sem("xb_ready"), sem("xb_hi"), sem("xb_split")
        mlp_ready, product_done, product_added = sem("mlp_ready"), sem("product_done"), sem("product_added")
        out_ready = sem("out_ready")
        out_stored = sem("out_stored")

        block = ctx.enter_context(nc.Block())
        NSMALL = 12

        def ys_of(m):
            return [m - 2] if m >= 6 else [2 * (m - 4), 2 * (m - 4) + 1]

        ALL, FIRST, LAST = slice(0, NB), slice(0, NB - 4), slice(NB - 4, NB)
        POOL_LOW = (1, 4, 7, 10, 13)

        def low_done(eng, b):
            n = sum(p <= b for p in POOL_LOW)
            eng.wait_ge(lo_ready, b + 1 - n)
            if n:
                eng.wait_ge(pool_lo_ready, n)

        DVE_BLOCKS = 10
        POOL_HALVES = 2 * (NB - DVE_BLOCKS)
        HALF = [slice(0, NB // 2), slice(NB // 2, NB)]
        NT = NC * NB
        NP = NT // 2
        NBP = NB // 2

        @block.sync
        def _(sp):
            sp.dma_start(nat_x[:, :, :], x.rearrange("(b p) d -> p b d", p=P)).then_inc(x_loaded, 16)
            for b in range(NB):
                if b == 1:
                    sp.dma_start(C["th0"], theta[0:1].partition_broadcast(P)).then_inc(theta_loaded, 16)
                    sp.dma_start(C["th1"], theta[1:2].partition_broadcast(P)).then_inc(theta_loaded, 16)
                if b == 3:
                    sp.dma_start(C["r"], r.partition_broadcast(P)).then_inc(small_loaded, 16)
                    sp.dma_start(C["batt"], b_att.partition_broadcast(P)).then_inc(small_loaded, 16)
                    sp.dma_start(C["tl3"], t_l3.partition_broadcast(P)).then_inc(small_loaded, 16)
                    sp.dma_start(C["b1c"], b1.unsqueeze(1)).then_inc(small_loaded, 16)
                    sp.dma_start(C["w1t"], w1[D:D + 1, :].rearrange("a h -> h a")).then_inc(small_loaded, 16)
                    sp.dma_start(wl_nat[:, :], w_l1).then_inc(small_loaded, 16)
                    sp.dma_start(bl_nat[:, :], b_l3).then_inc(small_loaded, 16)
                    sp.dma_start(w1_sb[:, :], w1[0:D, :]).then_inc(small_loaded, 16)
                    sp.dma_start(w2_sb[:, :], w2).then_inc(small_loaded, 16)
                    sp.dma_start(wattB[:, :, :].rearrange("p k d -> p (k d)"),
                                 w_att.rearrange("(d a) o -> d (a o)", a=1).rearrange("d a -> a d").squeeze(0).partition_broadcast(P)
                                 ).then_inc(small_loaded, 16)
                    sp.dma_start(b1B[:, :], b_l1.partition_broadcast(P)).then_inc(small_loaded, 16)
                    sp.dma_start(b2B[:, :], b2.partition_broadcast(P)).then_inc(small_loaded, 16)
                if b - NS in POOL_LOW:
                    sp.wait_ge(pool_lo_ready, POOL_LOW.index(b - NS) + 1)
                    sp.wait_ge(gram_used, NC * (b - NS + 1))
                elif b >= NS:
                    low_done(sp, b - NS)
                sp.dma_start(load[b % NS], adj[b * P:(b + 1) * P, :]).then_inc(adj_loaded[b % NS], 16)
            def store_turned(m):
                sp.wait_ge(turned_copied, 4 * (m + 1))
                sp.dma_start(rt_dram[m], RT[:, m % 2, :, :, :].rearrange("p h k i -> p h (k i)")).then_inc(turned_stored[m % 2], 16)

            for m in range(4):
                store_turned(m)
            sp.wait_ge(x1_ready, 1)
            sp.dma_start(x1_dram.rearrange("(b p) d -> p b d", p=P), nat_y[:, :, :]).then_inc(x1_stored, 16)
            for m in range(4, NB):
                store_turned(m)
            for s in range(2):
                sp.wait_ge(turned_stored[s], 16 * (NB // 2))
            for m in range(NB):
                if m % BPC == 0:
                    sp.wait_ge(adjacency_ready, NB * (m // BPC + 1))
                sp.dma_start(Rhi[:, m, :], rt_dram[m, :, 0, :]).then_inc(turned_loaded[m // BPC], 16)
                sp.dma_start(Rlo[:, m, :], rt_dram[m, :, 1, :]).then_inc(turned_loaded[m // BPC], 16)
            for q in range(2):
                sp.wait_ge(out_ready, q + 1)
                sp.dma_start(out.rearrange("(b p) d -> p b d", p=P)[:, HALF[q], :], nat_y[:, HALF[q], :]).then_inc(out_stored, 16)
            sp.wait_ge(out_stored, 32)
            sp.wait_ge(x1_stored, 16)

        @block.gpsimd
        def _(pool):
            ch = Chain(pool, pool_chain)
            ch.link(nc.gpsimd.memset(identf[:, :], 0.0))
            ch.link(nc.gpsimd.memset(ident[:, :], 0.0))
            nc.gpsimd.memset(ones[:, :], 1.0).then_inc(consts_ready, 1)
            ch.settle()
            for m in (identf, ident):
                nc.gpsimd.affine_select(out=m[:, :], in_=m[:, :], compare_op=ALU.not_equal, fill=1.0, base=0,
                                        pattern=[[-1, P]], channel_multiplier=1).then_inc(consts_ready, 1)

            pool.wait_ge(consts_ready, 3)

            scaled = work[:, 0:2, :].rearrange("p w n -> p (w n)")
            pool.wait_ge(x_turned, 6)
            for n, b in enumerate(POOL_LOW):
                pool.wait_ge(hi_ready, b + 1)
                pool.wait_ge(scale_ready, b + 1)
                for h in range(2):
                    hs = slice(h * N // 2, (h + 1) * N // 2)
                    ch.step(nc.gpsimd.tensor_tensor(scaled, load[b % NS][:, hs], V["rs"][:, b:b + 1].to_broadcast([P, N // 2]), ALU.mult))
                    ch.step(nc.gpsimd.tensor_tensor(Rlo[:, b, hs], scaled, Rhi[:, b, hs], ALU.subtract))
                pool.engine_nop().then_inc(pool_lo_ready, 1)

            def start_v(m):
                v = stage[:, 1 - m % 2, :]
                if m < 2:
                    low_done(pool, NB - 3)
                    pool.wait_ge(gram_used, NC * (NB - 2))
                else:
                    pool.wait_ge(top_ready, m - 1)
                ch.step(nc.gpsimd.tensor_tensor(v, Rhi[:, m, :], Rlo[:, m, :], ALU.add))
                ch.step(nc.gpsimd.tensor_tensor(v, v, C["t0s"].to_broadcast([P, N]), ALU.mult))
                d = v[:, m * P:(m + 1) * P]
                nc.gpsimd.tensor_tensor(d, d, identf[:, :], ALU.add).then_inc(v_ready, 1)

            pool.wait_ge(theta_ready, 1)
            for m in range(2):
                start_v(m)
            for k in range(2):
                pool.wait_ge(vector_out, NC * (k + 1))
                for n in range(POOL_HALVES):
                    b, h, u = DVE_BLOCKS + n // 2, n % 2, POOL_HALVES * k + n
                    hs = slice(h * N // 2, (h + 1) * N // 2)
                    if u >= 2:
                        pool.wait_ge(dot_ready, u - 1)
                    ch.step(nc.gpsimd.tensor_tensor(products[h], Rhi[:, b, hs], Rlo[:, b, hs], ALU.add))
                    nc.gpsimd.tensor_tensor(products[h], products[h], vecB[:, hs], ALU.mult).then_inc(product_ready, 1)
            pool.wait_ge(x1_stored, 16)
            for m in range(NB):
                pool.wait_ge(top_ready, m + 1)
                if m >= 2:
                    pool.wait_ge(y_ready, m - 1)
                for t in range(TOP):
                    nc.gpsimd.indirect_dma_start(gath[:, m % 2, t, :], None, x1_dram,
                                                 bass.IndirectOffsetOnAxis(idx[:, m % 2, t:t + 1], 0)).then_inc(gathered[m % 2], 16)
                if m + 2 < NB:
                    start_v(m + 2)

            for n in range(NP):
                dn, cd, tt = pt("dn", n), pt("cd", n), pt("tt", n)
                pool.wait_ge(weight_ready, n + 1)
                pool.wait_ge(siglog_ready, n + 1)
                nc.gpsimd.tensor_tensor(dn, dn, pt("sg", n), ALU.subtract).then_inc(logw_ready, 1)
                pool.wait_ge(artanh_ready, n + 1)
                nc.gpsimd.tensor_tensor(cd, cd, tt, ALU.subtract).then_inc(artanh_sub, 1)
                pool.wait_ge(artanh_sub, n + 1)
                pool.wait_ge(wexp_ready, n + 1)
                nc.gpsimd.tensor_tensor(dn, dn, cd, ALU.mult).then_inc(diff_ready, 1)

        @block.scalar
        def _(act):
            ch = Chain(act, act_chain)
            nc.scalar.preload_act_table_set("natural_log_exp_and_others")

            def rsqrt(k, v, e):
                act.wait_ge(rsq_asked, k + 1)
                ch.step(nc.scalar.activation(e, v, ACT.Ln))
                nc.scalar.activation(e, e, ACT.Exp, scale=-0.5).then_inc(rsq_given, 1)

            def spread_out(k):
                for n in range(NC * k, NC * k + NC):
                    act.wait_ge(spread_ready, n + 1)
                    q = n % NC
                    nc.scalar.copy(vecB[:, q * CW:(q + 1) * CW], bank[6 + n % 2][:, :]).then_inc(vector_out, 1)

            def turned_quarter_out(g):
                h, half = (g % 4) // 2, g % 2
                act.wait_ge(r_turned, g + 1)
                nc.scalar.copy(RT[:, g // 4 % 2, h, half * 8:half * 8 + 8, :].rearrange("p k i -> p (k i)"),
                               bank16[4 + g % 2]).then_inc(turned_copied, 1)

            def quarters_out(m, lo, hi):
                if lo == 0 and m >= 2:
                    act.wait_ge(turned_stored[m % 2], 16 * (m // 2))
                for g in range(4 * m + lo, 4 * m + hi):
                    turned_quarter_out(g)

            def dots(k, lo, hi):
                for n in range(lo, hi):
                    act.wait_ge(product_ready, POOL_HALVES * k + n + 1)
                    nc.scalar.activation(products[n % 2], products[n % 2], ACT.Copy, scale=1.0 / R_SCALE,
                                         accum_out=outer4[:, DVE_BLOCKS + n // 2, n % 2:n % 2 + 1]).then_inc(dot_ready, 1)

            def put_aside(m):
                for c in range(NC):
                    act.wait_ge(square_ready, NC * m + c + 1)
                    nc.scalar.copy(aside[m - 2][c], bank[c][:, :]).then_inc(set_aside, 1)

            def rowsum(b):
                act.wait_ge(adj_loaded[b % NS], 16 * (b // NS + 1))
                nc.scalar.activation(Rhi[:, b, :], load[b % NS], ACT.Copy,
                                     accum_out=V["d"][:, b:b + 1]).then_inc(rowsum_ready, 1)

            for b in range(NB):
                if b == 2:
                    act.wait_ge(theta_loaded, 32)
                    nc.scalar.activation(C01, cols[:, 0:2], ACT.Exp, scale=-1.0).then_inc(theta_given, 1)
                rowsum(b)
                act.wait_ge(scale_ready, b + 1)
                nc.scalar.activation(Rhi[:, b, :], load[b % NS], ACT.Copy,
                                     scale=V["rs"][:, b:b + 1]).then_inc(hi_ready, 1)
            low_done(act, NB - 1)
            quarters_out(1, 0, 2)
            rsqrt(0, V["d"], V["rsq"])
            spread_out(0)
            act.wait_ge(wT_ready, 1)
            nc.scalar.copy(wlT[:, :], bank[6][0:D, 0:D]).then_inc(wT_out, 1)
            nc.scalar.copy(blT[:, :], bank[6][0:D, D:2 * D]).then_inc(wT_out, 1)
            quarters_out(1, 2, 4)
            dots(0, 0, 2)
            quarters_out(2, 0, 1)
            dots(0, 2, 5)
            quarters_out(2, 1, 2)
            dots(0, 5, 8)
            quarters_out(2, 2, 4)
            dots(0, 8, POOL_HALVES)
            quarters_out(3, 0, 1)
            spread_out(1)
            dots(1, 0, 1)
            quarters_out(3, 1, 2)
            dots(1, 1, 4)
            quarters_out(3, 2, 4)
            dots(1, 4, 6)
            put_aside(2)
            dots(1, 6, 8)
            rsqrt(1, V["stat2"], V["rsq"])
            dots(1, 8, 9)
            quarters_out(4, 0, 1)
            dots(1, 9, POOL_HALVES)
            quarters_out(4, 1, 2)
            rsqrt(2, V["a1"], V["rsq"])
            quarters_out(4, 2, 4)
            spread_out(2)
            put_aside(3)

            def turn_y(m):
                act.wait_ge(yT_ready, m + 1)
                nc.scalar.copy(yT[:, m % 2, :], bank[6][0:D, 0:P]).then_inc(yT_out, 1)

            def node_logs(k, bl):
                rsqrt(3 + 2 * k, V["stat2"][:, bl], V["rsq"][:, bl])
                rsqrt(4 + 2 * k, V["pn"][:, bl], V["rsq"][:, bl])
                act.wait_ge(artanh_asked, k + 1)
                nc.scalar.activation(V["lnp"][:, bl], V["tcl"][:, bl], ACT.Ln, bias=1.0)
                nc.scalar.activation(V["lnm"][:, bl], V["tcl"][:, bl], ACT.Ln, bias=1.0, scale=-1.0)
                nc.scalar.activation(C["lncmin"], C["cmin"], ACT.Ln).then_inc(artanh_given, 1)

            def operands_out(half):
                for kind in range(4):
                    n = 4 * half + kind
                    act.wait_ge(operand_ready, n + 1)
                    if n == 0:
                        act.wait_ge(turned_stored[0], 16 * (NB // 2))
                    if n == 2:
                        act.wait_ge(top_ready, NB - 1)
                    to = (pair_x, pair_nodes)[kind // 2]
                    rows = (E1, D)[kind // 2]
                    nc.scalar.copy(to[0:rows, kind % 2, half * N // 2:(half + 1) * N // 2],
                                   bank16[(4, 6)[half] + n % 2][0:rows, :]).then_inc(operand_out, 1)

            def exp_logit(n):
                sg = pt("sg", n)
                act.wait_ge(logits_ready, n + 1)
                if n >= 2:
                    act.wait_ge(logw_ready, n - 1)
                nc.scalar.activation(sg, logit_bank, ACT.Abs).then_inc(abs_ready, 1)
                act.wait_ge(abs_ready, n + 1)
                ch.step(nc.scalar.activation(sg, sg, ACT.Exp, scale=-1.0))

            def log_logit(n):
                nc.scalar.activation(pt("sg", n), pt("sg", n), ACT.Ln, bias=1.0).then_inc(siglog_ready, 1)

            def logs(n):
                act.wait_ge(den_ready, n + 1)
                nc.scalar.activation(pt("cd", n), pt("cd", n), ACT.Ln)
                nc.scalar.activation(pt("dn", n), pt("dn", n), ACT.Ln).then_inc(logs_ready, 1)

            def sum_out(c):
                act.wait_ge(sum_done, NB * (c + 1))
                if c == 0:
                    act.wait_ge(turned_stored[1], 16 * (NB // 2))
                nc.scalar.copy(WTs[0:D + 1, c * CW:(c + 1) * CW], bank[7][0:D + 1, :]).then_inc(sum_copied, 1)

            for m in range(4, NB):
                if m == NB - 2:
                    node_logs(0, FIRST)
                if m + 1 < NB:
                    quarters_out(m + 1, 0, 2)
                    for y in ys_of(m):
                        turn_y(y)
                    quarters_out(m + 1, 2, 4)
                else:
                    turn_y(m - 2)
                    operands_out(0)
            turn_y(NB - 2)
            act.wait_ge(top_ready, NB)
            exp_logit(0)
            log_logit(0)
            turn_y(NB - 1)
            logs(0)
            node_logs(1, LAST)
            operands_out(1)

            for n in range(NP):
                act.wait_ge(ratio_ready, n + 1)
                if n >= 1:
                    act.wait_ge(artanh_sub, n)
                nc.scalar.activation(pt("tt", n), pt("lz", n), ACT.Exp, scale=0.5).then_inc(root_ready, 1)
                if n + 1 < NP:
                    logs(n + 1)
                act.wait_ge(clipped_ready, n + 1)
                nc.scalar.activation(pt("cd", n), pt("tt", n), ACT.Ln, bias=1.0)
                nc.scalar.activation(pt("tt", n), pt("tt", n), ACT.Ln, bias=1.0, scale=-1.0).then_inc(artanh_ready, 1)
                if n + 1 < NP:
                    exp_logit(n + 1)
                if n > NBP and n % NBP == 1:
                    sum_out(n // NBP - 1)
                act.wait_ge(logw_ready, n + 1)
                nc.scalar.activation(pt("dn", n), pt("dn", n), ACT.Exp).then_inc(wexp_ready, 1)
                if n + 1 < NP:
                    log_logit(n + 1)
            sum_out(NC - 1)
            rsqrt(7, V["a1"], V["rsq"])
            act.wait_ge(tanh_asked, 1)
            nc.scalar.activation(V["a3"], V["a2"], ACT.Tanh).then_inc(tanh_given, 1)
            nc.scalar.preload_act_table_set("natural_log_exp_and_others")
            rsqrt(8, V["a1"], V["rsq"])
            rsqrt(9, V["stat2"], V["rsq"])

            for q in range(NC):
                act.wait_ge(x3T_ready, q + 1)
                nc.scalar.copy(x3T[0:D, q * CW:(q + 1) * CW], bank[q % 2][0:D, :]).then_inc(x3T_out, 1)
            for q in range(2):
                act.wait_ge(xb_ready, q + 1)
                nc.scalar.copy(xbs[:, HALF[q], 0, :], bank[q][:, :].rearrange("p (b d) -> p b d", b=8)).then_inc(xb_hi, 1)
            for q in range(NC):
                act.wait_ge(h_ready, q + 1)
                nc.scalar.activation(hT[:, q * CW:(q + 1) * CW], bank[2 + q % 2][:, :], ACT.Tanh,
                                     bias=C["hb"]).then_inc(h_out, 1)
            nc.scalar.preload_act_table_set("natural_log_exp_and_others")
            for q in range(2):
                rsqrt(10 + q, V["stat2"][:, HALF[q]], V["rsq"][:, HALF[q]])

        @block.vector
        def _(dve):
            ch = Chain(dve, dve_chain)
            v = nc.vector
            asked = [0]

            def ask_rsqrt():
                ch.settle()
                v.engine_nop().then_inc(rsq_asked, 1)
                asked[0] += 1

            def take_rsqrt(val, to, bl):
                dve.wait_ge(rsq_given, asked[0])
                e, t = V["rsq"][:, bl], V["newt"][:, bl]
                ch.step(v.tensor_tensor(t, e, e, ALU.mult))
                ch.step(v.tensor_tensor(t, t, val[:, bl], ALU.mult))
                ch.step(v.tensor_scalar(t, t, -0.5, 1.5, ALU.mult, ALU.add))
                ch.step(v.tensor_tensor(to[:, bl], e, t, ALU.mult))

            def rsqrt(val, to, bl=ALL):
                ask_rsqrt()
                take_rsqrt(val, to, bl)

            def rows_sum(to, src3):
                ch.step(v.tensor_reduce(to, src3, AX.X, ALU.add))

            def layer_norm(t, dst, bl=ALL):
                t, dst, sq, mean, var = t[:, bl, :], dst[:, bl, :], nat_t[:, bl, :], V["stat"][:, bl], V["stat2"][:, bl]
                rows_sum(mean, t)
                ch.step(v.tensor_scalar(mean, mean, 1.0 / D, None, ALU.mult))
                ch.step(v.tensor_tensor(dst, t, over_d(mean), ALU.subtract))
                ch.step(v.tensor_tensor(sq, dst, dst, ALU.mult))
                rows_sum(var, sq)
                ch.step(v.tensor_scalar(var, var, 1.0 / D, EPS_LN, ALU.mult, ALU.add))
                rsqrt(V["stat2"], V["stat"], bl)
                return v.tensor_tensor(dst, dst, over_d(mean), ALU.mult)

            def diag(k, vec):
                ch.settle()
                for q in range(NC):
                    n = NC * k + q
                    if n >= 2:
                        dve.wait_ge(spread_ready, n - 1)
                    for j in range(BPC):
                        b = BPC * q + j
                        ins = v.tensor_scalar(w_pair[n % 2][:, j * P:(j + 1) * P], identf[:, :], vec[:, b:b + 1], None, ALU.mult)
                    ins.then_inc(diag_ready, 1)

            dve.wait_ge(x_loaded, 16)
            ch.link(v.tensor_copy(x_hl[:, :, 0:D], nat_x[:, :, :]))
            ch.settle()
            ch.link(v.tensor_tensor(x_hl[:, :, D:2 * D], nat_x[:, :, :], x_hl[:, :, 0:D], ALU.subtract))
            ch.link(v.tensor_copy(x_hh[:, :, 0:D], x_hl[:, :, 0:D]))
            ch.link(v.tensor_copy(x_hh[:, :, D:2 * D], x_hl[:, :, 0:D]))
            ch.settle()
            v.engine_nop().then_inc(x_split, 1)
            def factor(b):
                dve.wait_ge(rowsum_ready, b + 1)
                ch.step(v.reciprocal(V["rd"][:, b:b + 1], V["d"][:, b:b + 1]))
                v.tensor_scalar(V["rs"][:, b:b + 1], V["rd"][:, b:b + 1], R_SCALE, None, ALU.mult).then_inc(scale_ready, 1)

            for n in range(6):
                if n == 2:
                    factor(0)
                kind, half = n // 2, n % 2
                to = (xT[:, 0, :], xT[:, 1, :], xT_low)[kind]
                dve.wait_ge(x_turned, n + 1)
                v.tensor_copy(to[:, half * N // 2:(half + 1) * N // 2], bank16[n % 2][0:to.shape[0], :]).then_inc(xT_out, 1)
            dve.wait_ge(x_turned, 6)
            def low(b):
                dve.wait_ge(scale_ready, b + 1)
                dve.wait_ge(hi_ready, b + 1)
                v.scalar_tensor_tensor(Rlo[:, b, :], load[b % NS], V["rs"][:, b:b + 1], Rhi[:, b, :],
                                       ALU.mult, ALU.subtract).then_inc(lo_ready, 1)

            for b in range(NB):
                if b == 3:
                    dve.wait_ge(theta_given, 1)
                    ch.step(v.tensor_scalar(C01, C01, 1.0, None, ALU.add))
                    ch.step(v.reciprocal(C01, C01))
                    ch.link(v.tensor_scalar(C["t1s"], C["e1"], 1.0 / (R_SCALE * R_SCALE), None, ALU.mult))
                    v.tensor_scalar(C["t0s"], C["e0"], 1.0 / R_SCALE, None, ALU.mult).then_inc(theta_ready, 1)
                if b:
                    factor(b)
                if b and b - 1 not in POOL_LOW:
                    low(b - 1)
                if b == 2:
                    for g in range(4):
                        dve.wait_ge(r_turned, g + 1)
                        v.tensor_copy(RT[:, 0, g // 2, g % 2 * 8:g % 2 * 8 + 8, :].rearrange("p k i -> p (k i)"),
                                      bank16[4 + g % 2]).then_inc(turned_copied, 1)
                dve.wait_ge(adj_loaded[b % NS], 16 * (b // NS + 1))
                for c in range(NC):
                    g = NC * b + c
                    dve.wait_ge(gram_ready, g + 1)
                    v.tensor_tensor_reduce(w_pair[2 + g % 4], load[b % NS][:, c * CW:(c + 1) * CW], bank[4 + g % 4][:, :],
                                           1.0, 0.0, ALU.mult, ALU.add, outer4[:, b, c:c + 1]).then_inc(gram_used, 1)
            low(NB - 1)
            rsqrt(V["d"], V["dinv"])
            ch.link(v.tensor_tensor(V["sqd"], V["d"], V["dinv"], ALU.mult))
            dve.wait_ge(gram_used, NC * NB)
            rows_sum(V["outer"], outer4[:, :, :])
            dve.wait_ge(consts_ready, 3)
            dve.wait_ge(pool_lo_ready, len(POOL_LOW))
            diag(0, V["dinv"])

            def fold(m, c):
                vc = stage[:, 1 - m % 2, c * CW:(c + 1) * CW]
                dve.wait_ge(v_ready, m + 1)
                if m in (2, 3):
                    square = aside[m - 2][c]
                    dve.wait_ge(set_aside, NC * (m - 2) + c + 1)
                else:
                    square = bank[c][:, :]
                    dve.wait_ge(square_ready, NC * m + c + 1)
                v.scalar_tensor_tensor(vc, square, C["t1s"], vc, ALU.mult, ALU.add).then_inc(square_folded, 1)

            def scale(m, c):
                vc = stage[:, 1 - m % 2, c * CW:(c + 1) * CW]
                dve.wait_ge(square_folded, NC * m + c + 1)
                ch.link(v.tensor_tensor(vc, vc, vecB[:, c * CW:(c + 1) * CW], ALU.mult))

            def end_layer_one(step):
                mean, var = V["stat"], V["stat2"]
                if step == 0:
                    ch.link(v.tensor_scalar(V["outer"], V["outer"], -0.01, None, ALU.mult))
                    ch.step(v.tensor_scalar(nat_y[:, :, :], nat_x[:, :, :], -0.1, 1.0, ALU.mult, ALU.add))
                    ch.step(v.tensor_tensor(nat_y[:, :, :], nat_y[:, :, :], over_d(V["outer"]), ALU.add))
                elif step == 1:
                    ch.step(v.tensor_tensor(nat_y[:, :, :], nat_y[:, :, :], nat_x[:, :, :], ALU.add))
                    rows_sum(mean, nat_y[:, :, :])
                elif step == 2:
                    ch.step(v.tensor_scalar(mean, mean, 1.0 / D, None, ALU.mult))
                    ch.step(v.tensor_tensor(nat_y[:, :, :], nat_y[:, :, :], over_d(mean), ALU.subtract))
                elif step == 3:
                    sq = work[:, 0:2, :].rearrange("p w n -> p (w n)").rearrange("p (b d) -> p b d", b=NB)
                    ch.step(v.tensor_tensor(sq, nat_y[:, :, :], nat_y[:, :, :], ALU.mult))
                    rows_sum(var, sq)
                else:
                    ch.step(v.tensor_scalar(var, var, 1.0 / D, EPS_LN, ALU.mult, ALU.add))
                    rsqrt(var, mean)
                    v.tensor_tensor(nat_y[:, :, :], nat_y[:, :, :], over_d(mean), ALU.mult).then_inc(x1_ready, 1)

            def times_r(k, to):
                dve.wait_ge(vector_out, NC * (k + 1))
                for b in range(DVE_BLOCKS):
                    for h, part in enumerate((Rhi, Rlo)):
                        ch.step(v.tensor_tensor_reduce(unread, part[:, b, :], vecB, 1.0 / R_SCALE, 0.0,
                                                       ALU.mult, ALU.add, outer4[:, b, h:h + 1]))
                    if k == 0 and b in (3, 5, 8):
                        fold(1, (3, 5, 8).index(b))
                    if k == 1 and 1 <= b <= 5:
                        end_layer_one(b - 1)
                ch.settle()
                dve.wait_ge(dot_ready, POOL_HALVES * (k + 1))
                rows_sum(to, outer4[:, :, 0:2])

            for c in range(NC):
                fold(0, c)
            times_r(0, V["u1"])
            diag(1, V["u1"])
            fold(1, NC - 1)
            times_r(1, V["v2"])
            ch.step(v.tensor_scalar(V["a1"], V["u1"], C["e0"], None, ALU.mult))
            ch.step(v.scalar_tensor_tensor(V["a1"], V["v2"], C["e1"], V["a1"], ALU.mult, ALU.add))
            ch.step(v.tensor_tensor(V["a1"], V["a1"], V["sqd"], ALU.mult))
            ch.step(v.tensor_scalar(V["a1"], V["a1"], 1.0, None, ALU.add))
            rsqrt(V["a1"], V["dinv2"])
            ch.link(v.tensor_tensor(V["cvec"], V["dinv"], V["dinv2"], ALU.mult))
            ch.link(v.tensor_tensor(V["rowfac"], V["sqd"], V["dinv2"], ALU.mult))
            diag(2, V["cvec"])

            def top(m):
                s = m % 2
                for c in range(NC):
                    if m >= 2:
                        fold(m, c)
                    scale(m, c)
                ch.settle()
                ch.step(v.max(vals[:, s, :], stage[:, 1 - s, :]))
                if m >= 2:
                    dve.wait_ge(gathered[s], 16 * TOP * (m // 2))
                v.max_index(idx[:, s, :], vals[:, s, :], stage[:, 1 - s, :]).then_inc(top_ready, 1)

            def top_weights(m):
                s = m % 2
                ch.step(v.tensor_scalar(wts[:, s, :], vals[:, s, 0:TOP], V["rowfac"][:, m:m + 1], None, ALU.mult))

            dve.wait_ge(vector_out, 3 * NC)

            def weighted(m):
                s = m % 2
                dve.wait_ge(gathered[s], 16 * TOP * (m // 2 + 1))
                if m >= 2:
                    dve.wait_ge(yT_ready, m - 1)
                ch.step(v.tensor_scalar(y_sb[:, s, :], gath[:, s, 0, :], wts[:, s, 0:1], None, ALU.mult))
                for t in range(1, TOP):
                    ins = v.scalar_tensor_tensor(y_sb[:, s, :], gath[:, s, t, :], wts[:, s, t:t + 1], y_sb[:, s, :],
                                                 ALU.mult, ALU.add)
                    if t < TOP - 1:
                        ch.step(ins)
                    else:
                        ins.then_inc(y_ready, 1)

            def residual(m):
                dve.wait_ge(yw_ready, m + 1)
                ch.step(v.tensor_tensor(nat_x[:, m, :], bank[7][:, 0:D], b1B[:, :], ALU.add))
                v.tensor_tensor(nat_x[:, m, :], nat_x[:, m, :], nat_y[:, m, :], ALU.add).then_inc(z_ready, 1)

            def curvature():
                ch.step(v.reciprocal(C["rr"], C["r"]))
                ch.link(v.tensor_tensor(C["c"], C["rr"], C["rr"], ALU.mult))
                ch.step(v.tensor_scalar(C["nr"], C["rr"], -1.0, None, ALU.mult))
                ch.step(v.tensor_tensor(C["sqc"], C["rr"], C["nr"], ALU.max))
                ch.link(v.reciprocal(C["rsqc"], C["sqc"]))
                ch.link(v.tensor_scalar(C["c2"], C["c"], 2.0, None, ALU.mult))
                ch.link(v.tensor_scalar(C["nc2"], C["c"], -2.0, None, ALU.mult))
                ch.link(v.tensor_scalar(C["cmin"], C["c"], MIN_NORM, None, ALU.mult))
                ch.settle()
                ch.link(v.tensor_scalar(C["mxn"], C["rsqc"], MAX_NORM, None, ALU.mult))
                ch.link(v.memset(nat_hi[:, :, E0 + 3:E1], 1.0))
                ch.link(v.memset(nat_lo[:, :, E0:E0 + 3], 1.0))
                ch.link(v.memset(work[:, 4:6, :].rearrange("p w n -> p (w n)"), 0.0))
                ch.settle()
                ch.link(v.memset(nat_left[:, :, LROW + 3:LROW + 6], 1.0))
                ch.link(v.memset(nat_right[:, :, LROW:LROW + 3], 1.0))

            def in_parts(a, b, bl):
                part, rest, src = parts[:, :, a:b, bl], sm[:, 4 + a:4 + b, bl], sm[:, a:b, bl]
                ch.step(v.tensor_copy(part[:, 0, :, :], src))
                ch.step(v.tensor_tensor(rest, src, part[:, 0, :, :], ALU.subtract))
                ch.step(v.tensor_copy(part[:, 1, :, :], rest))
                ch.step(v.tensor_tensor(rest, rest, part[:, 1, :, :], ALU.subtract))
                ch.step(v.tensor_copy(part[:, 2, :, :], rest))

            def node_terms(bl):
                B = {n: t[:, bl] for n, t in V.items()}
                xb, tb = x2[:, bl, :], nat_t[:, bl, :]
                ch.step(layer_norm(nat_x, x2, bl))
                ch.link(v.tensor_tensor(tb, xb, xb, ALU.mult))
                ch.step(v.tensor_copy(nat_hi[:, bl, 0:D], xb))
                rows_sum(B["n2"], tb)
                ch.link(v.tensor_scalar(B["pn"], B["n2"], MIN_NORM, None, ALU.max))
                ask_rsqrt()
                ch.link(v.tensor_tensor(nat_lo[:, bl, 0:D], xb, nat_hi[:, bl, 0:D], ALU.subtract))
                ch.link(v.tensor_scalar(B["X"], B["n2"], C["c"], None, ALU.mult))
                ch.step(v.tensor_scalar(B["cf"], B["n2"], -0.5, None, ALU.mult))
                ch.link(v.tensor_scalar(B["om"], B["X"], -1.0, 1.0, ALU.mult, ALU.add))
                ch.link(v.tensor_scalar(xaug[:, bl, D], B["X"], 1.0, None, ALU.add))
                in_parts(0, 1, bl)
                cf_parts = parts[:, :, 0, bl].rearrange("p w b -> p b w")
                ch.link(v.tensor_copy(nat_hi[:, bl, E0:E0 + 3], cf_parts))
                ch.link(v.tensor_copy(nat_lo[:, bl, E0 + 3:E1], cf_parts))
                ch.settle()
                v.engine_nop().then_inc(node_terms_ready, 1)
                take_rsqrt(V["pn"], V["a1"], bl)
                ch.step(v.tensor_tensor(B["a1"], B["a1"], B["pn"], ALU.mult))
                ch.step(v.tensor_scalar(B["a1"], B["a1"], C["sqc"], None, ALU.mult))
                v.tensor_scalar(B["tcl"], B["a1"], T_MAX, None, ALU.min).then_inc(artanh_asked, 1)
                ch.link(v.reciprocal(B["a2"], B["a1"]))
                for k, side in enumerate(["left", "right"]):
                    ch.step(v.tensor_tensor(tb, xb, wattB[:, k, :].unsqueeze(1).to_broadcast([P, bl.stop - bl.start, D]), ALU.mult))
                    rows_sum(B[side], tb)
                dve.wait_ge(artanh_given, 1 + (bl is LAST))
                ch.step(v.tensor_tensor(B["q"], B["lnp"], B["lnm"], ALU.subtract))
                ch.step(v.scalar_tensor_tensor(B["q"], B["q"], 0.5, B["a2"], ALU.mult, ALU.mult))
                ch.link(v.tensor_tensor(B["left"], B["left"], B["q"], ALU.mult))
                ch.step(v.tensor_tensor(B["right"], B["right"], B["q"], ALU.mult))
                ch.step(v.tensor_scalar(B["right"], B["right"], C["batt"], None, ALU.add))
                in_parts(1, 4, bl)
                om = parts[:, :, 1, bl].rearrange("p w b -> p b w")
                nb = bl.stop - bl.start
                for k, (lo, hi) in enumerate([(0, 3), (3, 5), (5, 6)]):
                    ch.link(v.tensor_copy(nat_left[:, bl, lo:hi], om[:, :, k:k + 1].to_broadcast([P, nb, hi - lo])))
                    ch.link(v.tensor_copy(nat_right[:, bl, lo:hi], om[:, :, 0:hi - lo]))
                ch.link(v.tensor_copy(nat_left[:, bl, LROW:LROW + 3], parts[:, :, 2, bl].rearrange("p w b -> p b w")))
                ch.link(v.tensor_copy(nat_right[:, bl, LROW + 3:LROW + 6], parts[:, :, 3, bl].rearrange("p w b -> p b w")))
                ch.settle()
                v.engine_nop().then_inc(node_terms_ready, 1)

            dve.wait_ge(x1_ready, 1)
            dve.wait_ge(small_loaded, 16 * NSMALL)
            for m in range(NB):
                if m >= 6:
                    residual(m - 2)
                elif m == 5:
                    residual(2)
                top(m)
                if m >= 1:
                    weighted(m - 1)
                top_weights(m)
                if 3 <= m <= 5:
                    residual((0, 1, 3)[m - 3])
                if m == NB - 3:
                    curvature()
                    dve.wait_ge(z_ready, m - 1)
                    node_terms(FIRST)
            def distance(n):
                dve.wait_ge(dist_ready, n + 1)
                ch.link(v.tensor_scalar(pt("cd", n), dist_bank, C["nc2"], TINY, ALU.mult, ALU.max))
                return ch.n

            def den(n, distance_done):
                ch.settle(distance_done)
                if n >= 4:
                    dve.wait_ge(sum_done, 2 * (n - 3))
                v.tensor_tensor(pt("dn", n), pt("cd", n), om_bank, ALU.add).then_inc(dist_read, 1)

            def den_guard(n):
                dve.wait_ge(dist_read, n + 1)
                v.tensor_scalar(pt("dn", n), pt("dn", n), MIN_NORM, None, ALU.max).then_inc(den_ready, 1)

            def weights(g):
                t = pt("dn", g // 2)[:, g % 2 * CW:(g % 2 + 1) * CW]
                dve.wait_ge(diff_ready, g // 2 + 1)
                dve.wait_ge(adjacency_ready, g + 1)
                v.tensor_tensor(t, t, bank[6][:, :], ALU.mult).then_inc(weight_done, 1)

            weighted(NB - 1)
            residual(NB - 2)
            dve.wait_ge(top_ready, NB)
            den(0, distance(0))
            den_guard(0)
            residual(NB - 1)
            dve.wait_ge(z_ready, NB)
            node_terms(LAST)

            dve.wait_ge(operand_ready, 8)
            for n in range(NP):
                cd, dn, lz, tt = (pt(k, n) for k in ("cd", "dn", "lz", "tt"))
                if 0 < n < NP - 1:
                    distance_done = distance(n + 1)
                dve.wait_ge(logs_ready, n + 1)
                ch.link(v.tensor_tensor(lz, cd, dn, ALU.subtract))
                log_done = ch.n
                if n == 0:
                    distance_done = distance(1)
                if n >= 2:
                    weights(2 * n - 3)
                if n + 1 < NP:
                    den(n + 1, distance_done)
                ch.settle(log_done)
                v.tensor_scalar(lz, lz, C["lncmin"], None, ALU.max).then_inc(ratio_ready, 1)
                if n + 1 < NP:
                    den_guard(n + 1)
                dve.wait_ge(ratio_ready, n + 1)
                ch.link(v.scalar_tensor_tensor(dn, lz, 0.5, dn, ALU.mult, ALU.add))
                dve.wait_ge(root_ready, n + 1)
                v.tensor_scalar(tt, tt, T_MAX, None, ALU.min).then_inc(clipped_ready, 1)
                ch.settle()
                dve.wait_ge(abs_ready, n + 1)
                v.scalar_tensor_tensor(dn, logit_bank, 0.0, dn, ALU.min, ALU.subtract).then_inc(weight_ready, 1)
                if n >= 1:
                    weights(2 * n - 2)
            for g in range(NT - 3, NT):
                weights(g)

            weighted_nodes = psum[:, 0:NC * CW].rearrange("p (b e) -> p b e", b=NB)
            wv, sv = weighted_nodes[:, :, 0:D], weighted_nodes[:, :, D]
            A, B = nat_x[:, :, :], nat_y[:, :, :]
            ch.step(v.tensor_scalar(V["omc"], V["om"], MIN_NORM, None, ALU.max))
            ch.step(v.tensor_tensor(V["kf"], V["omc"], V["d"], ALU.mult))
            ch.link(v.reciprocal(V["reach"], V["omc"]))
            ch.step(v.tensor_scalar(V["kf"], V["kf"], 0.5 / R_SCALE, None, ALU.mult))
            ch.link(v.tensor_tensor(V["okf"], V["om"], V["kf"], ALU.mult))
            ch.step(v.tensor_scalar(V["reach"], V["reach"], C["sqc"], None, ALU.mult))
            dve.wait_ge(sum_done, NT)
            dve.wait_ge(sums_turned, NC)
            ch.link(v.tensor_tensor(nat_t, x2, wv, ALU.mult))
            ch.link(v.tensor_tensor(B, wv, over_d(V["okf"]), ALU.mult))
            ch.settle()
            rows_sum(V["inner"], nat_t)
            ch.step(v.scalar_tensor_tensor(V["cf"], V["inner"], C["c2"], sv, ALU.mult, ALU.subtract))
            ch.step(v.tensor_tensor(V["cf"], V["cf"], V["kf"], ALU.mult))
            ch.step(v.tensor_tensor(A, x2, over_d(V["cf"]), ALU.mult))
            ch.step(v.tensor_tensor(A, A, B, ALU.add))
            ch.link(v.tensor_tensor(nat_t, A, A, ALU.mult))
            ch.link(v.tensor_tensor(B, A, x2, ALU.mult))
            ch.settle()
            rows_sum(V["uu"], nat_t)
            ch.step(v.tensor_scalar(V["a1"], V["uu"], MIN_NORM, None, ALU.max))
            ask_rsqrt()
            rows_sum(V["ux"], B)
            take_rsqrt(V["a1"], V["a4"], ALL)
            ch.step(v.tensor_tensor(V["a2"], V["a1"], V["a4"], ALU.mult))
            v.tensor_tensor(V["a2"], V["a2"], V["reach"], ALU.mult).then_inc(tanh_asked, 1)
            ch.step(v.tensor_scalar(V["a4"], V["a4"], C["rsqc"], None, ALU.mult))
            dve.wait_ge(tanh_given, 1)
            ch.step(v.tensor_tensor(V["f"], V["a3"], V["a4"], ALU.mult))
            ch.link(v.tensor_tensor(V["a1"], V["uu"], V["f"], ALU.mult))
            ch.step(v.tensor_tensor(V["a2"], V["ux"], V["f"], ALU.mult))
            ch.link(v.scalar_tensor_tensor(V["a3"], V["a1"], C["c"], V["f"], ALU.mult, ALU.mult))
            ch.step(v.tensor_scalar(V["a2"], V["a2"], C["c2"], 1.0, ALU.mult, ALU.add))
            ch.link(v.tensor_tensor(V["a5"], V["X"], V["a3"], ALU.mult))
            ch.step(v.tensor_tensor(V["a4"], V["a2"], V["a3"], ALU.add))
            ch.step(v.tensor_tensor(V["a5"], V["a5"], V["a2"], ALU.add))
            ch.step(v.tensor_scalar(V["a5"], V["a5"], MIN_NORM, None, ALU.max))
            ch.step(v.reciprocal(V["a6"], V["a5"]))
            ch.link(v.tensor_tensor(V["a4"], V["a4"], V["a6"], ALU.mult))
            ch.step(v.tensor_tensor(V["a5"], V["om"], V["a6"], ALU.mult))
            ch.step(v.tensor_tensor(V["a5"], V["a5"], V["f"], ALU.mult))
            ch.link(v.tensor_tensor(B, x2, over_d(V["a4"]), ALU.mult))
            ch.step(v.tensor_tensor(A, A, over_d(V["a5"]), ALU.mult))
            ch.step(v.tensor_tensor(A, A, B, ALU.add))
            ch.step(v.tensor_tensor(nat_t, A, A, ALU.mult))
            rows_sum(V["a1"], nat_t)
            ch.step(v.tensor_scalar(V["a1"], V["a1"], MIN_NORM, None, ALU.max))
            ask_rsqrt()
            ch.step(v.tensor_tensor(C["hb"], C["w1t"], C["tl3"], ALU.mult))
            ch.link(v.tensor_tensor(C["hb"], C["hb"], C["b1c"], ALU.add))
            ch.link(v.tensor_scalar(V["dsc"], V["d"], 1.0 / R_SCALE, None, ALU.mult))
            take_rsqrt(V["a1"], V["a2"], ALL)
            ch.step(v.tensor_scalar(V["a2"], V["a2"], C["mxn"], 1.0, ALU.mult, ALU.min))
            ch.step(v.tensor_tensor(A, A, over_d(V["a2"]), ALU.mult))
            ch.step(v.tensor_tensor(A, A, x2, ALU.add))
            layer_norm(A, nat_y).then_inc(x3_ready, 1)

            for q in range(2):
                dve.wait_ge(xb_hi, q + 1)
                ch.step(v.tensor_copy(nat_x[:, HALF[q], :], bank[q][:, :].rearrange("p (b d) -> p b d", b=8)))
                v.tensor_tensor(xbs[:, HALF[q], 1, :], nat_x[:, HALF[q], :], xbs[:, HALF[q], 0, :], ALU.subtract).then_inc(xb_split, 1)
            dve.wait_ge(x3_ready, 1)
            ch.step(v.tensor_tensor(nat_t, nat_x[:, :, :], over_d(V["d"]), ALU.mult))
            ch.step(v.tensor_tensor(nat_t, nat_y[:, :, :], nat_t, ALU.subtract))
            ch.step(v.tensor_tensor(nat_t, nat_t, b2B[:, :].unsqueeze(1).to_broadcast([P, NB, D]), ALU.add))
            for q in range(2):
                dve.wait_ge(mlp_ready, q + 1)
                ch.link(v.tensor_tensor(base[:, HALF[q], :], bank[2 + q][:, :].rearrange("p (b d) -> p b d", b=8),
                                        nat_t[:, HALF[q], :], ALU.add))
            ch.settle()

            def add_product(i):
                dve.wait_ge(product_done, i + 1)
                o, row = bank[4 + i % 4], base[:, i, :]
                ch.step(v.scalar_tensor_tensor(row, o[:, D:2 * D], V["dsc"][:, i:i + 1], row, ALU.mult, ALU.add))
                v.scalar_tensor_tensor(row, o[:, 0:D], V["dsc"][:, i:i + 1], row, ALU.mult, ALU.add).then_inc(product_added, 1)

            for q in range(2):
                for i in range(NB // 2 * q, NB // 2 * (q + 1)):
                    add_product(i)
                dve.wait_ge(product_added, NB // 2 * (q + 1))
                layer_norm(base, nat_y, HALF[q]).then_inc(out_ready, 1)

        @block.tensor
        def _(pe):
            mm = nc.tensor.matmul

            def spread(k):
                for n in range(NC * k, NC * k + NC):
                    pe.wait_ge(diag_ready, n + 1)
                    if n >= 2:
                        pe.wait_ge(vector_out, n - 1)
                    mm(bank[6 + n % 2][:, :], ones[:, :], w_pair[n % 2], start=True, stop=True).then_inc(spread_ready, 1)

            def turn_quarter(g):
                part, half = (Rhi, Rlo)[(g % 4) // 2], g % 2
                if g >= 2:
                    pe.wait_ge(turned_copied, g - 1)
                for k in range(8):
                    ins = nc.tensor.transpose(bank16[4 + g % 2][:, k * P:(k + 1) * P],
                                              part[:, g // 4, (8 * half + k) * P:(8 * half + k + 1) * P], ident[:, :])
                ins.then_inc(r_turned, 1)

            def square(m, c):
                if c == 0:
                    pe.wait_ge(turned_copied, 4 * (m + 1))
                if m in (3, 4):
                    pe.wait_ge(set_aside, NC * (m - 3) + c + 1)
                else:
                    pe.wait_ge(square_folded, NC * (m - 1) + c + 1)
                cs = slice(c * CW, (c + 1) * CW)
                for k in range(NB):
                    hi, lo = RT[:, m % 2, 0, k, :], RT[:, m % 2, 1, k, :]
                    mm(bank[c][:, :], hi, Rhi[:, k, cs], start=(k == 0), stop=False)
                    mm(bank[c][:, :], hi, Rlo[:, k, cs], start=False, stop=False)
                    ins = mm(bank[c][:, :], lo, Rhi[:, k, cs], start=False, stop=(k == NB - 1))
                ins.then_inc(square_ready, 1)

            def turn_y(m):
                pe.wait_ge(y_ready, m + 1)
                if m >= 1:
                    pe.wait_ge(yT_out, m)
                nc.tensor.transpose(bank[6][0:D, 0:P], y_sb[:, m % 2, :], identf[:, :]).then_inc(yT_ready, 1)

            def y_w(m):
                pe.wait_ge(yT_out, m + 1)
                if m >= 1:
                    pe.wait_ge(z_ready, m)
                mm(bank[7][:, 0:D], yT[:, m % 2, :], wlT[:, :], start=True, stop=True).then_inc(yw_ready, 1)

            pe.wait_ge(consts_ready, 3)
            pe.wait_ge(x_loaded, 16)
            pe.wait_ge(x_split, 1)
            for n in range(6):
                kind, half = n // 2, n % 2
                src = (x_hl[:, :, :], x_hh[:, :, :], x_hl[:, :, D:2 * D])[kind]
                if n >= 2:
                    pe.wait_ge(xT_out, n - 1)
                for k in range(8):
                    ins = nc.tensor.transpose(bank16[n % 2][0:src.shape[2], k * P:(k + 1) * P], src[:, 8 * half + k, :],
                                              ident[:, :])
                ins.then_inc(x_turned, 1)
            pe.wait_ge(xT_out, 6)

            def square_step(m, k, chunks):
                pe.wait_ge(turned_copied, 4 * (m + 1))
                for c in chunks:
                    if k == 0 and m:
                        pe.wait_ge(square_folded, NC * (m - 1) + c + 1)
                    hi, lo = RT[:, m % 2, 0, k, :], RT[:, m % 2, 1, k, :]
                    cs = slice(c * CW, (c + 1) * CW)
                    mm(bank[c][:, :], hi, Rhi[:, k, cs], start=(k == 0), stop=False)
                    mm(bank[c][:, :], hi, Rlo[:, k, cs], start=False, stop=False)
                    ins = mm(bank[c][:, :], lo, Rhi[:, k, cs], start=False, stop=(k == NB - 1))
                    if k == NB - 1:
                        ins.then_inc(square_ready, 1)

            SQUARE_LAG = 2
            for g in range(NC * NB):
                b, c = g // NC, g % NC
                if g >= 4:
                    pe.wait_ge(gram_used, g - 3)
                if g == 2 * NC:
                    pe.wait_ge(gram_used, 2 * NC)
                    low_done(pe, 0)
                    for quarter in range(4):
                        turn_quarter(quarter)
                    pe.wait_ge(turned_copied, 4)
                bs, cs = slice(b * P, (b + 1) * P), slice(c * CW, (c + 1) * CW)
                mm(bank[4 + g % 4][:, :], xT[:, 0, bs], xT[:, 1, cs], start=True, stop=False)
                mm(bank[4 + g % 4][:, :], xT[0:D, 0, bs], xT_low[:, cs], start=False, stop=True).then_inc(gram_ready, 1)
                if c == NC - 1 and b >= SQUARE_LAG:
                    low_done(pe, b - SQUARE_LAG)
                    square_step(0, b - SQUARE_LAG, range(NC))
            pe.wait_ge(gram_used, NC * NB)
            turn_quarter(4)
            turn_quarter(5)
            for k in range(NB - SQUARE_LAG, NB):
                low_done(pe, k)
                square_step(0, k, range(NC))
            spread(0)
            pe.wait_ge(small_loaded, 16 * NSMALL)
            pe.wait_ge(vector_out, NC)
            nc.tensor.transpose(bank[6][0:D, 0:D], wl_nat[:, :], identf[0:D, 0:D])
            nc.tensor.transpose(bank[6][0:D, D:2 * D], bl_nat[:, :], identf[0:D, 0:D]).then_inc(wT_ready, 1)
            turn_quarter(6)
            turn_quarter(7)
            pe.wait_ge(wT_out, 2)

            def turn_operand(n):
                half, kind = n // 4, n % 4
                if n >= 2:
                    pe.wait_ge(operand_out, n - 1)
                src = (nat_hi, nat_lo, nat_left_bits, nat_right_bits)[kind]
                rows = (E1, D)[kind // 2]
                to = bank16[(4, 6)[half] + n % 2]
                for k in range(8):
                    ins = nc.tensor.transpose(to[0:rows, k * P:(k + 1) * P], src[:, 8 * half + k, 0:rows], ident[:, :])
                ins.then_inc(operand_ready, 1)

            xh, xl = pair_x[:, 0, :], pair_x[:, 1, :]
            node_l, node_r = pair_nodes[:, 0, :].bitcast(BF16), pair_nodes[:, 1, :].bitcast(BF16)

            def tiles_of(n):
                c = n // NBP
                for h in range(2):
                    j = 2 * (n % NBP) + h
                    yield slice(j * P, (j + 1) * P), slice(c * CW, (c + 1) * CW), slice(h * CW, (h + 1) * CW)

            def pair_distance(n):
                if n >= 1:
                    pe.wait_ge(dist_read, n)
                for js, cs, o in tiles_of(n):
                    mm(dist_bank[:, o], xh[0:D, js], xh[0:D, cs], start=True, stop=False)
                    mm(dist_bank[:, o], xl[0:D, js], xh[0:D, cs], start=False, stop=False)
                    mm(dist_bank[:, o], xh[0:E1, js], xl[0:E1, cs], start=False, stop=True)
                    ins = mm(om_bank[:, o], node_l[0:6, js], node_r[0:6, cs], start=True, stop=True)
                ins.then_inc(dist_ready, 1)

            def pair_logit(n):
                if n >= 1:
                    pe.wait_ge(weight_ready, n)
                ls = slice(LROW, LROW + 6)
                for js, cs, o in tiles_of(n):
                    ins = mm(logit_bank[:, o], node_l[ls, js], node_r[ls, cs], start=True, stop=True)
                ins.then_inc(logits_ready, 1)

            for m in range(1, NB):
                ys = ys_of(m) if m >= 4 else []
                square(m, 0)
                if m + 1 < NB:
                    turn_quarter(4 * m + 4)
                if m == 2:
                    spread(1)
                square(m, 1)
                if m + 1 < NB:
                    turn_quarter(4 * m + 5)
                if ys:
                    turn_y(ys[0])
                if m == NB - 1:
                    pe.wait_ge(node_terms_ready, 2)
                    turn_operand(0)
                    turn_operand(1)
                square(m, 2)
                if ys:
                    y_w(ys[0])
                for y in ys[1:]:
                    turn_y(y)
                if m + 1 < NB:
                    turn_quarter(4 * m + 6)
                    turn_quarter(4 * m + 7)
                else:
                    turn_operand(2)
                    turn_operand(3)
                if m == 3:
                    spread(2)
                square(m, 3)
                for y in ys[1:]:
                    y_w(y)
            turn_y(NB - 2)
            y_w(NB - 2)
            pe.wait_ge(square_folded, NC * NB)
            pe.wait_ge(operand_out, 4)
            pair_logit(0)
            pair_distance(0)
            turn_y(NB - 1)
            y_w(NB - 1)
            pair_distance(1)

            pe.wait_ge(yT_out, NB)
            pe.wait_ge(z_ready, NB)
            pe.wait_ge(node_terms_ready, 3)
            turn_operand(4)
            turn_operand(5)
            pe.wait_ge(node_terms_ready, 4)
            turn_operand(6)
            turn_operand(7)
            pe.wait_ge(operand_out, 8)
            def adjacency(g):
                c, j = g // NB, g % NB
                if g >= 1:
                    pe.wait_ge(weight_done, g)
                for k in range(BPC):
                    i = BPC * c + k
                    o = bank[6][:, k * P:(k + 1) * P]
                    mm(o, Rhi[:, i, j * P:(j + 1) * P], ident[:, :], start=True, stop=False)
                    ins = mm(o, Rlo[:, i, j * P:(j + 1) * P], ident[:, :], start=False, stop=True)
                ins.then_inc(adjacency_ready, 1)

            def weighted_sum(g):
                c, j = g // NB, g % NB
                pe.wait_ge(weight_done, g + 1)
                if j == 0 and c:
                    pe.wait_ge(sum_copied, c)
                mm(bank[7][0:D + 1, :], xaug[:, j, :], pt("dn", g // 2)[:, g % 2 * CW:(g % 2 + 1) * CW],
                   start=(j == 0), stop=(j == NB - 1)).then_inc(sum_done, 1)

            for n in range(NP):
                if n >= 1:
                    adjacency(2 * n - 2)
                if n >= 2:
                    weighted_sum(2 * n - 3)
                if n + 2 < NP:
                    pair_distance(n + 2)
                if n + 1 < NP:
                    pair_logit(n + 1)
                if n >= 1:
                    adjacency(2 * n - 1)
                    weighted_sum(2 * n - 2)
            adjacency(NT - 2)
            weighted_sum(NT - 3)
            adjacency(NT - 1)
            weighted_sum(NT - 2)
            weighted_sum(NT - 1)
            pe.wait_ge(sum_copied, NC)
            for q in range(NC):
                for j in range(BPC):
                    b = BPC * q + j
                    ins = nc.tensor.transpose(bank[q][:, j * P:j * P + D + 1], WTs[0:D + 1, b * P:(b + 1) * P],
                                              identf[0:D + 1, 0:D + 1])
                ins.then_inc(sums_turned, 1)

            pe.wait_ge(x3_ready, 1)
            for q in range(NC):
                if q >= 2:
                    pe.wait_ge(x3T_out, q - 1)
                for j in range(BPC):
                    ins = nc.tensor.transpose(bank[q % 2][0:D, j * P:(j + 1) * P], nat_y[:, BPC * q + j, :], identf[:, :])
                ins.then_inc(x3T_ready, 1)
            pe.wait_ge(x3T_out, NC)
            for q in range(2):
                for b in range(8):
                    i = 8 * q + b
                    ins = mm(bank[q][:, b * D:(b + 1) * D], x3T[0:D, i * P:(i + 1) * P], blT[:, :], start=True, stop=True)
                ins.then_inc(xb_ready, 1)
            for q in range(NC):
                if q >= 2:
                    pe.wait_ge(h_out, q - 1)
                mm(bank[2 + q % 2][:, :], w1_sb[:, :], x3T[0:D, q * CW:(q + 1) * CW], start=True, stop=True).then_inc(h_ready, 1)
            pe.wait_ge(xb_split, 2)

            def product(i):
                pe.wait_ge(turned_loaded[i // BPC], 32 * BPC)
                if i >= 4:
                    pe.wait_ge(product_added, i - 3)
                o = bank[4 + i % 4]
                for k in range(NB):
                    ks = slice(k * P, (k + 1) * P)
                    mm(o[:, 0:2 * D], Rhi[:, i, ks], xbs[:, k, :, :].rearrange("p h d -> p (h d)"),
                       start=(k == 0), stop=False, skip_group_check=True)
                    ins = mm(o[:, 0:D], Rlo[:, i, ks], xbs[:, k, 0, :], start=False, stop=(k == NB - 1),
                             skip_group_check=True)
                ins.then_inc(product_done, 1)

            for i in range(4):
                product(i)
            pe.wait_ge(h_out, NC)
            for q in range(2):
                for b in range(8):
                    i = 8 * q + b
                    ins = mm(bank[2 + q][:, b * D:(b + 1) * D], hT[:, i * P:(i + 1) * P], w2_sb[:, :], start=True, stop=True)
                ins.then_inc(mlp_ready, 1)
            for i in range(4, NB):
                product(i)


_INS = ["x", "adj", "L1_gnn_theta", "L1_gnn_W", "L1_gnn_b", "L2_gnn_r", "L2_gnn_w_att", "L2_gnn_b_att",
        "L3_gnn_t", "L3_gnn_B", "L3_gnn_W1", "L3_gnn_b1", "L3_gnn_W2", "L3_gnn_b2"]


def kernel(**inputs):
    import numpy as _np
    import concourse.bacc as _bacc
    from concourse import mybir as _mybir
    from concourse.bass_utils import run_bass_kernel_spmd as _run

    nc = _bacc.Bacc("TRN2", target_bir_lowering=False, num_devices=1)
    arrays, args = {}, []
    for name in _INS:
        a = _np.ascontiguousarray(inputs[name])
        arrays[f"in_{name}_dram"] = a
        args.append(nc.dram_tensor(f"in_{name}_dram", a.shape, _mybir.dt.from_np(a.dtype), kind="ExternalInput").ap())
    out = nc.dram_tensor("out_dram", (2048, 64), _mybir.dt.float32, kind="ExternalOutput").ap()
    build(nc, *args, out)
    res = _run(nc, [arrays], core_ids=[0])
    return res.results[0]["out_dram"]
```
